# Optimizing a Trainium2 kernel written in Bass

```python
import numpy as np
import jax
import jax.numpy as jnp

def _softmax(x, axis=-1):
    return jax.nn.softmax(x, axis=axis)

def _gelu(x):
    return jax.nn.gelu(x, approximate=True)

def _silu(x):
    return jax.nn.silu(x)

def _sigmoid(x):
    return jax.nn.sigmoid(x)

def _layernorm(x, axis=-1, eps=1e-05):
    m = jnp.mean(x, axis=axis, keepdims=True)
    v = jnp.var(x, axis=axis, keepdims=True)
    return (x - m) / jnp.sqrt(v + eps)

def _scatter_add(tgt, idx, src, axis=0):
    return tgt.at[idx].add(src)

def _segment_sum(src, seg, n):
    return jax.ops.segment_sum(src, seg, n)
kernel_name = 'mk_flamingo_gated_d2_seqx_r8_cba63e'

def setup_inputs(seed: int=0):
    np.random.seed(seed)
    _w = jnp.asarray

    def _rec_inputs():
        import jax
        import jax.numpy as jnp
        _rk = jax.random.key(seed)
        x = 7.22e-05 + 1 * jax.random.normal(jax.random.fold_in(_rk, 1), (32, 64, 256), jnp.float32)
        _lenS = 64 - jax.random.randint(jax.random.fold_in(_rk, 7), (32,), 0, max(1, 64 // 4) + 1, jnp.int32)
        _lenS2 = 64 - jax.random.randint(jax.random.fold_in(_rk, 8), (32,), 0, max(1, 64 // 4) + 1, jnp.int32)
        _ctx_2048P = jax.random.normal(jax.random.fold_in(_rk, 11), (32, 16, 256), jnp.float32)
        _ctx_2048c = jax.random.dirichlet(jax.random.fold_in(_rk, 511), 0.3 * jnp.ones((16,), jnp.float32), (32, 64))
        _ctx_2048t = jnp.einsum('bsk,bkd->bsd', _ctx_2048c, _ctx_2048P)
        _ctx_2048t = _ctx_2048t * jax.lax.rsqrt(jnp.mean(jnp.square(_ctx_2048t)) + 1e-12) * 0.953939
        ctx_2048 = 4.13588e-05 + 0.999923 * (_ctx_2048t + 0.3 * jax.random.normal(jax.random.fold_in(_rk, 611), (32, 64, 256), jnp.float32))
        _validS = jnp.arange(64)[None, :] < _lenS[:, None]
        _validS2 = jnp.arange(64)[None, :] < _lenS2[:, None]
        _causal = jnp.tril(jnp.ones((64, 64), dtype=bool))
        mask_BxS2_bk0 = jnp.logical_not(jnp.broadcast_to(_validS2[:, :], (32, 64)))
        _g = jax.random.normal(jax.random.fold_in(_rk, 9001), (2, 2), jnp.float32)
        _g = jnp.sign(_g) * jnp.maximum(jnp.abs(_g), 1.0) + (_g == 0) * 1.0
        g_xattn = _g[0]
        g_ffn = _g[1]
        return (x, ctx_2048, mask_BxS2_bk0, g_xattn, g_ffn)
    x, ctx_2048, mask_BxS2_bk0, g_xattn, g_ffn = _rec_inputs()

    def _L0_xattn_setup():
        import jax, jax.numpy as jnp
        import numpy as np
        B, S, DIM, HD = (4, 128, 256, 128)
        H = DIM // HD
        GN_EPS = 0.001

        def _decay_masks(n_heads, seq_len):
            gam = 1.0 - 2.0 ** (-5.0 - jnp.arange(n_heads, dtype=jnp.float32))
            idx = jnp.arange(seq_len, dtype=jnp.float32)
            expo = idx[None, :] - idx[:, None]
            D = jnp.where(expo[None, :, :] <= 0, gam[:, None, None] ** expo[None, :, :], 0.0)
            return D / jnp.sqrt(D.sum(axis=-1))[:, None, :]
        key = jax.random.key(seed)
        ks = jax.random.split(key, 8)
        x = jax.random.normal(ks[0], (B, S, DIM), dtype=jnp.float32)
        k = jax.random.normal(ks[1], (B, S, DIM), dtype=jnp.float32)
        v = jax.random.normal(ks[2], (B, S, DIM), dtype=jnp.float32)
        Wh = jax.random.normal(ks[3], (H, HD, HD), dtype=jnp.float32) / np.sqrt(HD)
        wg_w = jax.random.normal(ks[4], (DIM, DIM), dtype=jnp.float32) / np.sqrt(DIM)
        wo_w = jax.random.normal(ks[5], (DIM, DIM), dtype=jnp.float32) / np.sqrt(DIM)
        gn_gamma = jnp.ones((DIM,), dtype=jnp.float32)
        gn_beta = jnp.zeros((DIM,), dtype=jnp.float32)
        return {'x': x, 'k': k, 'v': v, 'Wh': Wh, 'wg_w': wg_w, 'wo_w': wo_w, 'gn_gamma': gn_gamma, 'gn_beta': gn_beta}
    _L0_xattn_all = _L0_xattn_setup()
    _L0_xattn_in = {k: v for k, v in _L0_xattn_all.items() if k in ('Wh', 'wg_w', 'wo_w', 'gn_gamma', 'gn_beta')}
    del _L0_xattn_all

    def _L0_ffn_setup():
        import jax, jax.numpy as jnp
        import numpy as np
        E = 32
        G = 8
        TKG = 4
        K = 4
        D = 256
        H = 128
        HS = 512
        SCALE = 2.5
        CAP = 128

        def relu2(x):
            r = jnp.maximum(x, 0.0)
            return r * r

        def route_tokens(scores, bias_corr):
            T = scores.shape[0]
            scores_c = scores + bias_corr
            group_scores = jax.lax.top_k(scores_c.reshape(T, G, E // G), 2)[0].sum(-1)
            _, group_idx = jax.lax.top_k(group_scores, TKG)
            group_mask = jnp.zeros((T, G), scores.dtype).at[jnp.arange(T)[:, None], group_idx].set(1.0)
            score_mask = jnp.repeat(group_mask, E // G, axis=1)
            masked = jnp.where(score_mask > 0, scores_c, 0.0)
            _, topk_idx = jax.lax.top_k(masked, K)
            topk_w = jnp.take_along_axis(scores, topk_idx, axis=1)
            topk_w = topk_w / (topk_w.sum(-1, keepdims=True) + 1e-20)
            return (topk_idx, topk_w * SCALE)
        key = jax.random.key(seed)
        ks = jax.random.split(key, 6)
        B, S = (2, 256)
        return dict(hidden_states=jax.random.normal(ks[0], (B, S, D), jnp.float32), gate_w=jax.random.normal(ks[1], (E, D), jnp.float32) * 0.02, bias_corr=jnp.zeros((E,), jnp.float32), up_w=jax.random.normal(ks[2], (E, H, D), jnp.float32) * 0.02, down_w=jax.random.normal(ks[3], (E, D, H), jnp.float32) * 0.02, shared_up_w=jax.random.normal(ks[4], (HS, D), jnp.float32) * 0.02, shared_down_w=jax.random.normal(ks[5], (D, HS), jnp.float32) * 0.02)
    _L0_ffn_all = _L0_ffn_setup()
    _L0_ffn_in = {k: v for k, v in _L0_ffn_all.items() if k in ('gate_w', 'bias_corr', 'up_w', 'down_w', 'shared_up_w', 'shared_down_w')}
    del _L0_ffn_all

    def _L1_xattn_setup():
        import jax, jax.numpy as jnp
        import numpy as np
        key = jax.random.key(seed)
        k1, k2, k3 = jax.random.split(key, 3)
        B, S, D, M = (8, 256, 256, 128)
        hidden_states = jax.random.normal(k1, (B, S, D), dtype=jnp.float32)
        memory_tokens = jax.random.normal(k2, (B, M, D), dtype=jnp.float32)
        memory_mask = jax.random.randint(k3, (B, M), 0, 2).astype(jnp.bool_)
        return {'hidden_states': hidden_states, 'memory_tokens': memory_tokens, 'memory_mask': memory_mask}
    _L1_xattn_all = _L1_xattn_setup()
    _L1_xattn_in = {k: v for k, v in _L1_xattn_all.items() if k in ()}
    del _L1_xattn_all

    def _L1_ffn_setup():
        import jax, jax.numpy as jnp
        import numpy as np
        EPS = 1e-05
        RMS_EPS = 1e-06

        def activation_quant(x, num_bits=8):
            qn = -2 ** (num_bits - 1)
            qp = 2 ** (num_bits - 1) - 1
            xf = x.astype(jnp.float32)
            s = qp / jnp.clip(jnp.max(jnp.abs(xf), axis=-1, keepdims=True), EPS, None)
            return (jnp.clip(jnp.round(xf * s), qn, qp) / s).astype(x.dtype)

        def weight_quant(w):
            wf = w.astype(jnp.float32)
            s = 1.0 / jnp.clip(jnp.mean(jnp.abs(wf)), EPS, None)
            return (jnp.clip(jnp.round(wf * s), -1.0, 1.0) / s).astype(w.dtype)

        def bit_linear(x, w):
            qx = x + jax.lax.stop_gradient(activation_quant(x) - x)
            qw = w + jax.lax.stop_gradient(weight_quant(w) - w)
            return jnp.einsum('bsh,oh->bso', qx, qw)

        def rms_norm(x, weight, eps=RMS_EPS):
            xf = x.astype(jnp.float32)
            var = jnp.mean(xf * xf, axis=-1, keepdims=True)
            return weight * (xf * jax.lax.rsqrt(var + eps)).astype(x.dtype)
        key = jax.random.key(seed)
        k1, k2, k3, k4 = jax.random.split(key, 4)
        B, S, H, I = (2, 256, 256, 1024)
        scale = 1.0 / np.sqrt(H)
        return {'x': jax.random.normal(k1, (B, S, H), dtype=jnp.float32), 'w_gate': jax.random.normal(k2, (I, H), dtype=jnp.float32) * scale, 'w_up': jax.random.normal(k3, (I, H), dtype=jnp.float32) * scale, 'w_down': jax.random.normal(k4, (H, I), dtype=jnp.float32) * (1.0 / np.sqrt(I)), 'ln_weight': jnp.ones((I,), dtype=jnp.float32)}
    _L1_ffn_all = _L1_ffn_setup()
    _L1_ffn_in = {k: v for k, v in _L1_ffn_all.items() if k in ('w_gate', 'w_up', 'w_down', 'ln_weight')}
    del _L1_ffn_all
    return {'x': x, 'ctx_2048': ctx_2048, 'mask_BxS2_bk0': mask_BxS2_bk0, 'g_xattn': g_xattn, 'g_ffn': g_ffn, 'L0_xattn_Wh': _L0_xattn_in['Wh'], 'L0_xattn_wg_w': _L0_xattn_in['wg_w'], 'L0_xattn_wo_w': _L0_xattn_in['wo_w'], 'L0_xattn_gn_gamma': _L0_xattn_in['gn_gamma'], 'L0_xattn_gn_beta': _L0_xattn_in['gn_beta'], 'L0_ffn_gate_w': _L0_ffn_in['gate_w'], 'L0_ffn_bias_corr': _L0_ffn_in['bias_corr'], 'L0_ffn_up_w': _L0_ffn_in['up_w'], 'L0_ffn_down_w': _L0_ffn_in['down_w'], 'L0_ffn_shared_up_w': _L0_ffn_in['shared_up_w'], 'L0_ffn_shared_down_w': _L0_ffn_in['shared_down_w'], 'L1_ffn_w_gate': _L1_ffn_in['w_gate'], 'L1_ffn_w_up': _L1_ffn_in['w_up'], 'L1_ffn_w_down': _L1_ffn_in['w_down'], 'L1_ffn_ln_weight': _L1_ffn_in['ln_weight']}

def reference(x, ctx_2048, mask_BxS2_bk0, g_xattn, g_ffn, L0_xattn_Wh, L0_xattn_wg_w, L0_xattn_wo_w, L0_xattn_gn_gamma, L0_xattn_gn_beta, L0_ffn_gate_w, L0_ffn_bias_corr, L0_ffn_up_w, L0_ffn_down_w, L0_ffn_shared_up_w, L0_ffn_shared_down_w, L1_ffn_w_gate, L1_ffn_w_up, L1_ffn_w_down, L1_ffn_ln_weight):
    import jax
    import jax.numpy as jnp

    def _L0_xattn_ref(x, k, v, Wh, wg_w, wo_w, gn_gamma, gn_beta):
        import jax, jax.numpy as jnp
        import numpy as np
        B, S, DIM, HD = (4, 128, 256, 128)
        H = DIM // HD
        GN_EPS = 0.001

        def _decay_masks(n_heads, seq_len):
            gam = 1.0 - 2.0 ** (-5.0 - jnp.arange(n_heads, dtype=jnp.float32))
            idx = jnp.arange(seq_len, dtype=jnp.float32)
            expo = idx[None, :] - idx[:, None]
            D = jnp.where(expo[None, :, :] <= 0, gam[:, None, None] ** expo[None, :, :], 0.0)
            return D / jnp.sqrt(D.sum(axis=-1))[:, None, :]
        b, s, dim = x.shape
        h, hd, _ = Wh.shape
        xh = x.reshape(b, s, h, hd)
        kh = k.reshape(b, s, h, hd)
        vh = v.reshape(b, s, h, hd)
        Q = jnp.einsum('bshd,hde->bshe', xh, Wh)
        K = jnp.einsum('bshd,hde->bshe', kh, Wh)
        V = jnp.einsum('bshd,hde->bshe', vh, Wh)
        scores = jnp.einsum('bshe,bthe->bhst', Q, K) / jnp.sqrt(jnp.float32(hd))
        Dn = _decay_masks(h, s)
        masked = scores * Dn[None, :, :, :]
        A = jnp.maximum(jnp.abs(masked.sum(axis=0)), 1.0)
        O = jnp.einsum('hst,bthe->bshe', A, V).reshape(b, s, dim)
        mu = O.mean(axis=-1, keepdims=True)
        var = O.var(axis=-1, keepdims=True)
        Y = (O - mu) / jnp.sqrt(var + GN_EPS) * gn_gamma + gn_beta
        W = jax.nn.relu(x @ wg_w)
        return W * Y @ wo_w

    def _L0_ffn_ref(hidden_states, gate_w, bias_corr, up_w, down_w, shared_up_w, shared_down_w):
        import jax, jax.numpy as jnp
        import numpy as np
        E = 32
        G = 8
        TKG = 4
        K = 4
        D = 256
        H = 128
        HS = 512
        SCALE = 2.5
        CAP = 128

        def relu2(x):
            r = jnp.maximum(x, 0.0)
            return r * r

        def route_tokens(scores, bias_corr):
            T = scores.shape[0]
            scores_c = scores + bias_corr
            group_scores = jax.lax.top_k(scores_c.reshape(T, G, E // G), 2)[0].sum(-1)
            _, group_idx = jax.lax.top_k(group_scores, TKG)
            group_mask = jnp.zeros((T, G), scores.dtype).at[jnp.arange(T)[:, None], group_idx].set(1.0)
            score_mask = jnp.repeat(group_mask, E // G, axis=1)
            masked = jnp.where(score_mask > 0, scores_c, 0.0)
            _, topk_idx = jax.lax.top_k(masked, K)
            topk_w = jnp.take_along_axis(scores, topk_idx, axis=1)
            topk_w = topk_w / (topk_w.sum(-1, keepdims=True) + 1e-20)
            return (topk_idx, topk_w * SCALE)
        B, S, _ = hidden_states.shape
        T = B * S
        flat = hidden_states.reshape(T, D)
        logits = flat @ gate_w.T
        scores = jax.nn.sigmoid(logits)
        topk_idx, topk_w = route_tokens(scores, bias_corr)
        e_flat = topk_idx.reshape(-1)
        oh = jax.nn.one_hot(e_flat, E, dtype=jnp.int32)
        pos = jnp.take_along_axis(jnp.cumsum(oh, axis=0) - 1, e_flat[:, None], axis=1)[:, 0]
        tok = jnp.repeat(jnp.arange(T), K)
        valid = pos < CAP
        xe = jnp.zeros((E, CAP, D), flat.dtype).at[e_flat, pos].set(flat[tok], mode='drop')
        h = relu2(jnp.einsum('ecd,ehd->ech', xe, up_w))
        ye = jnp.einsum('ech,edh->ecd', h, down_w)
        gathered = ye[e_flat, jnp.minimum(pos, CAP - 1)]
        gathered = jnp.where(valid[:, None], gathered, 0.0) * topk_w.reshape(-1)[:, None]
        routed = gathered.reshape(T, K, D).sum(axis=1).reshape(B, S, D)
        shared = relu2(hidden_states @ shared_up_w.T) @ shared_down_w.T
        return routed + shared

    def _L1_xattn_ref(hidden_states, memory_tokens, memory_mask):
        import jax, jax.numpy as jnp
        import numpy as np
        B, S, D = hidden_states.shape
        scale = 1.0 / jnp.sqrt(jnp.asarray(D, hidden_states.dtype))
        scores = jnp.einsum('bsd,bmd->bsm', hidden_states, memory_tokens) * scale
        neg_inf = jnp.asarray(-1e+30, scores.dtype)
        scores = jnp.where(memory_mask[:, None, :], scores, neg_inf)
        attn = jax.nn.softmax(scores, axis=-1)
        readout = jnp.einsum('bsm,bmd->bsd', attn, memory_tokens)
        valid_b = jnp.any(memory_mask, axis=-1)
        out = jnp.where(valid_b[:, None, None], readout, jnp.zeros_like(readout))
        return out

    def _L1_ffn_ref(x, w_gate, w_up, w_down, ln_weight):
        import jax, jax.numpy as jnp
        import numpy as np
        EPS = 1e-05
        RMS_EPS = 1e-06

        def activation_quant(x, num_bits=8):
            qn = -2 ** (num_bits - 1)
            qp = 2 ** (num_bits - 1) - 1
            xf = x.astype(jnp.float32)
            s = qp / jnp.clip(jnp.max(jnp.abs(xf), axis=-1, keepdims=True), EPS, None)
            return (jnp.clip(jnp.round(xf * s), qn, qp) / s).astype(x.dtype)

        def weight_quant(w):
            wf = w.astype(jnp.float32)
            s = 1.0 / jnp.clip(jnp.mean(jnp.abs(wf)), EPS, None)
            return (jnp.clip(jnp.round(wf * s), -1.0, 1.0) / s).astype(w.dtype)

        def bit_linear(x, w):
            qx = x + jax.lax.stop_gradient(activation_quant(x) - x)
            qw = w + jax.lax.stop_gradient(weight_quant(w) - w)
            return jnp.einsum('bsh,oh->bso', qx, qw)

        def rms_norm(x, weight, eps=RMS_EPS):
            xf = x.astype(jnp.float32)
            var = jnp.mean(xf * xf, axis=-1, keepdims=True)
            return weight * (xf * jax.lax.rsqrt(var + eps)).astype(x.dtype)
        h = jax.nn.silu(bit_linear(x, w_gate)) * bit_linear(x, w_up)
        h = rms_norm(h, ln_weight)
        return bit_linear(h, w_down)
    x = x + jnp.tanh(g_xattn[0]) * _L0_xattn_ref(_layernorm(x, axis=-1), ctx_2048, ctx_2048, L0_xattn_Wh, L0_xattn_wg_w, L0_xattn_wo_w, L0_xattn_gn_gamma, L0_xattn_gn_beta)
    x = x + jnp.tanh(g_ffn[0]) * _L0_ffn_ref(_layernorm(x, axis=-1), L0_ffn_gate_w, L0_ffn_bias_corr, L0_ffn_up_w, L0_ffn_down_w, L0_ffn_shared_up_w, L0_ffn_shared_down_w)
    x = x + jnp.tanh(g_xattn[1]) * _L1_xattn_ref(_layernorm(x, axis=-1), ctx_2048, mask_BxS2_bk0)
    x = x + jnp.tanh(g_ffn[1]) * _L1_ffn_ref(_layernorm(x, axis=-1), L1_ffn_w_gate, L1_ffn_w_up, L1_ffn_w_down, L1_ffn_ln_weight)
    return x

_drawn_inputs = setup_inputs


def setup_inputs(seed=0):
    import zlib

    import numpy as np

    out = dict(_drawn_inputs(seed))
    spreads = {'g_ffn': (-1.0, 0.596),
     'L0_xattn_gn_gamma': (1.0, 0.2),
     'L0_xattn_gn_beta': (0.0, 0.1),
     'L0_ffn_bias_corr': (0.0, 0.408),
     'L1_ffn_ln_weight': (1.0, 0.2)}
    factors = {'L0_ffn_gate_w': 4.158, 'L0_ffn_up_w': 4.154, 'L0_ffn_down_w': 3.88}
    for name, (base, spread) in spreads.items():
        noise = np.random.default_rng([zlib.crc32(name.encode()), seed]).standard_normal(out[name].shape)
        drawn = base * np.exp(spread * noise) if base else spread * noise
        out[name] = jnp.asarray(drawn.astype(out[name].dtype))
    for name, factor in factors.items():
        out[name] = (out[name] * factor).astype(out[name].dtype)
    return out
```

```python
from contextlib import ExitStack

import concourse.bass as bass
import numpy as np
from concourse import mybir

F32 = mybir.dt.float32
F16 = mybir.dt.float16
BF16 = mybir.dt.bfloat16
U32 = mybir.dt.uint32
I32 = mybir.dt.int32
U8 = mybir.dt.uint8
ALU = mybir.AluOpType
ACT = mybir.ActivationFunctionType
AX = mybir.AxisListType

P = 128
B, S, D = 32, 64, 256
T = B * S
NT = T // P
NP = NT // 2
K = D // P
H, HD = 2, 128
E, G, TOPG, TOPK, CAP = 32, 8, 4, 4, 128
HS = 512
NHS = HS // P
I = 1024
NI = I // P
NG = E // 2
ROUTE_SCALE = 2.5
GN_EPS, LN_EPS, RMS_EPS, Q_EPS = 1e-3, 1e-5, 1e-6, 1e-5
ROUND = 1.5 * 2.0 ** 23
NEG = -1.6e31
SM_SCALE = 1.0 / 16.0
RA, RA_MASK = 29, 22
RB = 18
QQ = 9
SKIP = 65536.0


class Item:

    def __init__(self, c, j=None):
        self.c, self.j, self.slot = c, j, c % 2

    def at(self, per=1, plus=0):
        if self.j is None:
            return self.c * per + plus
        assert self.c * per + plus >= 0
        return self.j * (2 * per) + (self.c * per + plus)

    def below(self, n):
        return self.j is None and self.c < n


def run_steps(eng, n, stages):
    top = max(lag for lag, _ in stages)
    first = top + 2
    turns = max(0, (n - first) // 2)

    def step(t):
        for lag, stage in stages:
            if 0 <= t - lag < n:
                stage(Item(t - lag), (t - lag) % 2)

    for t in range(first):
        step(t)
    if turns:
        with eng.Fori(0, turns) as j:
            for k in range(2):
                for lag, stage in stages:
                    stage(Item(first + k - lag, j), (first + k - lag) % 2)
    for t in range(first + 2 * turns, n + top):
        step(t)


def slot_free(done, i, per=1):
    return [] if i.below(2) else [(done, i.at(per, -per))]


def free(done, i, per=1, plus=0):
    return [] if i.below(1) else [(done, i.at(per, plus))]


def landed(i, s):
    return i.at(8, 16 - 8 * s)


def landed_before(done, i, s):
    return [] if i.below(2) else [(done, i.at(8, -8 * s))]


def build(nc, a, out):
    with ExitStack() as ctx:
        def sb(name, shape, dt=F32):
            return ctx.enter_context(nc.sbuf_tensor(name, shape, dt))

        def sem(name):
            return ctx.enter_context(nc.semaphore(name))

        psum = ctx.enter_context(nc.psum_tensor("psum", [P, 8, 512], F32))

        xn_dram = nc.dram_tensor("xn_dram", (T, D), F32, kind="Internal").ap()
        ye_dram = nc.dram_tensor("ye_dram", (E * CAP, D), F32, kind="Internal").ap()

        ident = sb("ident", [P, P])
        dn = sb("dn", [S, H, S])
        tri = sb("tri", [P, P], BF16)
        ones = sb("ones", [P, P], BF16)
        onesf = sb("onesf", [P, P])
        iota_c = sb("iota_c", [P, P], F16)
        iota_e = sb("iota_e", [P, E])
        tokid = sb("tokid", [P, NT])
        sel = sb("sel", [2, P], BF16)
        mhalf = sb("mhalf", [P, 4])
        mround = sb("mround", [P, 1])
        wh = sb("wh", [P, H, HD])
        whT = sb("whT", [P, H, HD])
        gram = sb("gram", [P, H, HD])
        wg = sb("wg", [P, K, D])
        wo = sb("wo", [P, K, D])
        gnp = sb("gnp", [P, 2, K])
        gateT = sb("gateT", [P, K, E])
        biasc = sb("biasc", [P, E])
        shup = sb("shup", [P, K, HS])
        shdn = sb("shdn", [P, NHS, D])
        upT = sb("upT", [P, E, K, P])
        dnT = sb("dnT", [P, E, D])
        gates = sb("gates", [P, 4])
        tg = sb("tg", [P, 4])
        q_w = sb("q_w", [P, 3, K * I], BF16)
        wabs = sb("wabs", [P, 4])
        wmean = sb("wmean", [P, 3])
        winv = sb("winv", [P, 3])
        msk = sb("msk", [2, NT, S // 4], I32)
        msk8 = msk[:, :, :].bitcast(U8)

        x_all = sb("x_all", [P, NT, D])
        ctx_all = sb("ctx_all", [P, NT, D])
        ctxT_all = sb("ctxT_all", [P, K, T])
        big = sb("big", [P, 2, NT * D])
        v_all = big[:, 0, :].rearrange("p (n d) -> p n d", n=NT)
        xhT_all = big[:, 1, :].rearrange("p (k t) -> p k t", k=K)
        gath = big[:, 0, :].rearrange("p (s r d) -> p s r d", s=2, r=8)
        wraw = big[:, :, :].rearrange("p a n -> p (a n)")[:, 2 * NT * D - 3 * K * I:].rearrange("p (w n) -> p w n", w=3)

        bn = sb("bn", [P, 2, 2, 6])
        mv = sb("mv", [P, 2, 2, 2])
        ve = sb("ve", [P, 2, 2])
        rs = sb("rs", [P, 2, 2])
        bnx = sb("bnx", [P, 2, 2, 6])
        mvx = sb("mvx", [P, 2, 2, 2])
        vex = sb("vex", [P, 2, 2])
        rsx = sb("rsx", [P, 2, 2])
        xn = sb("xn", [P, 2, 2, D])
        xnT = sb("xnT", [P, 2, K, 2 * P])
        zr = sb("zr", [P, 2, 2, D])
        tr = sb("tr", [P, 2, K, 2 * P])
        wyT = tr
        rh = sb("rh", [P, 2, NHS * 2 * P])
        cring = rh[:, :, 0:K * 2 * P].rearrange("p s (k t) -> p s k t", k=K)
        ptr = wyT
        amat = tr[0:S, 0, :, 0:2 * S]
        bda = sb("bda", [P, H, P])
        lgt = sb("lgt", [P, 2 * E])
        sig = sb("sig", [P, 2, E])
        sc = sb("sc", [P, 2, E])
        psm = sb("psm", [P, 2 * G, 6])
        gs = sb("gs", [P, 2 * G])
        m8 = sb("m8", [P, 2, 8])
        i8 = sb("i8", [P, 2, 8], U32)
        gif = sb("gif", [P, 2, TOPG])
        eqg = sb("eqg", [P, 2, G, TOPG])
        gm = sb("gm", [P, 2 * G])
        msc = sb("msc", [P, 2, E])
        eif = sb("eif", [P, 2, TOPK])
        oh = wh[:, :, :].rearrange("p h (k e) -> p h k e", k=TOPK)
        mm = sb("mm", [P, 2, E], BF16)
        mcum = sb("mcum", [P, E], BF16)
        wsel = whT[:, :, :].rearrange("p h (k e) -> p h k e", k=TOPK)
        w4 = sb("w4", [P, 2, TOPK])
        wden = sb("wden", [P, 2, 1])
        wrec = sb("wrec", [P, 2, 1])
        wn = sb("wn", [P, 2, TOPK])
        posk = sb("posk", [P, 2, TOPK])
        vald = sb("vald", [P, 2, TOPK])
        dst = sb("dst", [P, 2, TOPK])
        ck = sb("ck", [P, 8, P], F16)
        te = gram[:, 0, :].bitcast(F16).rearrange("p (t n) -> p t n", t=2)
        idxf = sb("idxf", [P, E])
        idxi = sb("idxi", [P, E], I32)
        tix = sb("tix", [P, 2, 2], I32)
        rix = sb("rix", [P, 2, 2 * TOPK], I32)
        wk_all = sb("wk_all", [P, NT, TOPK])
        dst_all = sb("dst_all", [P, NT, TOPK], I32)

        xe = xn
        xeT = xnT
        hr = zr
        h2T = tr
        yr = rh[:, :, 0:2 * D].rearrange("p s (t d) -> p s t d", t=2)

        smx = sb("smx", [P, 2, 2])
        nmx = sb("nmx", [P, 2, 2])
        pexp = rh[:, 0, 0:4 * P].rearrange("p (s t m) -> p s t m", s=2, t=2)
        psumr = sb("psumr", [P, 2, 2])
        prec = sb("prec", [P, 2, 2])
        prt = sb("prt", [P, 2, 2])
        pT = rh[:, 1, 0:4 * P].rearrange("p (s m) -> p s m", s=2)
        x3n = zr
        amx = sb("amx", [P, 2, 2])
        qs = sb("qs", [P, 2, 2])
        dq = sb("dq", [P, 2, 2])
        cgs = sb("cgs", [P, 2, 2])
        cus = sb("cus", [P, 2, 2])
        xq = tr
        xqT = rh[:, 0, 4 * P:8 * P].bitcast(BF16).rearrange("p (s k t) -> p s k t", s=2, k=K)
        upf = upT[:, :, :, :].rearrange("p e k h -> p (e k h)")
        sg = upf[:, 0:2048].rearrange("p (s i) -> p s i", s=2)
        hh = upf[:, 2048:4096].rearrange("p (s i) -> p s i", s=2)
        hw = upf[:, 4096:6144].rearrange("p (s i) -> p s i", s=2)
        sqj = upf[:, 6144:7168]
        lnw = upf[:, 7168:8192]
        hq = sg
        dnf = dnT[:, :, :].rearrange("p e d -> p (e d)")
        hqT = dnf[:, 0:1024].bitcast(BF16).rearrange("p (s i) -> p s i", s=2)
        mnegb = shup[0:2, :, :].rearrange("p k n -> p (k n)").bitcast(BF16).rearrange("p (n a m) -> p n a m", n=NT, a=2)
        sst = sb("sst", [P, 2, 1])
        msq = sb("msq", [P, 2, 1])
        rq = sb("rq", [P, 2, 1])
        ham = sb("ham", [P, 2, 1])
        hs1 = sb("hs1", [P, 2, 4])

        c_in = sem("consts_in")
        c_x = [sem(f"x_in{i}") for i in range(2)]
        c_cr = [sem(f"ctxT_ring_in{i}") for i in range(2)]
        c_ctxT = sem("ctxT_in")
        c_ctx = sem("ctx_in")
        c_w2 = sem("phase2_weights_in")
        c_w3 = sem("expert_weights_in")
        c_w4 = sem("ffn_weights_in")
        c_lnw = sem("ln_weight_in")
        tixs, rixs, wqs, fsc = sem("token_index"), sem("row_index"), sem("ternary_steps"), sem("final_scale")
        hqs = [sem(f"h_quant_steps{t}") for t in range(2)]
        half_ok = sem("half_ok")
        gates_in, tg_ok = sem("gates_in"), sem("tanh_of_gates")
        gram_ps, gram_sb = sem("gram_ps"), sem("gram_sb")
        st1, rs1, xh1 = sem("stats1"), sem("rstd1"), sem("normed1")
        t1, xhT1 = sem("transposed1"), sem("xhT_copied")
        pt1, ptc1 = sem("proj1"), sem("proj_copied")
        v1, vc1 = sem("values"), sem("values_copied")
        s1 = sem("scores1")
        am, at, bd = sem("a_matrix"), sem("a_transposed"), sem("a_blocks")
        o2, sto, rso, z2 = sem("o_ready"), sem("o_stats"), sem("o_rstd"), sem("z_ready")
        w2, zt2, aff, wy2 = sem("w_ready"), sem("z_transposed"), sem("z_scaled"), sem("wy_ready")
        y2, x2, rs2, xn2 = sem("y_ready"), sem("x1_stats"), sem("x1_rstd"), sem("xn_ready")
        xnst = [sem(f"xn_stored{i}") for i in range(2)]
        t2, xnT2 = sem("xn_transposed"), sem("xnT_copied")
        lg2, su2, lt2, rl2, sq2 = sem("logits"), sem("shared_up"), sem("tanh_logits"), sem("shared_relu"), sem("shared_sq")
        sd2, sa2 = sem("shared_down"), sem("shared_added")
        ra, pos2, rb, ix2, ia2 = sem("route_a"), sem("positions"), sem("route_b"), sem("slots_ready"), sem("slots_added")
        idx_ok = sem("indices_ready")
        xg = [sem(f"tokens_gathered{i}") for i in range(4)]
        t3, xeT3, u3, hr3 = sem("xe_transposed"), sem("xeT_copied"), sem("h_ready"), sem("h_relu")
        ht3, h23, yd3, yc3 = sem("h_transposed"), sem("h_squared"), sem("ye_ready"), sem("ye_copied")
        yst = [sem(f"ye_stored{i}") for i in range(2)]
        gz = sem("gather_zeroed")
        gin = [[sem(f"rows_gathered{i}_{r}") for r in range(2)] for i in range(2)]
        c4, rs4, xn4 = sem("combined"), sem("x2_rstd"), sem("x2_normed")
        t4, xT4, sc4, mx4, ex4 = sem("x2_transposed"), sem("x2T_copied"), sem("scores4"), sem("scores_max"), sem("exp_done")
        pt4, pc4, ro4, x34 = sem("p_transposed"), sem("pT_copied"), sem("read_out"), sem("x3_stats")
        rs5, q5, t5, qT5 = sem("x3_rstd"), sem("x3_quant"), sem("xq_transposed"), sem("xqT_copied")
        gu, sl, hd, ssd = sem("gate_up"), sem("silu_done"), sem("h_done"), sem("h_sumsq")
        hwd, ms, rr, hqd = sem("hw_done"), sem("mean_square"), sem("h_rstd"), sem("h_quant")
        ht, hc, dwn, fo = sem("hq_transposed"), sem("hqT_copied"), sem("down_ready"), sem("x4_ready")
        wq_a, wq_s, wq_r, wq_g = sem("w_abs"), sem("w_total"), sem("w_scale"), sem("w_quant")
        mask_in, mk = sem("mask_in"), sem("mask_ready")
        ost = [sem(f"out_stored{i}") for i in range(2)]

        wait_value = {e.engine: e.alloc_register("wait_value") for e in (nc.scalar, nc.vector, nc.gpsimd)}

        def hold(eng, *waits):
            apart = eng.engine in wait_value and bool(waits) and not isinstance(waits[-1][1], int)
            if apart:
                eng.reg_mov(wait_value[eng.engine], waits[-1][1])
            for n, (s, v) in enumerate(waits):
                if apart and n == len(waits) - 1:
                    eng.wait_ge(half_ok, 1)
                    eng.wait_ge(s, wait_value[eng.engine])
                elif not isinstance(v, int) or v > 0:
                    eng.wait_ge(s, v)

        def tiles(i, n=2):
            return bass.ds(i.at(2), n)

        def tok(i):
            return bass.ds(i.at(2 * P), 2 * P)

        def xt(i, t):
            return x_all[:, bass.ds(i.at(2, t), 1), :].rearrange("p a d -> p (a d)")

        def bank(b, *shape):
            v = psum[:, b, :]
            if len(shape) == 2:
                return v.rearrange("p (a b) -> p a b", a=shape[0])
            return v

        block = ctx.enter_context(nc.Block())

        @block.sync
        def _(sp):
            for name, t in (("whT", whT), ("wh", wh)):
                sp.dma_start(t[:, :, :], a[name]).then_inc(c_in, 16)
            sp.dma_start(ident[:, :], a["c_ident"]).then_inc(c_in, 16)
            sp.dma_start(dn[:, :, :], a["c_dn"]).then_inc(c_in, 16)
            xv = a["x"].rearrange("(n p) d -> p n d", p=P)
            cv = a["ctx"].rearrange("(n p) d -> p n d", p=P)
            ctv = a["ctxT"].rearrange("(k p) t -> p k t", p=P)

            for i in range(2):
                sp.dma_start(x_all[:, tiles(Item(i)), :], xv[:, tiles(Item(i)), :]).then_inc(c_x[i], 16)
                sp.dma_start(cring[:, i, :, :], ctv[:, :, tok(Item(i))]).then_inc(c_cr[i], 16)
            sp.dma_start(ctxT_all[:, :, :], ctv).then_inc(c_ctxT, 16)
            with sp.Fori(0, (NP - 2) // 2) as j:
                for k in range(2):
                    i = Item(2 + k, j)
                    hold(sp, (c_x[k], i.at(8, -8 * k)))
                    sp.dma_start(x_all[:, tiles(i), :], xv[:, tiles(i), :]).then_inc(c_x[k], 16)
                    hold(sp, (v1, i.at(1, -1)))
                    sp.dma_start(cring[:, k, :, :], ctv[:, :, tok(i)]).then_inc(c_cr[k], 16)
            for name, t in (("wg", wg), ("wo", wo), ("gateT", gateT), ("shup", shup), ("shdn", shdn), ("gnp", gnp)):
                sp.dma_start(t[:, :, :], a[name]).then_inc(c_w2, 16)
            for name, t in (("c_tri", tri), ("c_iota_c", iota_c), ("c_iota_e", iota_e), ("c_tokid", tokid)):
                sp.dma_start(t[:, :], a[name]).then_inc(c_w2, 16)
            sp.dma_start(biasc[:, :], a["bias"].to_broadcast([P, E])).then_inc(c_w2, 16)
            sp.dma_start(ctx_all[:, :, :], cv).then_inc(c_ctx, 16)
            sp.dma_start(upT[:, :, :, :], a["upT"]).then_inc(c_w3, 16)
            sp.dma_start(dnT[:, :, :], a["dnT"]).then_inc(c_w3, 16)

            xnv = xn_dram.rearrange("(n p) d -> p n d", p=P)

            def store_xn(i, s):
                hold(sp, (xn2, i.at(2, 2)))
                sp.dma_start(xnv[:, tiles(i), :], xn[:, s, :, :]).then_inc(xnst[s], 16)

            run_steps(sp, NP - 1, [(0, store_xn)])
            sp.wait_ge(o2, NP)
            sp.wait_ge(w2, NP)
            for n, name in enumerate(("w_gate", "w_up", "w_down")):
                sp.dma_start(wraw[:, n, :], a[name]).then_inc(c_w4, 16)
            store_xn(Item(NP - 1), (NP - 1) % 2)

            yev = ye_dram.rearrange("(e c) d -> c e d", c=CAP)

            def store_ye(i, s):
                hold(sp, (yc3, i.at(1, 1)))
                sp.dma_start(yev[:, tiles(i), :], yr[:, s, :, :]).then_inc(yst[s], 16)

            run_steps(sp, NG, [(0, store_ye)])

            sp.wait_ge(yc3, NG)
            sp.dma_start(lnw, a["lnw"].to_broadcast([P, I])).then_inc(c_lnw, 16)
            ov = out.rearrange("(n p) d -> p n d", p=P)

            def store_out(i, s):
                hold(sp, (fo, i.at(2, 2)))
                sp.dma_start(ov[:, tiles(i), :], x_all[:, tiles(i), :]).then_inc(ost[s], 16)

            run_steps(sp, NP, [(0, store_out)])
            for s in range(2):
                sp.wait_ge(ost[s], 16 * NP // 2)

        @block.gpsimd
        def _(pl):
            pl.memset(mhalf[:, :], -0.5).then_inc(half_ok, 1)
            pl.dma_start(gates[:, :], a["gates"].to_broadcast([P, 4])).then_inc(gates_in, 16)
            pl.dma_start(msk[:, :, :], a["mask"]).then_inc(mask_in, 16)
            pl.memset(ones[:, :], 1.0)
            pl.memset(onesf[:, :], 1.0)
            pl.memset(mround[:, :], -ROUND)
            pl.memset(mcum[:, :], 0.0)
            pl.memset(idxf[:, :], 0.0)
            pl.memset(bda[:, :, :], 0.0)
            pl.memset(sel[:, :], 1.0).then_inc(half_ok, 1)
            pl.wait_ge(half_ok, 2)
            pl.affine_select(out=sel[:, :], in_=sel[:, :], compare_op=ALU.is_ge, fill=0.0, base=0,
                             pattern=[[1, P]], channel_multiplier=-S).then_inc(half_ok, 1)
            pl.wait_ge(half_ok, 3)
            pl.affine_select(out=sel[:, :], in_=sel[:, :], compare_op=ALU.is_ge, fill=0.0, base=S - 1,
                             pattern=[[-1, P]], channel_multiplier=S).then_inc(half_ok, 1)

            def rstd(stats, val, mvb, veb, rsb, eps, done):
                def stage(i, s):
                    hold(pl, (stats, val(i)))
                    pl.tensor_scalar(veb[:, s, :], mvb[:, s, :, 1], eps, None, ALU.add).then_inc(done, 1)
                    hold(pl, (done, i.at(2, 1)))
                    pl.tensor_tensor(rsb[:, s, :], veb[:, s, :], mhalf[:, 0:2], ALU.pow).then_inc(done, 1)
                return stage

            run_steps(pl, NP, [(0, rstd(st1, lambda i: i.at(4, 4), mv, ve, rs, LN_EPS, rs1))])

            def square_shared(i, s):
                hold(pl, (rl2, i.at(1, 1)))
                pl.tensor_tensor(rh[:, s, :], rh[:, s, :], rh[:, s, :], ALU.mult).then_inc(sq2, 1)

            run_steps(pl, NP, [
                (0, rstd(sto, lambda i: i.at(4, 4), mv, ve, rs, GN_EPS, rso)),
                (1, rstd(x2, lambda i: i.at(5, 5), mvx, vex, rsx, LN_EPS, rs2)),
                (1, square_shared)])

            for s in range(2):
                pl.wait_ge(xnst[s], 16 * NP // 2)
            pl.wait_ge(idx_ok, 1)

            def gather_tokens(i, s):
                hold(pl, *slot_free(t3, i))
                pl.tensor_copy(tix[:, s, :], idxi[:, tiles(i)]).then_inc(tixs, 1)
                hold(pl, (tixs, i.at(1, 1)))
                for k in range(2):
                    pl.indirect_dma_start(out=xe[:, s, k, :], out_offset=None, in_=xn_dram[:, :],
                                          in_offset=bass.IndirectOffsetOnAxis(ap=tix[:, s, k:k + 1], axis=0),
                                          bounds_check=T - 1, oob_is_err=False).then_inc(xg[2 * s + k], 16)

            run_steps(pl, NG, [(0, gather_tokens)])

            pl.wait_ge(su2, NP)
            pl.wait_ge(mask_in, 16)
            for b in range(2):
                ins = pl.tensor_scalar(mnegb[:, :, b, :], msk8[:, :, :], -1.0, -NEG, ALU.add, ALU.mult)
            ins.then_inc(mk, 1)
            pl.wait_ge(mk, 1)
            pl.affine_select(out=mnegb, in_=mnegb, compare_op=ALU.is_equal, fill=NEG, base=0,
                             pattern=[[0, NT], [-1, 2], [0, S]], channel_multiplier=1).then_inc(mk, 1)

            pl.wait_ge(wqs, 3 * NG)
            pl.memset(gath[:, :, :, :], 0.0).then_inc(gz, 1)
            for s in range(2):
                pl.wait_ge(yst[s], 16 * NG // 2)
            pl.wait_ge(gz, 1)

            def rows(part):
                def stage(i, s):
                    if part == 0:
                        hold(pl, *slot_free(c4, i, 12))
                        pl.tensor_copy(rix[:, s, :], dst_all[:, tiles(i), :].rearrange("p t k -> p (t k)"))\
                          .then_inc(rixs, 1)
                        hold(pl, (rixs, i.at(1, 1)))
                    for r in range(2 * part, 2 * part + 2):
                        pl.indirect_dma_start(
                            out=gath[:, s, r, :], out_offset=None, in_=ye_dram[:, :],
                            in_offset=bass.IndirectOffsetOnAxis(ap=rix[:, s, r:r + 1], axis=0),
                            bounds_check=E * CAP - 1, oob_is_err=False).then_inc(gin[s][r // TOPK], 16)
                return stage

            def rms(t):
                def stage(i, s):
                    hold(pl, (ssd, i.at(2, t + 1)), *free(hqd, i, 2, t - 1))
                    pl.tensor_scalar(msq[:, t, :], sst[:, t, :], 1.0 / I, RMS_EPS, ALU.mult, ALU.add).then_inc(ms, 1)
                    hold(pl, (ms, i.at(2, t + 1)))
                    pl.tensor_tensor(rq[:, t, :], msq[:, t, :], mhalf[:, 0:1], ALU.pow).then_inc(rr, 1)
                return stage

            run_steps(pl, NP, [
                (0, rows(0)), (2, rstd(c4, lambda i: i.at(12, 12), mv, ve, rs, LN_EPS, rs4)), (0, rows(1)),
                (4, rms(0)), (0, rows(2)), (4, rms(1)), (0, rows(3)),
                (3, rstd(x34, lambda i: i.at(9, 9), mvx, vex, rsx, LN_EPS, rs5))])

        @block.scalar
        def _(act):
            def copy_to(dst_ap, src, done, func=ACT.Copy, **kw):
                return act.activation(dst_ap, src, func, **kw).then_inc(done, 1)

            act.wait_ge(gates_in, 16)
            act.activation(tg[:, :], gates[:, :], ACT.Tanh).then_inc(tg_ok, 1)
            act.wait_ge(gram_ps, 1)
            act.activation(gram[:, :, :], bank(0)[:, 0:H * HD].rearrange("p (h e) -> p h e", h=H), ACT.Copy)\
               .then_inc(gram_sb, 1)

            def p1_v(i, s):
                hold(act, (v1, i.at(1, 1)))
                copy_to(v_all[:, tiles(i), :], bank(1, 2, D), vc1)

            def p1_t(i, s):
                hold(act, (t1, i.at(1, 1)))
                copy_to(xhT_all[:, :, tok(i)], bank(2, K, 2 * P), xhT1)

            run_steps(act, NP, [(0, p1_v), (0, p1_t)])

            def affine(i, s):
                hold(act, (zt2, i.at(1, 1)), *slot_free(wy2, i))
                for k in range(K):
                    ins = act.activation(tr[:, s, k, :], bank(2, K, 2 * P)[:, k, :], ACT.Identity,
                                         scale=gnp[:, 0, k:k + 1], bias=gnp[:, 1, k:k + 1])
                ins.then_inc(aff, 1)

            def copy_xnT(i, s):
                hold(act, (t2, i.at(1, 1)), *slot_free(su2, i))
                copy_to(xnT[:, s, :, :], bank(2, K, 2 * P), xnT2)

            def tanh_logits(i, s):
                hold(act, (lg2, i.at(1, 1)), *free(ra, i, RA))
                copy_to(lgt[:, :], bank(5)[:, 0:2 * E], lt2, ACT.Tanh, scale=0.5)

            def relu_shared(i, s):
                hold(act, (su2, i.at(1, 1)), *slot_free(sd2, i))
                copy_to(rh[:, s, :].rearrange("p (b n) -> p b n", b=2), psum[:, 6:8, :], rl2, ACT.Relu)

            act.wait_ge(c_w2, 16 * 11)
            run_steps(act, NP, [(0, affine), (1, copy_xnT), (1, tanh_logits), (1, relu_shared)])

            def copy_xeT(i, s):
                hold(act, (t3, i.at(1, 1)), *slot_free(u3, i))
                copy_to(xeT[:, s, :, :], bank(2, K, 2 * P), xeT3)

            def square_h(i, s):
                hold(act, (ht3, i.at(1, 1)), *slot_free(yd3, i))
                copy_to(h2T[:, s, 0, :], bank(4)[:, 0:2 * P], h23, ACT.Square)

            act.wait_ge(c_w4, 48)
            for n in range(3):
                act.activation(q_w[:, n, :], wraw[:, n, :], ACT.Abs, accum_out=wabs[:, n:n + 1]).then_inc(wq_a, 1)

            run_steps(act, NG, [(0, copy_xeT), (1, square_h)])

            def copy_x2T(i, s):
                hold(act, (t4, i.at(1, 1)), *slot_free(sc4, i))
                copy_to(xnT[:, s, :, :], bank(4, K, 2 * P), xT4)

            def exps(i, s):
                hold(act, (mx4, i.at(2, 2)), *slot_free(pt4, i))
                for t in range(2):
                    ins = act.activation(pexp[:, s, t, :], bank(5)[:, t * P:(t + 1) * P], ACT.Exp, scale=SM_SCALE,
                                         bias=nmx[:, s, t:t + 1], accum_out=psumr[:, s, t:t + 1])
                ins.then_inc(ex4, 1)

            def copy_pT(i, s):
                hold(act, (pt4, i.at(1, 1)), *slot_free(ro4, i))
                copy_to(pT[:, s, :], bank(4)[:, 0:2 * P], pc4)

            def copy_xqT(i, s):
                hold(act, (t5, i.at(1, 1)), *slot_free(gu, i, 2))
                copy_to(xqT[:, s, :, :], bank(4, K, 2 * P), qT5, ACT.Identity, bias=mround[:, :])

            def silu(t):
                def stage(i, s):
                    hold(act, (gu, i.at(2, t + 1)), *free(ht, i, 4, 2 * t - 2))
                    act.activation(sg[:, t, :].rearrange("p (b n) -> p b n", b=2), psum[:, 0:2, :], ACT.Silu,
                                   scale=cgs[:, s, t:t + 1]).then_inc(sl, 1)
                return stage

            def sumsq(t):
                def stage(i, s):
                    hold(act, (hd, i.at(2, t + 1)), *([] if i.below(1) and t == 0 else [(ssd, i.at(2, t))]),
                         *free(ms, i, 2, t - 1))
                    act.activation(sqj, hh[:, t, :], ACT.Square, accum_out=sst[:, t, :]).then_inc(ssd, 1)
                return stage

            def copy_hqT(t, b):
                def stage(i, s):
                    hold(act, (ht, i.at(4, 2 * t + b + 1)), *free(dwn, i, 2, t - 1))
                    copy_to(hqT[:, t, b * 512:(b + 1) * 512], bank(7), hc, ACT.Identity, bias=mround[:, :])
                return stage

            run_steps(act, NP, [
                (2, copy_xqT), (2, silu(0)), (0, copy_x2T), (2, sumsq(0)), (2, silu(1)), (2, sumsq(1)), (0, exps),
                (1, copy_pT), (2, copy_hqT(0, 0)), (2, copy_hqT(0, 1)), (2, copy_hqT(1, 0)), (2, copy_hqT(1, 1))])

        @block.tensor
        def _(pe):
            def mm_(o, l, r, first=True, last=True):
                return pe.matmul(o, l, r, start=first, stop=last, skip_group_check=True)

            pe.wait_ge(half_ok, 4)
            pe.wait_ge(c_in, 16 * 4)
            for h in range(H):
                ins = mm_(bank(0)[:, h * HD:(h + 1) * HD], whT[:, h, :], whT[:, h, :])
            ins.then_inc(gram_ps, 1)
            for h in range(H):
                mm_(bank(3)[0:S, h * S:(h + 1) * S], bda[:, h, 0:S], bda[:, h, 0:S], h == 0, False)

            def p1_v(i, s):
                n16 = landed(i, s)
                hold(pe, (c_cr[s], n16), *free(vc1, i))
                for t in range(2):
                    for h in range(H):
                        ins = mm_(bank(1, 2, D)[:, t, h * HD:(h + 1) * HD],
                                  cring[:, s, h, t * P:(t + 1) * P], wh[:, h, :])
                ins.then_inc(v1, 1)

            def p1_t(i, s):
                hold(pe, (xh1, i.at(2, 2)), *free(xhT1, i))
                for t in range(2):
                    for k in range(K):
                        ins = pe.transpose(bank(2, K, 2 * P)[:, k, t * P:(t + 1) * P],
                                           xn[:, s, t, k * P:(k + 1) * P], ident[:, :])
                ins.then_inc(t1, 1)

            def p1_p(i, s):
                hold(pe, (xhT1, i.at(1, 1)), *free(ptc1, i))
                for h in range(H):
                    ins = mm_(bank(0, H, 2 * P)[:, h, :], gram[:, h, :], xhT_all[:, h, tok(i)])
                ins.then_inc(pt1, 1)

            def p1_s(i, s):
                hold(pe, (ptc1, i.at(1, 1)))
                for b in range(4):
                    for h in range(H):
                        ins = mm_(bank(3)[0:S, h * S:(h + 1) * S], ptr[:, s, h, b * S:(b + 1) * S],
                                  ctxT_all[:, h, bass.ds(i.at(2 * P, b * S), S)], False, False)
                ins.then_inc(s1, 1)

            pe.wait_ge(gram_sb, 1)
            pe.wait_ge(c_ctxT, 16)
            run_steps(pe, NP, [(0, p1_v), (1, p1_s), (0, p1_t), (0, p1_p)])
            pe.wait_ge(am, 4)
            for h in range(H):
                ins = pe.transpose(bank(4)[:, h * S:(h + 1) * S], amat[:, h, :], ident[0:S, 0:S])
            ins.then_inc(at, 1)

            def p2_o(i, s):
                hold(pe, *free(z2, i, 2))
                for h in range(H):
                    ins = mm_(bank(0, 2, D)[:, :, h * HD:(h + 1) * HD], bda[:, h, :],
                              v_all[:, tiles(i), h * HD:(h + 1) * HD])
                ins.then_inc(o2, 1)

            def p2_w(i, s):
                hold(pe, *free(wy2, i))
                for j in range(K):
                    for k in range(K):
                        ins = mm_(bank(3, K, 2 * P)[:, j, :], wg[:, k, j * P:(j + 1) * P], xhT_all[:, k, tok(i)],
                                  k == 0, k == K - 1)
                ins.then_inc(w2, 1)

            def p2_zt(i, s):
                hold(pe, (z2, i.at(2, 2)), *slot_free(xnT2, i))
                for t in range(2):
                    for k in range(K):
                        ins = pe.transpose(bank(2, K, 2 * P)[:, k, t * P:(t + 1) * P],
                                           zr[:, s, t, k * P:(k + 1) * P], ident[:, :])
                ins.then_inc(zt2, 1)

            def p2_y(i, s):
                hold(pe, (wy2, i.at(1, 1)), *slot_free(sa2, i))
                for t in range(2):
                    for k in range(K):
                        ins = mm_(bank(4, 2, D)[:, t, :], wyT[:, s, k, t * P:(t + 1) * P], wo[:, k, :],
                                  k == 0, k == K - 1)
                ins.then_inc(y2, 1)

            def p2_xt(i, s):
                last = i.j is None and i.c == NP - 1
                hold(pe, (xn2, i.at(2, 2)), (aff, i.at(1, 1 if last else 2)))
                for t in range(2):
                    for k in range(K):
                        ins = pe.transpose(bank(2, K, 2 * P)[:, k, t * P:(t + 1) * P],
                                           xn[:, s, t, k * P:(k + 1) * P], ident[:, :])
                ins.then_inc(t2, 1)

            def p2_lg(i, s):
                hold(pe, (xnT2, i.at(1, 1)), *free(lt2, i))
                for t in range(2):
                    for k in range(K):
                        ins = mm_(bank(5)[:, t * E:(t + 1) * E], xnT[:, s, k, t * P:(t + 1) * P], gateT[:, k, :],
                                  k == 0, k == K - 1)
                ins.then_inc(lg2, 1)

            def p2_su(i, s):
                hold(pe, *free(rl2, i))
                for n in range(NHS):
                    for k in range(K):
                        ins = mm_(psum[:, 6 + n // 2, (n % 2) * 256:(n % 2) * 256 + 256],
                                  shup[:, k, n * P:(n + 1) * P], xnT[:, s, k, :], k == 0, k == K - 1)
                ins.then_inc(su2, 1)

            def p2_sd(i, s):
                last = i.j is None and i.c == NP - 1
                hold(pe, (sq2, i.at(1, 1)), (x2, i.at(5, 1 if last else 6)))
                for t in range(2):
                    for n in range(NHS):
                        ins = mm_(bank(4, 2, D)[:, t, :],
                                  rh[:, s, n * 256 + t * P:n * 256 + (t + 1) * P],
                                  shdn[:, n, :], n == 0, n == NHS - 1)
                ins.then_inc(sd2, 1)

            def p2_pos(i, s):
                hold(pe, (ra, i.at(RA, RA_MASK)), *free(rb, i, RB), *free(ia2, i))
                pos = bank(1)[:, 0:2 * E]
                mm_(pos[:, 0:E], tri[:, :], mm[:, 0, :], True, False)
                mm_(pos[:, 0:E], ones[:, :], mcum[:, :], False, True)
                mm_(pos[:, E:2 * E], tri[:, :], mm[:, 1, :], True, False)
                mm_(pos[:, E:2 * E], ones[:, :], mm[:, 0, :], False, False)
                mm_(pos[:, E:2 * E], ones[:, :], mcum[:, :], False, True).then_inc(pos2, 1)

            def p2_ix(i, s):
                hold(pe, (rb, i.at(RB, RB)), *free(ia2, i))
                for r in range(8):
                    ins = mm_(bank(1)[:, 2 * E:3 * E], ck[:, r, :], te[:, r // TOPK, (r % TOPK) * E:(r % TOPK + 1) * E],
                              r == 0, r == 7)
                ins.then_inc(ix2, 1)

            pe.wait_ge(c_w2, 16 * 11)
            pe.wait_ge(bd, 2 * H)
            pe.wait_ge(vc1, NP)
            run_steps(pe, NP, [(0, p2_o), (0, p2_w), (1, p2_y), (2, p2_pos), (0, p2_zt), (2, p2_sd), (1, p2_xt),
                               (1, p2_lg), (1, p2_su), (2, p2_ix)])

            def p3_t(i, s):
                n16 = landed(i, s)
                hold(pe, (xg[2 * s], n16), (xg[2 * s + 1], n16), *free(xeT3, i))
                for e in range(2):
                    for k in range(K):
                        ins = pe.transpose(bank(2, K, 2 * P)[:, k, e * P:(e + 1) * P],
                                           xe[:, s, e, k * P:(k + 1) * P], ident[:, :])
                ins.then_inc(t3, 1)

            def p3_u(i, s):
                hold(pe, (xeT3, i.at(1, 1)), *free(hr3, i))
                for e in range(2):
                    for k in range(K):
                        w = upT[:, bass.ds(i.at(2, e), 1), k, :]
                        ins = mm_(bank(3)[:, e * P:(e + 1) * P], xeT[:, s, k, e * P:(e + 1) * P],
                                  w.rearrange("p a h -> p (a h)"), k == 0, k == K - 1)
                ins.then_inc(u3, 1)

            def p3_ht(i, s):
                hold(pe, (hr3, i.at(1, 1)), *free(h23, i))
                for e in range(2):
                    ins = pe.transpose(bank(4)[:, e * P:(e + 1) * P], hr[:, s, 0, e * P:(e + 1) * P], ident[:, :])
                ins.then_inc(ht3, 1)

            def p3_d(i, s):
                hold(pe, (h23, i.at(1, 1)), *slot_free(yc3, i))
                for e in range(2):
                    w = dnT[:, bass.ds(i.at(2, e), 1), :]
                    ins = mm_(bank(s, 2, D)[:, e, :], h2T[:, s, 0, e * P:(e + 1) * P],
                              w.rearrange("p a d -> p (a d)"))
                ins.then_inc(yd3, 1)

            pe.wait_ge(wq_a, 3)
            mm_(bank(6)[:, 0:3], onesf[:, :], wabs[:, 0:3]).then_inc(wq_s, 1)
            pe.wait_ge(c_w3, 32)
            run_steps(pe, NG, [(0, p3_t), (1, p3_u), (2, p3_d), (1, p3_ht)])

            def x2t(i, s):
                hold(pe, (xn4, i.at(2, 2)), (xT4, i.at()) if i.below(2) else (qT5, i.at(1, -1)))
                for t in range(2):
                    for k in range(K):
                        ins = pe.transpose(bank(4, K, 2 * P)[:, k, t * P:(t + 1) * P],
                                           xn[:, s, t, k * P:(k + 1) * P], ident[:, :])
                ins.then_inc(t4, 1)

            def score(i, s):
                hold(pe, (xT4, i.at(1, 1)), *free(ex4, i))
                for t in range(2):
                    o = bank(5)[:, t * P:(t + 1) * P]
                    mm_(o, sel[:, :], mnegb[:, bass.ds(i.at(2, t), 1), :, :].rearrange("p n a m -> p (n a m)"),
                        True, False)
                    for k in range(K):
                        ins = mm_(o, xnT[:, s, k, t * P:(t + 1) * P],
                                  ctxT_all[:, k, bass.ds(i.at(2 * P, t * P), P)], False, k == K - 1)
                ins.then_inc(sc4, 1)

            def pt(i, s):
                last = i.j is None and i.c == NP - 1
                hold(pe, (ex4, i.at(1, 1)), (qT5, i.at()) if last else (xT4, i.at(1, 2)))
                for t in range(2):
                    ins = pe.transpose(bank(4)[:, t * P:(t + 1) * P], pexp[:, s, t, :], ident[:, :])
                ins.then_inc(pt4, 1)

            def read(i, s):
                hold(pe, (pc4, i.at(1, 1)), *free(x34, i, 9, -4))
                for t in range(2):
                    ins = mm_(bank(6, 2, D)[:, t, :], pT[:, s, t * P:(t + 1) * P],
                              ctx_all[:, bass.ds(i.at(2, t), 1), :].rearrange("p a d -> p (a d)"))
                ins.then_inc(ro4, 1)

            def xqt(i, s):
                hold(pe, (q5, i.at(QQ, QQ)), (pc4, i.at(1, 1)))
                for t in range(2):
                    for k in range(K):
                        ins = pe.transpose(bank(4, K, 2 * P)[:, k, t * P:(t + 1) * P],
                                           xq[:, s, t, k * P:(k + 1) * P], ident[:, :])
                ins.then_inc(t5, 1)

            def gateup(t):
                def stage(i, s):
                    hold(pe, (qT5, i.at(1, 1)), *([] if i.below(1) and t == 0 else [(sl, i.at(2, t)), (hd, i.at(2, t))]),
                         *(free(fo, i, 2) if t == 0 else []))
                    for w in range(2):
                        for b in range(2):
                            for k in range(K):
                                ins = mm_(psum[:, 2 * w + b, :], xqT[:, s, k, t * P:(t + 1) * P],
                                          q_w[:, w, k * I + b * 512:k * I + (b + 1) * 512], k == 0, k == K - 1)
                    ins.then_inc(gu, 1)
                return stage

            def hqt(t, b):
                def stage(i, s):
                    first = i.below(1) and t == 0 and b == 0
                    hold(pe, (hqd, i.at(2, t + 1)), *([] if first else [(hc, i.at(4, 2 * t + b))]))
                    for c in range(4):
                        ins = pe.transpose(bank(7)[:, c * P:(c + 1) * P],
                                           hq[:, t, (4 * b + c) * P:(4 * b + c + 1) * P], ident[:, :])
                    ins.then_inc(ht, 1)
                return stage

            def down(t):
                def stage(i, s):
                    hold(pe, (hc, i.at(4, 2 * t + 2)), (sl, i.at(2, 2)))
                    for c in range(NI):
                        ins = mm_(bank(t)[:, 0:D], hqT[:, t, c * P:(c + 1) * P],
                                  q_w[:, 2, c * D:(c + 1) * D], c == 0, c == NI - 1)
                    ins.then_inc(dwn, 1)
                return stage

            pe.wait_ge(c_ctx, 16)
            pe.wait_ge(mk, 2)
            pe.wait_ge(wqs, 3 * NG)
            run_steps(pe, NP, [
                (2, xqt), (2, gateup(0)), (0, x2t), (0, score), (2, gateup(1)), (1, pt), (1, read),
                (2, hqt(0, 0)), (2, hqt(0, 1)), (2, down(0)), (2, hqt(1, 0)), (2, hqt(1, 1)), (2, down(1))])

        @block.vector
        def _(dve):
            class Chain:

                def __init__(self, s_, i, per):
                    self.s, self.i, self.per, self.n = s_, i, per, 0

                def __call__(self, ins):
                    self.n += 1
                    return ins.then_inc(self.s, 1)

                def sync(self):
                    hold(dve, (self.s, self.i.at(self.per, self.n)))

                def end(self):
                    assert self.n == self.per, (self.n, self.per)

            def stats(c, src, s, bnb, mvb):
                for t in range(2):
                    c(dve.bn_stats(bnb[:, s, t, :], src(t)))
                c.sync()
                for t in range(2):
                    c(dve.bn_aggr(mvb[:, s, t, :], bnb[:, s, t, :]))

            dve.wait_ge(half_ok, 1)

            def p1_stats(i, s):
                n16 = landed(i, s)
                hold(dve, (c_x[s], n16))
                c = Chain(st1, i, 4)
                stats(c, lambda t: xt(i, t), s, bn, mv)
                c.end()

            def normalise(rsem, src, s, i, mvb, rsb, done, dest, *waits):
                hold(dve, (rsem, i.at(2, 2)), *waits)
                for t in range(2):
                    dve.tensor_scalar(dest[:, s, t, :], src(t), mvb[:, s, t, 0:1], rsb[:, s, t:t + 1],
                                      ALU.subtract, ALU.mult).then_inc(done, 1)

            def xtile(i):
                return lambda t: xt(i, t)

            def p1_norm(i, s):
                normalise(rs1, xtile(i), s, i, mv, rs, xh1, xn, (st1, i.at(4, 4)), *slot_free(t1, i))

            def p1_pt(i, s):
                hold(dve, (pt1, i.at(1, 1)), *slot_free(s1, i))
                dve.tensor_copy(ptr[:, s, :, :], bank(0, H, 2 * P)).then_inc(ptc1, 1)

            run_steps(dve, NP, [(0, p1_stats), (0, p1_norm), (0, p1_pt)])

            dve.wait_ge(s1, NP)
            dve.tensor_tensor(amat[:, :, 0:S], bank(3)[0:S, 0:H * S].rearrange("p (h t) -> p h t", h=H),
                              dn[:, :, :], ALU.mult).then_inc(am, 1)
            dve.wait_ge(am, 1)
            dve.scalar_tensor_tensor(amat[:, :, S:2 * S], amat[:, :, 0:S], -1.0, amat[:, :, 0:S],
                                     ALU.mult, ALU.max).then_inc(am, 1)
            dve.wait_ge(am, 2)
            dve.tensor_scalar(amat[:, :, 0:S], amat[:, :, S:2 * S], 1.0, None, ALU.max).then_inc(am, 1)
            dve.wait_ge(am, 3)
            dve.tensor_copy(amat[:, :, S:2 * S], amat[:, :, 0:S]).then_inc(am, 1)
            dve.wait_ge(at, 1)
            dve.wait_ge(half_ok, 2)
            for h in range(H):
                for b in range(2):
                    dve.tensor_copy(bda[b * S:(b + 1) * S, h, b * S:(b + 1) * S],
                                    bank(4)[b * S:(b + 1) * S, h * S:(h + 1) * S]).then_inc(bd, 1)

            def o_stats(i, s):
                hold(dve, (o2, i.at(1, 1)))
                c = Chain(sto, i, 4)
                stats(c, lambda t: bank(0, 2, D)[:, t, :], s, bn, mv)
                c.end()

            def z(i, s):
                normalise(rso, lambda t: bank(0, 2, D)[:, t, :], s, i, mv, rs, z2, zr, (sto, i.at(4, 4)), *slot_free(zt2, i))

            def wy(i, s):
                hold(dve, (aff, i.at(1, 1)), (w2, i.at(1, 1)), *slot_free(y2, i))
                dve.scalar_tensor_tensor(wyT[:, s, :, :], bank(3, K, 2 * P), 0.0, tr[:, s, :, :],
                                         ALU.max, ALU.mult).then_inc(wy2, 1)

            def x1(i, s):
                hold(dve, (y2, i.at(1, 1)))
                c = Chain(x2, i, 5)
                c(dve.scalar_tensor_tensor(x_all[:, tiles(i), :], bank(4, 2, D), tg[:, 0:1], x_all[:, tiles(i), :],
                                           ALU.mult, ALU.add))
                c.sync()
                stats(c, xtile(i), s, bnx, mvx)
                c.end()

            def xn_(i, s):
                st = landed_before(xnst[s], i, s)
                normalise(rs2, xtile(i), s, i, mvx, rsx, xn2, xn, (x2, i.at(5, 5)), *slot_free(t2, i), *st)

            def shared(i, s):
                hold(dve, (sd2, i.at(1, 1)))
                dve.scalar_tensor_tensor(x_all[:, tiles(i), :], bank(4, 2, D), tg[:, 2:3], x_all[:, tiles(i), :],
                                         ALU.mult, ALU.add).then_inc(sa2, 1)

            def route_a(i, s):
                hold(dve, (lt2, i.at(1, 1)))
                c = Chain(ra, i, RA)
                c(dve.tensor_scalar(sig[:, :, :], lgt[:, :].rearrange("p (t e) -> p t e", t=2), 0.5, 0.5,
                                    ALU.mult, ALU.add))
                c.sync()
                c(dve.tensor_tensor(sc[:, :, :], sig[:, :, :], biasc[:, None, :].to_broadcast([P, 2, E]), ALU.add))
                c.sync()
                v = sc[:, :, :].rearrange("p t (g m) -> p (t g) m", g=G)
                c(dve.tensor_tensor(psm[:, :, 0:2], v[:, :, 0:4:2], v[:, :, 1:4:2], ALU.add))
                c(dve.tensor_tensor(psm[:, :, 2:4], v[:, :, 0:2], v[:, :, 2:4], ALU.add))
                c(dve.tensor_tensor(psm[:, :, 4:5], v[:, :, 0:1], v[:, :, 3:4], ALU.add))
                c(dve.tensor_tensor(psm[:, :, 5:6], v[:, :, 1:2], v[:, :, 2:3], ALU.add))
                c.sync()
                c(dve.tensor_reduce(gs[:, :], psm[:, :, :], AX.X, ALU.max))
                c.sync()
                for t in range(2):
                    c(dve.max(m8[:, t, :], gs[:, t * G:(t + 1) * G]))
                c.sync()
                for t in range(2):
                    c(dve.max_index(i8[:, t, :], m8[:, t, :], gs[:, t * G:(t + 1) * G]))
                c.sync()
                c(dve.tensor_copy(gif[:, :, :], i8[:, :, 0:TOPG]))
                c.sync()
                c(dve.tensor_tensor(eqg[:, :, :, :], iota_e[:, None, 0:G, None].to_broadcast([P, 2, G, TOPG]),
                                    gif[:, :, None, :].to_broadcast([P, 2, G, TOPG]), ALU.is_equal))
                c.sync()
                c(dve.tensor_reduce(gm[:, :], eqg[:, :, :, :].rearrange("p t g k -> p (t g) k"), AX.X, ALU.add))
                c.sync()
                c(dve.tensor_tensor(msc[:, :, :].rearrange("p t (g m) -> p (t g) m", g=G), v,
                                    gm[:, :, None].to_broadcast([P, 2 * G, E // G]), ALU.mult))
                c.sync()
                for t in range(2):
                    c(dve.max(m8[:, t, :], msc[:, t, :]))
                c.sync()
                for t in range(2):
                    c(dve.max_index(i8[:, t, :], m8[:, t, :], msc[:, t, :]))
                c.sync()
                c(dve.tensor_copy(eif[:, :, :], i8[:, :, 0:TOPK]))
                c.sync()
                c(dve.tensor_tensor(oh[:, :, :, :], iota_e[:, None, None, :].to_broadcast([P, 2, TOPK, E]),
                                    eif[:, :, :, None].to_broadcast([P, 2, TOPK, E]), ALU.is_equal))
                c.sync()
                with nc.allow_low_precision(reason="sums of at most one 1"):
                    c(dve.tensor_reduce(mm[:, :, :], oh[:, :, :, :].rearrange("p t k e -> p t e k"), AX.X, ALU.add))
                assert c.n == RA_MASK, c.n
                c(dve.tensor_tensor(wsel[:, :, :, :], oh[:, :, :, :],
                                    sig[:, :, None, :].to_broadcast([P, 2, TOPK, E]), ALU.mult))
                c.sync()
                c(dve.tensor_reduce(w4[:, :, :], wsel[:, :, :, :], AX.X, ALU.add))
                c.sync()
                c(dve.tensor_reduce(wden[:, :, 0], w4[:, :, :], AX.X, ALU.add))
                c.sync()
                c(dve.tensor_scalar(wden[:, :, :], wden[:, :, :], 1e-20, None, ALU.add))
                c.sync()
                c(dve.reciprocal(wrec[:, :, :], wden[:, :, :]))
                c.sync()
                c(dve.tensor_tensor(wn[:, :, :], w4[:, :, :], wrec[:, :, :].to_broadcast([P, 2, TOPK]), ALU.mult))
                c.sync()
                c(dve.tensor_scalar(wn[:, :, :], wn[:, :, :], tg[:, 2:3], ROUTE_SCALE, ALU.mult, ALU.mult))
                c.end()

            def route_b(i, s):
                hold(dve, (pos2, i.at(1, 1)), (ra, i.at(RA, RA)), *free(ix2, i))
                c = Chain(rb, i, RB)
                pos = bank(1)[:, 0:2 * E].rearrange("p (t e) -> p t e", t=2)
                c(dve.tensor_tensor(wsel[:, :, :, :], oh[:, :, :, :],
                                    pos[:, :, None, :].to_broadcast([P, 2, TOPK, E]), ALU.mult))
                c(dve.tensor_tensor(mcum[:, :], mcum[:, :], mm[:, 0, :], ALU.add))
                c.sync()
                c(dve.tensor_tensor(mcum[:, :], mcum[:, :], mm[:, 1, :], ALU.add))
                c(dve.tensor_reduce(posk[:, :, :], wsel[:, :, :, :], AX.X, ALU.add))
                c.sync()
                c(dve.tensor_scalar(vald[:, :, :], posk[:, :, :], float(CAP), None, ALU.is_lt))
                c(dve.scalar_tensor_tensor(dst[:, :, :], eif[:, :, :], float(CAP), posk[:, :, :], ALU.mult, ALU.add))
                c.sync()
                c(dve.tensor_tensor(wk_all[:, tiles(i), :], wn[:, :, :], vald[:, :, :], ALU.mult))
                c(dve.scalar_tensor_tensor(dst[:, :, :], vald[:, :, :], -SKIP, dst[:, :, :], ALU.mult, ALU.add))
                c.sync()
                c(dve.tensor_scalar(dst_all[:, tiles(i), :], dst[:, :, :], SKIP, None, ALU.add))
                c(dve.tensor_tensor(te[:, :, :], oh[:, :, :, :].rearrange("p t k e -> p t (k e)"),
                                    tokid[:, tiles(i), None].to_broadcast([P, 2, TOPK * E]), ALU.mult))
                for r in range(8):
                    c(dve.tensor_scalar(ck[:, r, :], iota_c[:, :], posk[:, r // TOPK, r % TOPK:r % TOPK + 1], None,
                                        ALU.is_equal))
                c.end()

            def add_slots(i, s):
                hold(dve, (ix2, i.at(1, 1)), *free(ia2, i))
                dve.tensor_tensor(idxf[:, :], bank(1)[:, 2 * E:3 * E], idxf[:, :], ALU.add).then_inc(ia2, 1)

            dve.wait_ge(c_w2, 16 * 11)
            dve.wait_ge(tg_ok, 1)
            run_steps(dve, NP, [(3, add_slots), (0, o_stats), (2, route_a), (0, z), (1, x1), (0, wy), (1, xn_),
                                (2, shared), (2, route_b)])
            dve.wait_ge(ia2, NP)
            dve.tensor_copy(idxi[:, :], idxf[:, :]).then_inc(idx_ok, 1)

            def relu_h(i, s):
                hold(dve, (u3, i.at(1, 1)), *slot_free(ht3, i))
                dve.tensor_scalar(hr[:, s, 0, :], bank(3)[:, 0:2 * P], 0.0, None, ALU.max).then_inc(hr3, 1)

            def copy_y(i, s):
                st = landed_before(yst[s], i, s)
                hold(dve, (yd3, i.at(1, 1)), *st)
                dve.tensor_copy(yr[:, s, :, :], bank(s, 2, D)).then_inc(yc3, 1)

            dve.wait_ge(wq_s, 1)
            dve.tensor_scalar(wmean[:, :], bank(6)[:, 0:3], 1.0 / (I * D), Q_EPS, ALU.mult, ALU.max).then_inc(wq_r, 1)
            dve.wait_ge(wq_r, 1)
            dve.reciprocal(winv[:, :], wmean[:, :]).then_inc(wq_r, 1)
            dve.wait_ge(wq_r, 2)

            def ternary(i, s):
                n = K * I // NG
                cols = bass.ds(i.at(n), n)
                v = wraw[:, :, cols]
                c = Chain(wqs, i, 3)
                c(dve.tensor_tensor(v, v, winv[:, :, None].to_broadcast([P, 3, n]), ALU.mult))
                c.sync()
                c(dve.tensor_scalar(v, v, ROUND, ROUND + 1.0, ALU.add, ALU.min))
                c.sync()
                c(dve.tensor_scalar(q_w[:, :, cols], v, ROUND - 1.0, ROUND, ALU.max, ALU.subtract))
                c.end()

            run_steps(dve, NG, [(1, relu_h), (0, ternary), (2, copy_y)])

            def combine(i, s):
                c = Chain(c4, i, 12)
                hold(dve, *[(gin[s][t], i.at(8 * TOPK, 16 * TOPK - 8 * TOPK * s)) for t in range(2)])
                for k in range(TOPK):
                    for t in range(2):
                        w = wk_all[:, bass.ds(i.at(2, t), 1), k:k + 1].rearrange("p a b -> p (a b)")
                        c(dve.scalar_tensor_tensor(xt(i, t), gath[:, s, t * TOPK + k, :], w, xt(i, t),
                                                   ALU.mult, ALU.add))
                    c.sync()
                stats(c, xtile(i), s, bn, mv)
                c.end()

            def x2n(i, s):
                normalise(rs4, xtile(i), s, i, mv, rs, xn4, xn, (c4, i.at(12, 12)), *slot_free(t4, i))

            def smax(i, s):
                hold(dve, (sc4, i.at(1, 1)), *slot_free(x34, i, 9))
                dve.tensor_reduce(smx[:, s, :], bank(5)[:, 0:2 * P].rearrange("p (t m) -> p t m", t=2), AX.X, ALU.max)\
                   .then_inc(mx4, 1)
                hold(dve, (mx4, i.at(2, 1)))
                dve.tensor_scalar(nmx[:, s, :], smx[:, s, :], -SM_SCALE, None, ALU.mult).then_inc(mx4, 1)

            def x3(i, s):
                hold(dve, (ex4, i.at(1, 1)))
                c = Chain(x34, i, 9)
                c(dve.tensor_scalar(prt[:, s, :], smx[:, s, :], NEG / 2, None, ALU.is_gt))
                c(dve.reciprocal(prec[:, s, :], psumr[:, s, :]))
                c.sync()
                c(dve.scalar_tensor_tensor(prt[:, s, :], prt[:, s, :], tg[:, 1:2], prec[:, s, :], ALU.mult, ALU.mult))
                c.sync()
                hold(dve, (ro4, i.at(1, 1)))
                for t in range(2):
                    c(dve.scalar_tensor_tensor(xt(i, t), bank(6, 2, D)[:, t, :], prt[:, s, t:t + 1], xt(i, t),
                                               ALU.mult, ALU.add))
                c.sync()
                stats(c, xtile(i), s, bnx, mvx)
                c.end()

            def quant(i, s):
                hold(dve, (rs5, i.at(2, 2)), (x34, i.at(9, 9)), *slot_free(t5, i), *slot_free(hd, i, 2))
                c = Chain(q5, i, QQ)
                for t in range(2):
                    c(dve.tensor_scalar(x3n[:, s, t, :], xt(i, t), mvx[:, s, t, 0:1], rsx[:, s, t:t + 1],
                                        ALU.subtract, ALU.mult))
                c.sync()
                c(dve.tensor_reduce(amx[:, s, :], x3n[:, s, :, :], AX.X, ALU.max, apply_absolute_value=True))
                c.sync()
                c(dve.tensor_scalar(dq[:, s, :], amx[:, s, :], Q_EPS, 1.0 / 127.0, ALU.max, ALU.mult))
                c.sync()
                c(dve.reciprocal(qs[:, s, :], dq[:, s, :]))
                c(dve.tensor_scalar(cgs[:, s, :], dq[:, s, :], wmean[:, 0:1], None, ALU.mult))
                c(dve.tensor_scalar(cus[:, s, :], dq[:, s, :], wmean[:, 1:2], None, ALU.mult))
                c.sync()
                for t in range(2):
                    c(dve.tensor_scalar(xq[:, s, t, :], x3n[:, s, t, :], qs[:, s, t:t + 1], ROUND, ALU.mult, ALU.add))
                c.end()

            def h_(t):
                def stage(i, s):
                    hold(dve, (sl, i.at(2, t + 1)), *free(ssd, i, 2, t - 1))
                    dve.scalar_tensor_tensor(hh[:, t, :].rearrange("p (b n) -> p b n", b=2), psum[:, 2:4, :],
                                             cus[:, s, t:t + 1], sg[:, t, :].rearrange("p (b n) -> p b n", b=2),
                                             ALU.mult, ALU.mult).then_inc(hd, 1)
                return stage

            def hw_(t):
                def stage(i, s):
                    hold(dve, (hd, i.at(2, t + 1)))
                    dve.tensor_tensor(hw[:, t, :], hh[:, t, :], lnw[:, :], ALU.mult).then_inc(hwd, 1)
                    hold(dve, (hwd, i.at(4, 2 * t + 1)))
                    dve.tensor_reduce(ham[:, t, :], hw[:, t, :], AX.X, ALU.max, apply_absolute_value=True)\
                       .then_inc(hwd, 1)
                return stage

            def hquant(t):
                def stage(i, s):
                    hold(dve, (rr, i.at(2, t + 1)), (hwd, i.at(4, 2 * t + 2)))
                    dve.tensor_scalar(hs1[:, t, 0:1], ham[:, t, :], rq[:, t, :], Q_EPS, ALU.mult, ALU.max)\
                       .then_inc(hqs[t], 1)
                    hold(dve, (hqs[t], i.at(4, 1)))
                    dve.tensor_scalar(hs1[:, t, 1:2], hs1[:, t, 0:1], 1.0 / 127.0, None, ALU.mult).then_inc(hqs[t], 1)
                    hold(dve, (hqs[t], i.at(4, 2)))
                    dve.reciprocal(hs1[:, t, 2:3], hs1[:, t, 1:2]).then_inc(hqs[t], 1)
                    hold(dve, (hqs[t], i.at(4, 3)))
                    dve.tensor_scalar(hs1[:, t, 3:4], hs1[:, t, 2:3], rq[:, t, :], None, ALU.mult).then_inc(hqs[t], 1)
                    hold(dve, (hqs[t], i.at(4, 4)))
                    dve.tensor_scalar(hq[:, t, :], hw[:, t, :], hs1[:, t, 3:4], ROUND, ALU.mult, ALU.add)\
                       .then_inc(hqd, 1)
                return stage

            def final(t):
                def stage(i, s):
                    dve.tensor_scalar(hs1[:, t, 0:1], hs1[:, t, 1:2], wmean[:, 2:3], tg[:, 3:4], ALU.mult, ALU.mult)\
                       .then_inc(fsc, 1)
                    hold(dve, (dwn, i.at(2, t + 1)), (fsc, i.at(2, t + 1)))
                    dve.scalar_tensor_tensor(xt(i, t), bank(t)[:, 0:D], hs1[:, t, 0:1], xt(i, t),
                                             ALU.mult, ALU.add).then_inc(fo, 1)
                return stage

            dve.wait_ge(c_lnw, 16)
            run_steps(dve, NP, [
                (0, combine), (2, h_(0)), (2, hw_(0)), (0, x2n), (2, h_(1)), (2, hquant(0)), (2, hw_(1)), (0, smax),
                (1, x3), (2, hquant(1)), (1, quant), (2, final(0)), (2, final(1))])


def decay_masks():
    gam = (1.0 - 2.0 ** (-5.0 - np.arange(H, dtype=np.float32))).astype(np.float32)
    idx = np.arange(S, dtype=np.float32)
    expo = idx[None, :] - idx[:, None]
    d = np.where(expo[None] <= 0, gam[:, None, None] ** np.minimum(expo, 0)[None], np.float32(0)).astype(np.float32)
    d = d / np.sqrt(d.sum(axis=-1))[:, None, :]
    return np.ascontiguousarray((d / np.sqrt(np.float32(HD))).astype(np.float32).transpose(1, 0, 2))


def kernel(**inputs):
    import concourse.bacc as _bacc
    import ml_dtypes
    from concourse.bass_utils import run_bass_kernel_spmd as _run

    v = {k: np.asarray(w) for k, w in inputs.items()}

    def cont(w):
        return np.ascontiguousarray(w)

    def blocks(w, rows=P):
        return cont(w.reshape(-1, rows, w.shape[-1]).transpose(1, 0, 2))

    feeds = {
        "x": cont(v["x"].reshape(T, D)),
        "ctx": cont(v["ctx_2048"].reshape(T, D)),
        "ctxT": cont(v["ctx_2048"].reshape(T, D).T),
        "mask": cont(v["mask_BxS2_bk0"].reshape(NT, 2, S).transpose(1, 0, 2)).view(np.int32),
        "gates": cont(np.concatenate([v["g_xattn"], v["g_ffn"]])[None]),
        "wh": cont(v["L0_xattn_Wh"].transpose(1, 0, 2)),
        "whT": cont(v["L0_xattn_Wh"].transpose(2, 0, 1)),
        "wg": blocks(v["L0_xattn_wg_w"]),
        "wo": blocks(v["L0_xattn_wo_w"]),
        "gnp": cont(np.stack([v["L0_xattn_gn_gamma"].reshape(K, P), v["L0_xattn_gn_beta"].reshape(K, P)])
                    .transpose(2, 0, 1)),
        "gateT": blocks(cont(v["L0_ffn_gate_w"].T)),
        "bias": cont(v["L0_ffn_bias_corr"][None]),
        "upT": cont(v["L0_ffn_up_w"].reshape(E, P, K, P).transpose(3, 0, 2, 1)),
        "dnT": cont(v["L0_ffn_down_w"].transpose(2, 0, 1)),
        "shup": blocks(cont(v["L0_ffn_shared_up_w"].T)),
        "shdn": blocks(cont(v["L0_ffn_shared_down_w"].T)),
        "w_gate": blocks(cont(v["L1_ffn_w_gate"].T)).reshape(P, K * I),
        "w_up": blocks(cont(v["L1_ffn_w_up"].T)).reshape(P, K * I),
        "w_down": blocks(cont(v["L1_ffn_w_down"].T)).reshape(P, K * I),
        "lnw": cont(v["L1_ffn_ln_weight"][None]),
        "c_ident": np.eye(P, dtype=np.float32),
        "c_dn": decay_masks(),
        "c_tri": np.triu(np.ones((P, P), np.float32), 1).astype(ml_dtypes.bfloat16),
        "c_iota_c": np.tile(np.arange(P, dtype=np.float16), (P, 1)),
        "c_iota_e": np.tile(np.arange(E, dtype=np.float32), (P, 1)),
        "c_tokid": (np.arange(NT)[None, :] * P + np.arange(P)[:, None]).astype(np.float32),
    }
    nc = _bacc.Bacc("TRN2", target_bir_lowering=False, num_devices=1)
    arrays, aps = {}, {}
    for name, w in feeds.items():
        arrays[f"in_{name}_dram"] = w
        aps[name] = nc.dram_tensor(f"in_{name}_dram", w.shape, mybir.dt.from_np(w.dtype), kind="ExternalInput").ap()
    out = nc.dram_tensor("out_0_dram", (T, D), F32, kind="ExternalOutput").ap()
    build(nc, aps, out)
    r = _run(nc, [arrays], core_ids=[0])
    return r.results[0]["out_0_dram"].reshape(B, S, D)
```

```python
from contextlib import ExitStack

import concourse.bass as bass
import numpy as np
from concourse import mybir

F32 = mybir.dt.float32
F16 = mybir.dt.float16
BF16 = mybir.dt.bfloat16
U32 = mybir.dt.uint32
I32 = mybir.dt.int32
U8 = mybir.dt.uint8
ALU = mybir.AluOpType
ACT = mybir.ActivationFunctionType
AX = mybir.AxisListType

P = 128
B, S, D = 32, 64, 256
T = B * S
NT = T // P
NP = NT // 2
K = D // P
H, HD = 2, 128
E, G, TOPG, TOPK, CAP = 32, 8, 4, 4, 128
HS = 512
NHS = HS // P
I = 1024
NI = I // P
NG = E // 2
ROUTE_SCALE = 2.5
GN_EPS, LN_EPS, RMS_EPS, Q_EPS = 1e-3, 1e-5, 1e-6, 1e-5
ROUND = 1.5 * 2.0 ** 23
NEG = -1.6e31
SM_SCALE = 1.0 / 16.0
RA, RA_MASK = 29, 22
RB = 17


class Item:

    def __init__(self, c, j=None):
        self.c, self.j, self.slot = c, j, c % 2

    def at(self, per=1, plus=0):
        if self.j is None:
            return self.c * per + plus
        assert self.c * per + plus >= 0
        return self.j * (2 * per) + (self.c * per + plus)

    def below(self, n):
        return self.j is None and self.c < n


def run_steps(eng, n, stages):
    top = max(lag for lag, _ in stages)
    first = top + 2
    turns = max(0, (n - first) // 2)

    def step(t):
        for lag, stage in stages:
            if 0 <= t - lag < n:
                stage(Item(t - lag), (t - lag) % 2)

    for t in range(first):
        step(t)
    if turns:
        with eng.Fori(0, turns) as j:
            for k in range(2):
                for lag, stage in stages:
                    stage(Item(first + k - lag, j), (first + k - lag) % 2)
    for t in range(first + 2 * turns, n + top):
        step(t)


def slot_free(done, i, per=1):
    return [] if i.below(2) else [(done, i.at(per, -per))]


def free(done, i, per=1, plus=0):
    return [] if i.below(1) else [(done, i.at(per, plus))]


def landed(i, s):
    return i.at(8, 16 - 8 * s)


def landed_before(done, i, s):
    return [] if i.below(2) else [(done, i.at(8, -8 * s))]


def build(nc, a, out):
    with ExitStack() as ctx:
        def sb(name, shape, dt=F32):
            return ctx.enter_context(nc.sbuf_tensor(name, shape, dt))

        def sem(name):
            return ctx.enter_context(nc.semaphore(name))

        psum = ctx.enter_context(nc.psum_tensor("psum", [P, 8, 512], F32))

        xn_dram = nc.dram_tensor("xn_dram", (T, D), F32, kind="Internal").ap()
        ye_dram = nc.dram_tensor("ye_dram", (E * CAP, D), F32, kind="Internal").ap()

        ident = sb("ident", [P, P])
        dn = sb("dn", [S, H, S])
        tri = sb("tri", [P, P], BF16)
        ones = sb("ones", [P, P], BF16)
        onesf = sb("onesf", [P, P])
        iota_c = sb("iota_c", [P, P], F16)
        iota_e = sb("iota_e", [P, E])
        tokid = sb("tokid", [P, NT])
        sel = sb("sel", [2, P], BF16)
        mhalf = sb("mhalf", [P, 4])
        mround = sb("mround", [P, 1])
        mone = sb("mone", [P, 2])
        wh = sb("wh", [P, H, HD])
        whT = sb("whT", [P, H, HD])
        gram = sb("gram", [P, H, HD])
        wg = sb("wg", [P, K, D])
        wo = sb("wo", [P, K, D])
        gnp = sb("gnp", [P, 2, K])
        gateT = sb("gateT", [P, K, E])
        biasc = sb("biasc", [P, E])
        shup = sb("shup", [P, K, HS])
        shdn = sb("shdn", [P, NHS, D])
        upT = sb("upT", [P, E, K, P])
        dnT = sb("dnT", [P, E, D])
        gates = sb("gates", [P, 4])
        tg = sb("tg", [P, 4])
        q_w = sb("q_w", [P, 3, K * I], BF16)
        wabs = sb("wabs", [P, 4])
        wmean = sb("wmean", [P, 3])
        winv = sb("winv", [P, 3])
        wdown = sb("wdown", [P, 1])
        table = sb("table", [P, 1])
        msk = sb("msk", [2, NT, S // 4], I32)
        msk8 = msk[:, :, :].bitcast(U8)

        x_all = sb("x_all", [P, NT, D])
        ctx_all = sb("ctx_all", [P, NT, D])
        ctxT_all = sb("ctxT_all", [P, K, T])
        big = sb("big", [P, 2, NT * D])
        v_all = big[:, 0, :].rearrange("p (n d) -> p n d", n=NT)
        xhT_all = big[:, 1, :].rearrange("p (k t) -> p k t", k=K)
        gath = big[:, 0, :].rearrange("p (s r d) -> p s r d", s=2, r=8)
        wraw = big[:, :, :].rearrange("p a n -> p (a n)")[:, 2 * NT * D - 3 * K * I:].rearrange("p (w n) -> p w n", w=3)

        bn = sb("bn", [P, 2, 2, 6])
        mv = sb("mv", [P, 2, 2, 2])
        ve = sb("ve", [P, 2, 2])
        rs = sb("rs", [P, 2, 2])
        bnx = sb("bnx", [P, 2, 2, 6])
        mvx = sb("mvx", [P, 2, 2, 2])
        vex = sb("vex", [P, 2, 2])
        rsx = sb("rsx", [P, 2, 2])
        xn = sb("xn", [P, 2, 2, D])
        xnT = sb("xnT", [P, 2, K, 2 * P])
        zr = sb("zr", [P, 2, 2, D])
        tr = sb("tr", [P, 2, K, 2 * P])
        wyT = tr
        rh = sb("rh", [P, 2, NHS * 2 * P])
        cring = rh[:, :, 0:K * 2 * P].rearrange("p s (k t) -> p s k t", k=K)
        ptr = wyT
        amat = tr[0:S, 0, :, 0:2 * S]
        bda = sb("bda", [P, H, P])
        lgt = sb("lgt", [P, 2 * E])
        sig = sb("sig", [P, 2, E])
        sc = sb("sc", [P, 2, E])
        psm = sb("psm", [P, 2 * G, 6])
        gs = sb("gs", [P, 2 * G])
        m8 = sb("m8", [P, 2, 8])
        i8 = sb("i8", [P, 2, 8], U32)
        gif = sb("gif", [P, 2, TOPG])
        eqg = sb("eqg", [P, 2, G, TOPG])
        gm = sb("gm", [P, 2 * G])
        msc = sb("msc", [P, 2, E])
        eif = sb("eif", [P, 2, TOPK])
        oh = wh[:, :, :].rearrange("p h (k e) -> p h k e", k=TOPK)
        mm = sb("mm", [P, 2, E], BF16)
        mcum = sb("mcum", [P, E], BF16)
        wsel = whT[:, :, :].rearrange("p h (k e) -> p h k e", k=TOPK)
        w4 = sb("w4", [P, 2, TOPK])
        wden = sb("wden", [P, 2, 1])
        wrec = sb("wrec", [P, 2, 1])
        wn = sb("wn", [P, 2, TOPK])
        posk = sb("posk", [P, 2, TOPK])
        vald = sb("vald", [P, 2, TOPK])
        dst = sb("dst", [P, 2, TOPK])
        ck = sb("ck", [P, 8, P], F16)
        te = gram[:, 0, :].bitcast(F16).rearrange("p (t n) -> p t n", t=2)
        idxf = sb("idxf", [P, E])
        idxi = sb("idxi", [P, E], I32)
        tix = sb("tix", [P, 2, 2], I32)
        rix = sb("rix", [P, 2, 2 * TOPK], I32)
        wk_all = sb("wk_all", [P, NT, TOPK])
        dst_all = sb("dst_all", [P, NT, TOPK], I32)

        xe = xn
        xeT = xnT
        hr = zr
        h2T = tr
        yr = rh[:, :, 0:2 * D].rearrange("p s (t d) -> p s t d", t=2)

        smx = sb("smx", [P, 2, 2])
        nmx = sb("nmx", [P, 2, 2])
        pexp = rh[:, 0, 0:4 * P].rearrange("p (s t m) -> p s t m", s=2, t=2)
        psumr = sb("psumr", [P, 2, 2])
        prec = sb("prec", [P, 2, 2])
        prt = sb("prt", [P, 2, 2])
        pT = rh[:, 1, 0:4 * P].rearrange("p (s m) -> p s m", s=2)
        x3n = zr
        amx = sb("amx", [P, 2, 2])
        qc = sb("qc", [P, 2, 2])
        qs = sb("qs", [P, 2, 2])
        cgs = sb("cgs", [P, 2, 2])
        cus = sb("cus", [P, 2, 2])
        xq = tr
        xqT = rh[:, 0, 4 * P:8 * P].bitcast(BF16).rearrange("p (s k t) -> p s k t", s=2, k=K)
        upf = upT[:, :, :, :].rearrange("p e k h -> p (e k h)")
        sg = upf[:, 0:2048].rearrange("p (s i) -> p s i", s=2)
        hh = upf[:, 2048:4096].rearrange("p (s i) -> p s i", s=2)
        hw = upf[:, 4096:6144].rearrange("p (s i) -> p s i", s=2)
        sqj = upf[:, 6144:7168]
        lnw = upf[:, 7168:8192]
        dnf = dnT[:, :, :].rearrange("p e d -> p (e d)")
        hq = dnf[:, 2048:4096].rearrange("p (s i) -> p s i", s=2)
        hqT = dnf[:, 0:1024].bitcast(BF16).rearrange("p (s i) -> p s i", s=2)
        mnegb = shup[0:2, :, :].rearrange("p k n -> p (k n)").bitcast(BF16).rearrange("p (n a m) -> p n a m", n=NT, a=2)
        sst = sb("sst", [P, 2, 1])
        msq = sb("msq", [P, 2, 1])
        rq = sb("rq", [P, 2, 1])
        ham = sb("ham", [P, 2, 1])
        hs1 = sb("hs1", [P, 2, 4])

        c_in = sem("consts_in")
        c_x = [sem(f"x_in{i}") for i in range(2)]
        c_cr = [sem(f"ctxT_ring_in{i}") for i in range(2)]
        c_ctx = sem("ctx_in")
        c_w2 = sem("phase2_weights_in")
        c_w3 = sem("expert_weights_in")
        c_w4 = sem("ffn_weights_in")
        c_lnw = sem("ln_weight_in")
        tixs, rixs, wqs = sem("token_index"), sem("row_index"), sem("ternary_steps")
        hss = [sem(f"h_scale_steps{t}") for t in range(2)]
        rws, xsc, tbl = sem("read_weight"), sem("x_scale_steps"), sem("table_loads")
        half_ok = sem("half_ok")
        gates_in, tg_ok = sem("gates_in"), sem("tanh_of_gates")
        gram_ps, gram_sb = sem("gram_ps"), sem("gram_sb")
        st1, rs1, xh1 = sem("stats1"), sem("rstd1"), sem("normed1")
        t1, xhT1 = sem("transposed1"), sem("xhT_copied")
        pt1, ptc1 = sem("proj1"), sem("proj_copied")
        v1, vc1 = sem("values"), sem("values_copied")
        s1 = sem("scores1")
        am, at, bd = sem("a_matrix"), sem("a_transposed"), sem("a_blocks")
        o2, sto, rso, z2 = sem("o_ready"), sem("o_stats"), sem("o_rstd"), sem("z_ready")
        w2, zt2, aff, wy2 = sem("w_ready"), sem("z_transposed"), sem("z_scaled"), sem("wy_ready")
        y2, x2, rs2, xn2 = sem("y_ready"), sem("x1_stats"), sem("x1_rstd"), sem("xn_ready")
        xnst = [sem(f"xn_stored{i}") for i in range(2)]
        t2, xnT2 = sem("xn_transposed"), sem("xnT_copied")
        lg2, su2, lt2, rl2, sq2 = sem("logits"), sem("shared_up"), sem("tanh_logits"), sem("shared_relu"), sem("shared_sq")
        sd2, sa2 = sem("shared_down"), sem("shared_added")
        ra, pos2, rb, ix2, ia2 = sem("route_a"), sem("positions"), sem("route_b"), sem("slots_ready"), sem("slots_added")
        idx_ok = sem("indices_ready")
        xg = [sem(f"tokens_gathered{i}") for i in range(4)]
        t3, xeT3, u3, hr3 = sem("xe_transposed"), sem("xeT_copied"), sem("h_ready"), sem("h_relu")
        ht3, h23, yd3, yc3 = sem("h_transposed"), sem("h_squared"), sem("ye_ready"), sem("ye_copied")
        yst = [sem(f"ye_stored{i}") for i in range(2)]
        gin = [[sem(f"rows_gathered{i}_{r}") for r in range(2)] for i in range(2)]
        c4, rs4, xn4 = sem("combined"), sem("x2_rstd"), sem("x2_normed")
        t4, xT4, sc4, mx4, ex4 = sem("x2_transposed"), sem("x2T_copied"), sem("scores4"), sem("scores_max"), sem("exp_done")
        pt4, pc4, ro4, x34 = sem("p_transposed"), sem("pT_copied"), sem("read_out"), sem("x3_stats")
        rs5, qa5, q5, t5, qT5 = sem("x3_rstd"), sem("x3_absmax"), sem("x3_quant"), sem("xq_transposed"), sem("xqT_copied")
        ga, gu, sl, hd, ssd = sem("gate_ready"), sem("up_ready"), sem("silu_done"), sem("h_done"), sem("h_sumsq")
        hwd, hqd = sem("hw_done"), sem("h_quant")
        ht, hc, dwn, fo = sem("hq_transposed"), sem("hqT_copied"), sem("down_ready"), sem("x4_ready")
        wq_a, wq_s, wq_r, wq_g = sem("w_abs"), sem("w_total"), sem("w_scale"), sem("w_quant")
        mask_in, mk = sem("mask_in"), sem("mask_ready")
        ost = [sem(f"out_stored{i}") for i in range(2)]

        wait_values = {e.engine: [e.alloc_register(f"wait_value{n}") for n in range(4)]
                       for e in (nc.scalar, nc.vector, nc.gpsimd)}

        def hold(eng, *waits):
            waits = [(s, v) for s, v in waits if not isinstance(v, int) or v > 0]
            if eng.engine in wait_values and any(not isinstance(v, int) for _, v in waits):
                regs = iter(wait_values[eng.engine])
                values = []
                for _, v in waits:
                    if not isinstance(v, int):
                        reg = next(regs)
                        eng.reg_mov(reg, v)
                        v = reg
                    values.append(v)
                eng.wait_ge(half_ok, 1)
                waits = [(s, v) for (s, _), v in zip(waits, values)]
            for s, v in waits:
                eng.wait_ge(s, v)

        def tiles(i, n=2):
            return bass.ds(i.at(2), n)

        def tok(i):
            return bass.ds(i.at(2 * P), 2 * P)

        def xt(i, t):
            return x_all[:, bass.ds(i.at(2, t), 1), :].rearrange("p a d -> p (a d)")

        def bank(b, *shape):
            v = psum[:, b, :]
            if len(shape) == 2:
                return v.rearrange("p (a b) -> p a b", a=shape[0])
            return v

        block = ctx.enter_context(nc.Block())

        @block.sync
        def _(sp):
            for name, t in (("whT", whT), ("wh", wh)):
                sp.dma_start(t[:, :, :], a[name]).then_inc(c_in, 16)
            sp.dma_start(ident[:, :], a["c_ident"]).then_inc(c_in, 16)
            sp.dma_start(dn[:, :, :], a["c_dn"]).then_inc(c_in, 16)
            xv = a["x"].rearrange("(n p) d -> p n d", p=P)
            cv = a["ctx"].rearrange("(n p) d -> p n d", p=P)
            ctv = a["ctxT"].rearrange("(k p) t -> p k t", p=P)

            for i in range(2):
                sp.dma_start(x_all[:, tiles(Item(i)), :], xv[:, tiles(Item(i)), :]).then_inc(c_x[i], 16)
            with sp.Fori(0, (NP - 2) // 2) as j:
                for k in range(2):
                    i = Item(2 + k, j)
                    hold(sp, (c_x[k], i.at(8, -8 * k)))
                    sp.dma_start(x_all[:, tiles(i), :], xv[:, tiles(i), :]).then_inc(c_x[k], 16)
            sp.wait_ge(v1, NP // 2)
            for name, t in (("wg", wg), ("wo", wo), ("gateT", gateT), ("shup", shup), ("shdn", shdn), ("gnp", gnp)):
                sp.dma_start(t[:, :, :], a[name]).then_inc(c_w2, 16)
            for name, t in (("c_tri", tri), ("c_iota_c", iota_c), ("c_iota_e", iota_e), ("c_tokid", tokid)):
                sp.dma_start(t[:, :], a[name]).then_inc(c_w2, 16)
            sp.dma_start(biasc[:, :], a["bias"].to_broadcast([P, E])).then_inc(c_w2, 16)
            sp.wait_ge(v1, NP)
            sp.dma_start(upT[:, :, :, :], a["upT"]).then_inc(c_w3, 16)
            sp.dma_start(dnT[:, :, :], a["dnT"]).then_inc(c_w3, 16)
            sp.dma_start(ctx_all[:, :, :], cv).then_inc(c_ctx, 16)
            sp.dma_start(ctxT_all[:, :, :], ctv).then_inc(c_ctx, 16)

            xnv = xn_dram.rearrange("(n p) d -> p n d", p=P)

            def store_xn(i, s):
                hold(sp, (xn2, i.at(2, 2)))
                sp.dma_start(xnv[:, tiles(i), :], xn[:, s, :, :]).then_inc(xnst[s], 16)

            run_steps(sp, NP - 1, [(0, store_xn)])
            sp.wait_ge(o2, NP)
            sp.wait_ge(w2, NP)
            for n, name in enumerate(("w_gate", "w_up", "w_down")):
                sp.dma_start(wraw[:, n, :], a[name]).then_inc(c_w4, 16)
            store_xn(Item(NP - 1), (NP - 1) % 2)

            yev = ye_dram.rearrange("(e c) d -> c e d", c=CAP)

            def store_ye(i, s):
                hold(sp, (yc3, i.at(1, 1)))
                sp.dma_start(yev[:, tiles(i), :], yr[:, s, :, :]).then_inc(yst[s], 16)

            run_steps(sp, NG, [(0, store_ye)])

            sp.wait_ge(yc3, NG)
            sp.dma_start(lnw, a["lnw"].to_broadcast([P, I])).then_inc(c_lnw, 16)
            ov = out.rearrange("(n p) d -> p n d", p=P)

            def store_out(i, s):
                hold(sp, (fo, i.at(2, 2)))
                sp.dma_start(ov[:, tiles(i), :], x_all[:, tiles(i), :]).then_inc(ost[s], 16)

            run_steps(sp, NP, [(0, store_out)])
            for s in range(2):
                sp.wait_ge(ost[s], 16 * NP // 2)

        @block.gpsimd
        def _(pl):
            pl.memset(mhalf[:, :], -0.5).then_inc(half_ok, 1)
            pl.dma_start(gates[:, :], a["gates"].to_broadcast([P, 4])).then_inc(gates_in, 16)
            pl.dma_start(msk[:, :, :], a["mask"]).then_inc(mask_in, 16)
            pl.memset(ones[:, :], 1.0)
            pl.memset(onesf[:, :], 1.0)
            pl.memset(mround[:, :], -ROUND)
            pl.memset(mone[:, :], -1.0)
            pl.memset(mcum[:, :], 0.0)
            pl.memset(idxf[:, :], 0.0)
            pl.memset(bda[:, :, :], 0.0)
            pl.memset(sel[:, :], 1.0).then_inc(half_ok, 1)
            pl.wait_ge(half_ok, 2)
            pl.affine_select(out=sel[:, :], in_=sel[:, :], compare_op=ALU.is_ge, fill=0.0, base=0,
                             pattern=[[1, P]], channel_multiplier=-S).then_inc(half_ok, 1)
            pl.wait_ge(half_ok, 3)
            pl.affine_select(out=sel[:, :], in_=sel[:, :], compare_op=ALU.is_ge, fill=0.0, base=S - 1,
                             pattern=[[-1, P]], channel_multiplier=S).then_inc(half_ok, 1)

            def rstd(stats, val, mvb, veb, rsb, eps, done):
                def stage(i, s):
                    hold(pl, (stats, val(i)))
                    pl.tensor_scalar(veb[:, s, :], mvb[:, s, :, 1], eps, None, ALU.add).then_inc(done, 1)
                    hold(pl, (done, i.at(2, 1)))
                    pl.tensor_tensor(rsb[:, s, :], veb[:, s, :], mhalf[:, 0:2], ALU.pow).then_inc(done, 1)
                return stage

            run_steps(pl, NP, [(0, rstd(st1, lambda i: i.at(4, 4), mv, ve, rs, LN_EPS, rs1))])

            def square_shared(i, s):
                hold(pl, (rl2, i.at(1, 1)))
                pl.tensor_tensor(rh[:, s, :], rh[:, s, :], rh[:, s, :], ALU.mult).then_inc(sq2, 1)

            run_steps(pl, NP, [
                (0, rstd(sto, lambda i: i.at(4, 4), mv, ve, rs, GN_EPS, rso)),
                (2, square_shared),
                (1, rstd(x2, lambda i: i.at(5, 5), mvx, vex, rsx, LN_EPS, rs2))])

            pl.wait_ge(su2, NP)
            pl.wait_ge(mask_in, 16)
            for b in range(2):
                ins = pl.tensor_scalar(mnegb[:, :, b, :], msk8[:, :, :], -1.0, -NEG, ALU.add, ALU.mult)
            ins.then_inc(mk, 1)
            pl.wait_ge(mk, 1)
            pl.affine_select(out=mnegb, in_=mnegb, compare_op=ALU.is_equal, fill=NEG, base=0,
                             pattern=[[0, NT], [-1, 2], [0, S]], channel_multiplier=1).then_inc(mk, 1)

            for s in range(2):
                pl.wait_ge(xnst[s], 16 * NP // 2)
            pl.wait_ge(idx_ok, 1)

            def gather_tokens(i, s):
                hold(pl, *slot_free(t3, i))
                pl.tensor_copy(tix[:, s, :], idxi[:, tiles(i)]).then_inc(tixs, 1)
                hold(pl, (tixs, i.at(1, 1)))
                for k in range(2):
                    pl.indirect_dma_start(out=xe[:, s, k, :], out_offset=None, in_=xn_dram[:, :],
                                          in_offset=bass.IndirectOffsetOnAxis(ap=tix[:, s, k:k + 1], axis=0),
                                          bounds_check=T - 1, oob_is_err=False).then_inc(xg[2 * s + k], 16)

            run_steps(pl, NG, [(0, gather_tokens)])

            pl.wait_ge(wqs, 3 * NG)
            for s in range(2):
                pl.wait_ge(yst[s], 16 * NG // 2)

            def rows(part):
                def stage(i, s):
                    if part == 0:
                        hold(pl, *slot_free(c4, i, 12))
                        pl.tensor_copy(rix[:, s, :], dst_all[:, tiles(i), :].rearrange("p t k -> p (t k)"))\
                          .then_inc(rixs, 1)
                        hold(pl, (rixs, i.at(1, 1)))
                    for r in range(2 * part, 2 * part + 2):
                        pl.indirect_dma_start(
                            out=gath[:, s, r, :], out_offset=None, in_=ye_dram[:, :],
                            in_offset=bass.IndirectOffsetOnAxis(ap=rix[:, s, r:r + 1], axis=0),
                            bounds_check=E * CAP - 1, oob_is_err=False).then_inc(gin[s][r // TOPK], 16)
                return stage

            def read_weight(i, s):
                hold(pl, (ex4, i.at(1, 1)))
                pl.tensor_scalar(prt[:, s, :], smx[:, s, :], NEG / 2, tg[:, 1:2], ALU.is_gt, ALU.mult).then_inc(rws, 1)
                pl.tensor_tensor(prec[:, s, :], psumr[:, s, :], mone[:, :], ALU.pow).then_inc(rws, 1)
                hold(pl, (rws, i.at(3, 2)))
                pl.tensor_tensor(prt[:, s, :], prt[:, s, :], prec[:, s, :], ALU.mult).then_inc(rws, 1)

            def x_scale(i, s):
                hold(pl, (qa5, i.at(3, 3)), *slot_free(hd, i, 2))
                pl.tensor_scalar(qc[:, s, :], amx[:, s, :], Q_EPS, 1.0 / 127.0, ALU.max, ALU.mult).then_inc(xsc, 1)
                hold(pl, (xsc, i.at(4, 1)))
                pl.tensor_tensor(qs[:, s, :], qc[:, s, :], mone[:, :], ALU.pow).then_inc(xsc, 1)
                pl.tensor_scalar(cgs[:, s, :], qc[:, s, :], wmean[:, 0:1], None, ALU.mult).then_inc(xsc, 1)
                pl.tensor_scalar(cus[:, s, :], qc[:, s, :], wmean[:, 1:2], None, ALU.mult).then_inc(xsc, 1)

            def h_scale(t):
                def stage(i, s):
                    def step(n):
                        hold(pl, (hss[t], i.at(6, n)))

                    hold(pl, (ssd, i.at(2, t + 1)), (hwd, i.at(4, 2 * t + 2)), *free(fo, i, 2, t - 1))
                    pl.tensor_scalar(msq[:, t, :], sst[:, t, :], 1.0 / I, RMS_EPS, ALU.mult, ALU.add)\
                      .then_inc(hss[t], 1)
                    step(1)
                    pl.tensor_tensor(rq[:, t, :], msq[:, t, :], mhalf[:, 0:1], ALU.pow).then_inc(hss[t], 1)
                    step(2)
                    pl.tensor_scalar(hs1[:, t, 0:1], ham[:, t, :], rq[:, t, :], Q_EPS, ALU.mult, ALU.max)\
                      .then_inc(hss[t], 1)
                    step(3)
                    pl.tensor_tensor(hs1[:, t, 1:2], hs1[:, t, 0:1], mone[:, 0:1], ALU.pow).then_inc(hss[t], 1)
                    step(4)
                    pl.tensor_scalar(hs1[:, t, 2:3], hs1[:, t, 1:2], rq[:, t, :], 127.0, ALU.mult, ALU.mult).then_inc(hss[t], 1)
                    pl.tensor_tensor(hs1[:, t, 3:4], hs1[:, t, 0:1], wdown[:, :], ALU.mult).then_inc(hss[t], 1)
                return stage

            pl.wait_ge(wq_r, 3)
            pl.wait_ge(tg_ok, 1)
            run_steps(pl, NP, [
                (0, rows(0)), (0, rows(1)), (1, rstd(c4, lambda i: i.at(12, 12), mv, ve, rs, LN_EPS, rs4)),
                (0, rows(2)), (0, rows(3)), (2, h_scale(0)), (1, read_weight), (2, h_scale(1)),
                (1, rstd(x34, lambda i: i.at(6, 6), mvx, vex, rsx, LN_EPS, rs5)), (1, x_scale)])

        @block.scalar
        def _(act):
            def copy_to(dst_ap, src, done, func=ACT.Copy, **kw):
                return act.activation(dst_ap, src, func, **kw).then_inc(done, 1)

            ring = a["ctxT"].rearrange("(k p) t -> p k t", p=P)

            def load_ring(i, s):
                hold(act, *slot_free(s1, i))
                act.dma_start(cring[:, s, :, :], ring[:, :, tok(i)]).then_inc(c_cr[s], 16)

            load_ring(Item(0), 0)
            act.wait_ge(gates_in, 16)
            act.activation(tg[:, :], gates[:, :], ACT.Tanh).then_inc(tg_ok, 1)
            act.wait_ge(gram_ps, 1)
            act.activation(gram[:, :, :], bank(0)[:, 0:H * HD].rearrange("p (h e) -> p h e", h=H), ACT.Copy)\
               .then_inc(gram_sb, 1)

            def p1_v(i, s):
                hold(act, (v1, i.at(1, 1)))
                copy_to(v_all[:, tiles(i), :], bank(1, 2, D), vc1)

            def p1_t(i, s):
                hold(act, (t1, i.at(1, 1)))
                copy_to(xhT_all[:, :, tok(i)], bank(2, K, 2 * P), xhT1)

            def load_ring_next(i, s):
                if not i.below(2):
                    load_ring(i, s)

            load_ring(Item(1), 1)
            run_steps(act, NP, [(1, p1_t), (2, p1_v), (0, load_ring_next)])

            def affine(i, s):
                hold(act, (zt2, i.at(1, 1)), *slot_free(wy2, i))
                for k in range(K):
                    ins = act.activation(tr[:, s, k, :], bank(2, K, 2 * P)[:, k, :], ACT.Identity,
                                         scale=gnp[:, 0, k:k + 1], bias=gnp[:, 1, k:k + 1])
                ins.then_inc(aff, 1)

            def copy_xnT(i, s):
                hold(act, (t2, i.at(1, 1)), *slot_free(su2, i))
                copy_to(xnT[:, s, :, :], bank(2, K, 2 * P), xnT2)

            def tanh_logits(i, s):
                hold(act, (lg2, i.at(1, 1)), *free(ra, i, RA))
                copy_to(lgt[:, :], bank(5)[:, 0:2 * E], lt2, ACT.Tanh, scale=0.5)

            def relu_shared(i, s):
                hold(act, (su2, i.at(1, 1)), *slot_free(sd2, i))
                copy_to(rh[:, s, :].rearrange("p (b n) -> p b n", b=2), psum[:, 6:8, :], rl2, ACT.Relu)

            act.wait_ge(c_w2, 16 * 11)
            run_steps(act, NP, [(0, affine), (1, copy_xnT), (1, tanh_logits), (1, relu_shared)])

            def copy_xeT(i, s):
                hold(act, (t3, i.at(1, 1)), *slot_free(u3, i))
                copy_to(xeT[:, s, :, :], bank(2, K, 2 * P), xeT3)

            def square_h(i, s):
                hold(act, (ht3, i.at(1, 1)), *slot_free(yd3, i))
                copy_to(h2T[:, s, 0, :], bank(4)[:, 0:2 * P], h23, ACT.Square)

            act.wait_ge(c_w4, 48)
            for n in range(3):
                act.activation(q_w[:, n, :], wraw[:, n, :], ACT.Abs, accum_out=wabs[:, n:n + 1]).then_inc(wq_a, 1)

            run_steps(act, NG, [(0, copy_xeT), (1, square_h)])

            def copy_x2T(i, s):
                hold(act, (t4, i.at(1, 1)), *slot_free(sc4, i))
                copy_to(xnT[:, s, :, :], bank(4, K, 2 * P), xT4)

            def exps(i, s):
                hold(act, (mx4, i.at(2, 2)), *slot_free(pt4, i))
                for t in range(2):
                    ins = act.activation(pexp[:, s, t, :], bank(5)[:, t * P:(t + 1) * P], ACT.Exp, scale=SM_SCALE,
                                         bias=nmx[:, s, t:t + 1], accum_out=psumr[:, s, t:t + 1])
                ins.then_inc(ex4, 1)

            def copy_pT(i, s):
                hold(act, (pt4, i.at(1, 1)), *slot_free(ro4, i))
                copy_to(pT[:, s, :], bank(4)[:, 0:2 * P], pc4)

            def copy_xqT(i, s):
                hold(act, (t5, i.at(1, 1)), *slot_free(gu, i, 2))
                copy_to(xqT[:, s, :, :], bank(4, K, 2 * P), qT5, ACT.Identity, bias=mround[:, :])

            def silu(t):
                def stage(i, s):
                    hold(act, (ga, i.at(2, t + 1)), *free(hd, i, 2, t - 1))
                    act.activation(sg[:, t, :].rearrange("p (b n) -> p b n", b=2), psum[:, 0:2, :], ACT.Silu,
                                   scale=cgs[:, s, t:t + 1]).then_inc(sl, 1)
                return stage

            def sumsq(t):
                def stage(i, s):
                    hold(act, (hd, i.at(2, t + 1)), *([] if i.below(1) and t == 0 else [(ssd, i.at(2, t))]),
                         *free(hss[t], i, 6, -5))
                    act.activation(sqj, hh[:, t, :], ACT.Square, accum_out=sst[:, t, :]).then_inc(ssd, 1)
                return stage

            def copy_hqT(t, b):
                def stage(i, s):
                    hold(act, (ht, i.at(4, 2 * t + b + 1)), *free(dwn, i, 2, t - 1))
                    copy_to(hqT[:, t, b * 512:(b + 1) * 512], bank(7), hc, ACT.Identity, bias=mround[:, :])
                return stage

            def load_table(func, n):
                def stage(i, s):
                    if not (i.below(1) and n == 0):
                        hold(act, (tbl, i.at(2, n)))
                    act.activation(table[:, :], mround[:, :], func).then_inc(tbl, 1)
                return stage

            run_steps(act, NP, [
                (1, copy_xqT), (1, silu(0)), (1, sumsq(0)), (0, copy_x2T), (1, silu(1)), (1, load_table(ACT.Exp, 0)),
                (0, exps), (2, copy_hqT(1, 0)), (2, copy_hqT(1, 1)), (0, copy_pT), (1, sumsq(1)),
                (1, copy_hqT(0, 0)), (1, copy_hqT(0, 1)), (1, load_table(ACT.Silu, 1))])

        @block.tensor
        def _(pe):
            def mm_(o, l, r, first=True, last=True):
                return pe.matmul(o, l, r, start=first, stop=last, skip_group_check=True)

            pe.wait_ge(half_ok, 4)
            pe.wait_ge(c_in, 16 * 4)
            for h in range(H):
                ins = mm_(bank(0)[:, h * HD:(h + 1) * HD], whT[:, h, :], whT[:, h, :])
            ins.then_inc(gram_ps, 1)
            for h in range(H):
                mm_(bank(3)[0:S, h * S:(h + 1) * S], bda[:, h, 0:S], bda[:, h, 0:S], h == 0, False)

            def p1_v(i, s):
                n16 = landed(i, s)
                hold(pe, (c_cr[s], n16), *free(vc1, i))
                for t in range(2):
                    for h in range(H):
                        ins = mm_(bank(1, 2, D)[:, t, h * HD:(h + 1) * HD],
                                  cring[:, s, h, t * P:(t + 1) * P], wh[:, h, :])
                ins.then_inc(v1, 1)

            def p1_t(i, s):
                hold(pe, (xh1, i.at(2, 2)), *free(xhT1, i))
                for t in range(2):
                    for k in range(K):
                        ins = pe.transpose(bank(2, K, 2 * P)[:, k, t * P:(t + 1) * P],
                                           xn[:, s, t, k * P:(k + 1) * P], ident[:, :])
                ins.then_inc(t1, 1)

            def p1_p(i, s):
                hold(pe, (xhT1, i.at(1, 1)), *free(ptc1, i))
                for h in range(H):
                    ins = mm_(bank(0, H, 2 * P)[:, h, :], gram[:, h, :], xhT_all[:, h, tok(i)])
                ins.then_inc(pt1, 1)

            def p1_s(i, s):
                hold(pe, (ptc1, i.at(1, 1)))
                for b in range(4):
                    for h in range(H):
                        ins = mm_(bank(3)[0:S, h * S:(h + 1) * S], ptr[:, s, h, b * S:(b + 1) * S],
                                  cring[:, s, h, b * S:(b + 1) * S], False, False)
                ins.then_inc(s1, 1)

            pe.wait_ge(gram_sb, 1)
            run_steps(pe, NP, [(0, p1_t), (1, p1_v), (0, p1_p), (1, p1_s)])
            pe.wait_ge(am, 4)
            for h in range(H):
                ins = pe.transpose(bank(4)[:, h * S:(h + 1) * S], amat[:, h, :], ident[0:S, 0:S])
            ins.then_inc(at, 1)

            def p2_o(i, s):
                hold(pe, *free(z2, i, 2))
                for h in range(H):
                    ins = mm_(bank(0, 2, D)[:, :, h * HD:(h + 1) * HD], bda[:, h, :],
                              v_all[:, tiles(i), h * HD:(h + 1) * HD])
                ins.then_inc(o2, 1)

            def p2_w(i, s):
                hold(pe, *free(wy2, i))
                for j in range(K):
                    for k in range(K):
                        ins = mm_(bank(3, K, 2 * P)[:, j, :], wg[:, k, j * P:(j + 1) * P], xhT_all[:, k, tok(i)],
                                  k == 0, k == K - 1)
                ins.then_inc(w2, 1)

            def p2_zt(i, s):
                hold(pe, (z2, i.at(2, 2)), *slot_free(xnT2, i))
                for t in range(2):
                    for k in range(K):
                        ins = pe.transpose(bank(2, K, 2 * P)[:, k, t * P:(t + 1) * P],
                                           zr[:, s, t, k * P:(k + 1) * P], ident[:, :])
                ins.then_inc(zt2, 1)

            def p2_y(i, s):
                hold(pe, (wy2, i.at(1, 1)), *slot_free(sa2, i))
                for t in range(2):
                    for k in range(K):
                        ins = mm_(bank(4, 2, D)[:, t, :], wyT[:, s, k, t * P:(t + 1) * P], wo[:, k, :],
                                  k == 0, k == K - 1)
                ins.then_inc(y2, 1)

            def p2_xt(i, s):
                last = i.j is None and i.c == NP - 1
                hold(pe, (xn2, i.at(2, 2)), (aff, i.at(1, 1 if last else 2)))
                for t in range(2):
                    for k in range(K):
                        ins = pe.transpose(bank(2, K, 2 * P)[:, k, t * P:(t + 1) * P],
                                           xn[:, s, t, k * P:(k + 1) * P], ident[:, :])
                ins.then_inc(t2, 1)

            def p2_lg(i, s):
                hold(pe, (xnT2, i.at(1, 1)), *free(lt2, i))
                for t in range(2):
                    for k in range(K):
                        ins = mm_(bank(5)[:, t * E:(t + 1) * E], xnT[:, s, k, t * P:(t + 1) * P], gateT[:, k, :],
                                  k == 0, k == K - 1)
                ins.then_inc(lg2, 1)

            def p2_su(i, s):
                hold(pe, *free(rl2, i))
                for n in range(NHS):
                    for k in range(K):
                        ins = mm_(psum[:, 6 + n // 2, (n % 2) * 256:(n % 2) * 256 + 256],
                                  shup[:, k, n * P:(n + 1) * P], xnT[:, s, k, :], k == 0, k == K - 1)
                ins.then_inc(su2, 1)

            def p2_sd(i, s):
                last = i.j is None and i.c == NP - 1
                hold(pe, (sq2, i.at(1, 1)), (x2, i.at(5, 1 if last else 6)))
                for t in range(2):
                    for n in range(NHS):
                        ins = mm_(bank(4, 2, D)[:, t, :],
                                  rh[:, s, n * 256 + t * P:n * 256 + (t + 1) * P],
                                  shdn[:, n, :], n == 0, n == NHS - 1)
                ins.then_inc(sd2, 1)

            def p2_pos(i, s):
                hold(pe, (ra, i.at(RA, RA_MASK)), *free(rb, i, RB), *free(ia2, i))
                pos = bank(1)[:, 0:2 * E]
                mm_(pos[:, 0:E], tri[:, :], mm[:, 0, :], True, False)
                mm_(pos[:, 0:E], ones[:, :], mcum[:, :], False, True)
                mm_(pos[:, E:2 * E], tri[:, :], mm[:, 1, :], True, False)
                mm_(pos[:, E:2 * E], ones[:, :], mm[:, 0, :], False, False)
                mm_(pos[:, E:2 * E], ones[:, :], mcum[:, :], False, True).then_inc(pos2, 1)

            def p2_ix(i, s):
                hold(pe, (rb, i.at(RB, RB)), *free(ia2, i))
                for r in range(8):
                    ins = mm_(bank(1)[:, 2 * E:3 * E], ck[:, r, :], te[:, r // TOPK, (r % TOPK) * E:(r % TOPK + 1) * E],
                              r == 0, r == 7)
                ins.then_inc(ix2, 1)

            pe.wait_ge(c_w2, 16 * 11)
            pe.wait_ge(bd, 2 * H)
            pe.wait_ge(vc1, NP)
            run_steps(pe, NP, [(0, p2_o), (3, p2_sd), (2, p2_xt), (2, p2_lg), (2, p2_su), (3, p2_ix), (0, p2_w),
                               (1, p2_y), (2, p2_pos), (0, p2_zt)])

            def p3_t(i, s):
                n16 = landed(i, s)
                hold(pe, (xg[2 * s], n16), (xg[2 * s + 1], n16), *free(xeT3, i))
                for e in range(2):
                    for k in range(K):
                        ins = pe.transpose(bank(2, K, 2 * P)[:, k, e * P:(e + 1) * P],
                                           xe[:, s, e, k * P:(k + 1) * P], ident[:, :])
                ins.then_inc(t3, 1)

            def p3_u(i, s):
                hold(pe, (xeT3, i.at(1, 1)), *free(hr3, i))
                for e in range(2):
                    for k in range(K):
                        w = upT[:, bass.ds(i.at(2, e), 1), k, :]
                        ins = mm_(bank(3)[:, e * P:(e + 1) * P], xeT[:, s, k, e * P:(e + 1) * P],
                                  w.rearrange("p a h -> p (a h)"), k == 0, k == K - 1)
                ins.then_inc(u3, 1)

            def p3_ht(i, s):
                hold(pe, (hr3, i.at(1, 1)), *free(h23, i))
                for e in range(2):
                    ins = pe.transpose(bank(4)[:, e * P:(e + 1) * P], hr[:, s, 0, e * P:(e + 1) * P], ident[:, :])
                ins.then_inc(ht3, 1)

            def p3_d(i, s):
                hold(pe, (h23, i.at(1, 1)), *slot_free(yc3, i))
                for e in range(2):
                    w = dnT[:, bass.ds(i.at(2, e), 1), :]
                    ins = mm_(bank(s, 2, D)[:, e, :], h2T[:, s, 0, e * P:(e + 1) * P],
                              w.rearrange("p a d -> p (a d)"))
                ins.then_inc(yd3, 1)

            pe.wait_ge(wq_a, 3)
            mm_(bank(6)[:, 0:3], onesf[:, :], wabs[:, 0:3]).then_inc(wq_s, 1)
            pe.wait_ge(c_w3, 32)
            run_steps(pe, NG, [(0, p3_t), (1, p3_u), (2, p3_d), (1, p3_ht)])

            def x2t(i, s):
                hold(pe, (xn4, i.at(2, 2)), *free(qT5, i))
                for t in range(2):
                    for k in range(K):
                        ins = pe.transpose(bank(4, K, 2 * P)[:, k, t * P:(t + 1) * P],
                                           xn[:, s, t, k * P:(k + 1) * P], ident[:, :])
                ins.then_inc(t4, 1)

            def score(i, s):
                hold(pe, (xT4, i.at(1, 1)), *free(ex4, i))
                for t in range(2):
                    o = bank(5)[:, t * P:(t + 1) * P]
                    mm_(o, sel[:, :], mnegb[:, bass.ds(i.at(2, t), 1), :, :].rearrange("p n a m -> p (n a m)"),
                        True, False)
                    for k in range(K):
                        ins = mm_(o, xnT[:, s, k, t * P:(t + 1) * P],
                                  ctxT_all[:, k, bass.ds(i.at(2 * P, t * P), P)], False, k == K - 1)
                ins.then_inc(sc4, 1)

            def pt(i, s):
                hold(pe, (ex4, i.at(1, 1)), (xT4, i.at(1, 1)))
                for t in range(2):
                    ins = pe.transpose(bank(4)[:, t * P:(t + 1) * P], pexp[:, s, t, :], ident[:, :])
                ins.then_inc(pt4, 1)

            def read(i, s):
                hold(pe, (pc4, i.at(1, 1)), *free(x34, i, 6, -4))
                for t in range(2):
                    ins = mm_(bank(6, 2, D)[:, t, :], pT[:, s, t * P:(t + 1) * P],
                              ctx_all[:, bass.ds(i.at(2, t), 1), :].rearrange("p a d -> p (a d)"))
                ins.then_inc(ro4, 1)

            def xqt(i, s):
                hold(pe, (q5, i.at(2, 2)), (pc4, i.at(1, 1)))
                for t in range(2):
                    for k in range(K):
                        ins = pe.transpose(bank(4, K, 2 * P)[:, k, t * P:(t + 1) * P],
                                           xq[:, s, t, k * P:(k + 1) * P], ident[:, :])
                ins.then_inc(t5, 1)

            def project(w, t):
                def stage(i, s):
                    if w == 0:
                        hold(pe, (qT5, i.at(1, 1)), *([] if i.below(1) and t == 0 else [(sl, i.at(2, t))]),
                             *(free(fo, i, 2, -1) if t == 0 else []))
                    else:
                        hold(pe, (qT5, i.at(1, 1)), *([] if i.below(1) and t == 0 else [(hd, i.at(2, t))]))
                    for b in range(2):
                        for k in range(K):
                            ins = mm_(psum[:, 2 * w + b, :], xqT[:, s, k, t * P:(t + 1) * P],
                                      q_w[:, w, k * I + b * 512:k * I + (b + 1) * 512], k == 0, k == K - 1)
                    ins.then_inc(gu if w else ga, 1)
                return stage

            def hqt(t, b):
                def stage(i, s):
                    first = i.below(1) and t == 0 and b == 0
                    hold(pe, (hqd, i.at(2, t + 1)), *([] if first else [(hc, i.at(4, 2 * t + b))]))
                    for c in range(4):
                        ins = pe.transpose(bank(7)[:, c * P:(c + 1) * P],
                                           hq[:, t, (4 * b + c) * P:(4 * b + c + 1) * P], ident[:, :])
                    ins.then_inc(ht, 1)
                return stage

            def down(t):
                def stage(i, s):
                    last = i.j is None and i.c == NP - 1
                    hold(pe, (hc, i.at(4, 2 * t + 2)), (sl, i.at(2, 4 if t and not last else 2)),
                         *free(fo, i, 2, t - 1))
                    for c in range(NI):
                        ins = mm_(bank(t)[:, 0:D], hqT[:, t, c * P:(c + 1) * P],
                                  q_w[:, 2, c * D:(c + 1) * D], c == 0, c == NI - 1)
                    ins.then_inc(dwn, 1)
                return stage

            pe.wait_ge(c_ctx, 32)
            pe.wait_ge(mk, 2)
            pe.wait_ge(wqs, 3 * NG)
            run_steps(pe, NP, [
                (1, xqt), (1, project(0, 0)), (1, project(1, 0)), (1, project(0, 1)), (1, project(1, 1)), (0, x2t), (0, score), (2, hqt(1, 0)), (2, hqt(1, 1)),
                (0, pt), (2, down(1)), (0, read), (1, hqt(0, 0)), (1, hqt(0, 1)), (1, down(0))])

        @block.vector
        def _(dve):
            class Chain:

                def __init__(self, s_, i, per, n=0):
                    self.s, self.i, self.per, self.n = s_, i, per, n

                def __call__(self, ins):
                    self.n += 1
                    return ins.then_inc(self.s, 1)

                def sync(self, but=0):
                    hold(dve, (self.s, self.i.at(self.per, self.n - but)))

                def end(self):
                    assert self.n == self.per, (self.n, self.per)

            def stats(c, src, s, bnb, mvb):
                for t in range(2):
                    c(dve.bn_stats(bnb[:, s, t, :], src(t)))
                for t in range(2):
                    c.sync(1 - t)
                    c(dve.bn_aggr(mvb[:, s, t, :], bnb[:, s, t, :]))

            dve.wait_ge(half_ok, 1)

            def p1_stats(i, s):
                n16 = landed(i, s)
                hold(dve, (c_x[s], n16))
                c = Chain(st1, i, 4)
                stats(c, lambda t: xt(i, t), s, bn, mv)
                c.end()

            def normalise(rsem, src, s, i, mvb, rsb, done, dest, *waits):
                hold(dve, (rsem, i.at(2, 2)), *waits)
                for t in range(2):
                    dve.tensor_scalar(dest[:, s, t, :], src(t), mvb[:, s, t, 0:1], rsb[:, s, t:t + 1],
                                      ALU.subtract, ALU.mult).then_inc(done, 1)

            def xtile(i):
                return lambda t: xt(i, t)

            def p1_norm(i, s):
                normalise(rs1, xtile(i), s, i, mv, rs, xh1, xn, (st1, i.at(4, 4)), *slot_free(t1, i))

            def p1_pt(i, s):
                hold(dve, (pt1, i.at(1, 1)), *slot_free(s1, i))
                dve.tensor_copy(ptr[:, s, :, :], bank(0, H, 2 * P)).then_inc(ptc1, 1)

            run_steps(dve, NP, [(0, p1_stats), (1, p1_pt), (0, p1_norm)])

            dve.wait_ge(s1, NP)
            dve.tensor_tensor(amat[:, :, 0:S], bank(3)[0:S, 0:H * S].rearrange("p (h t) -> p h t", h=H),
                              dn[:, :, :], ALU.mult).then_inc(am, 1)
            dve.wait_ge(am, 1)
            dve.scalar_tensor_tensor(amat[:, :, S:2 * S], amat[:, :, 0:S], -1.0, amat[:, :, 0:S],
                                     ALU.mult, ALU.max).then_inc(am, 1)
            dve.wait_ge(am, 2)
            dve.tensor_scalar(amat[:, :, 0:S], amat[:, :, S:2 * S], 1.0, None, ALU.max).then_inc(am, 1)
            dve.wait_ge(am, 3)
            dve.tensor_copy(amat[:, :, S:2 * S], amat[:, :, 0:S]).then_inc(am, 1)
            dve.wait_ge(at, 1)
            dve.wait_ge(half_ok, 2)
            for h in range(H):
                for b in range(2):
                    dve.tensor_copy(bda[b * S:(b + 1) * S, h, b * S:(b + 1) * S],
                                    bank(4)[b * S:(b + 1) * S, h * S:(h + 1) * S]).then_inc(bd, 1)

            def o_stats(i, s):
                hold(dve, (o2, i.at(1, 1)))
                c = Chain(sto, i, 4)
                stats(c, lambda t: bank(0, 2, D)[:, t, :], s, bn, mv)
                c.end()

            def z(i, s):
                normalise(rso, lambda t: bank(0, 2, D)[:, t, :], s, i, mv, rs, z2, zr, (sto, i.at(4, 4)), *slot_free(zt2, i))

            def wy(i, s):
                hold(dve, (aff, i.at(1, 1)), (w2, i.at(1, 1)), *slot_free(y2, i))
                dve.scalar_tensor_tensor(wyT[:, s, :, :], bank(3, K, 2 * P), 0.0, tr[:, s, :, :],
                                         ALU.max, ALU.mult).then_inc(wy2, 1)

            def x1(i, s):
                hold(dve, (y2, i.at(1, 1)))
                c = Chain(x2, i, 5)
                c(dve.scalar_tensor_tensor(x_all[:, tiles(i), :], bank(4, 2, D), tg[:, 0:1], x_all[:, tiles(i), :],
                                           ALU.mult, ALU.add))
                c.sync()
                stats(c, xtile(i), s, bnx, mvx)
                c.end()

            def xn_(i, s):
                st = landed_before(xnst[s], i, s)
                normalise(rs2, xtile(i), s, i, mvx, rsx, xn2, xn, (x2, i.at(5, 5)), *slot_free(t2, i), *st)

            def shared(i, s):
                hold(dve, (sd2, i.at(1, 1)))
                dve.scalar_tensor_tensor(x_all[:, tiles(i), :], bank(4, 2, D), tg[:, 2:3], x_all[:, tiles(i), :],
                                         ALU.mult, ALU.add).then_inc(sa2, 1)

            def route_a1(i, s):
                hold(dve, (lt2, i.at(1, 1)))
                c = Chain(ra, i, RA)
                c(dve.tensor_scalar(sig[:, :, :], lgt[:, :].rearrange("p (t e) -> p t e", t=2), 0.5, 0.5,
                                    ALU.mult, ALU.add))
                c.sync()
                c(dve.tensor_tensor(sc[:, :, :], sig[:, :, :], biasc[:, None, :].to_broadcast([P, 2, E]), ALU.add))
                c.sync()
                v = sc[:, :, :].rearrange("p t (g m) -> p (t g) m", g=G)
                c(dve.tensor_tensor(psm[:, :, 0:2], v[:, :, 0:4:2], v[:, :, 1:4:2], ALU.add))
                c(dve.tensor_tensor(psm[:, :, 2:4], v[:, :, 0:2], v[:, :, 2:4], ALU.add))
                c(dve.tensor_tensor(psm[:, :, 4:5], v[:, :, 0:1], v[:, :, 3:4], ALU.add))
                c(dve.tensor_tensor(psm[:, :, 5:6], v[:, :, 1:2], v[:, :, 2:3], ALU.add))

            def route_a2(i, s):
                c = Chain(ra, i, RA, 6)
                c.sync()
                c(dve.tensor_reduce(gs[:, :], psm[:, :, :], AX.X, ALU.max))
                c.sync()
                for t in range(2):
                    c(dve.max(m8[:, t, :], gs[:, t * G:(t + 1) * G]))
                c.sync()
                for t in range(2):
                    c(dve.max_index(i8[:, t, :], m8[:, t, :], gs[:, t * G:(t + 1) * G]))
                c.sync()
                c(dve.tensor_copy(gif[:, :, :], i8[:, :, 0:TOPG]))

            def route_a3(i, s):
                v = sc[:, :, :].rearrange("p t (g m) -> p (t g) m", g=G)
                c = Chain(ra, i, RA, 12)
                c.sync()
                c(dve.tensor_tensor(eqg[:, :, :, :], iota_e[:, None, 0:G, None].to_broadcast([P, 2, G, TOPG]),
                                    gif[:, :, None, :].to_broadcast([P, 2, G, TOPG]), ALU.is_equal))
                c.sync()
                c(dve.tensor_reduce(gm[:, :], eqg[:, :, :, :].rearrange("p t g k -> p (t g) k"), AX.X, ALU.add))
                c.sync()
                c(dve.tensor_tensor(msc[:, :, :].rearrange("p t (g m) -> p (t g) m", g=G), v,
                                    gm[:, :, None].to_broadcast([P, 2 * G, E // G]), ALU.mult))
                c.sync()
                for t in range(2):
                    c(dve.max(m8[:, t, :], msc[:, t, :]))
                c.sync()
                for t in range(2):
                    c(dve.max_index(i8[:, t, :], m8[:, t, :], msc[:, t, :]))
                c.sync()
                c(dve.tensor_copy(eif[:, :, :], i8[:, :, 0:TOPK]))

            def route_a4(i, s):
                c = Chain(ra, i, RA, 20)
                c.sync()
                c(dve.tensor_tensor(oh[:, :, :, :], iota_e[:, None, None, :].to_broadcast([P, 2, TOPK, E]),
                                    eif[:, :, :, None].to_broadcast([P, 2, TOPK, E]), ALU.is_equal))
                c.sync()
                with nc.allow_low_precision(reason="sums of at most one 1"):
                    c(dve.tensor_reduce(mm[:, :, :], oh[:, :, :, :].rearrange("p t k e -> p t e k"), AX.X, ALU.add))
                assert c.n == RA_MASK, c.n
                c(dve.tensor_tensor(wsel[:, :, :, :], oh[:, :, :, :],
                                    sig[:, :, None, :].to_broadcast([P, 2, TOPK, E]), ALU.mult))
                c.sync()
                c(dve.tensor_reduce(w4[:, :, :], wsel[:, :, :, :], AX.X, ALU.add))
                c.sync()
                c(dve.tensor_reduce(wden[:, :, 0], w4[:, :, :], AX.X, ALU.add))
                c.sync()
                c(dve.tensor_scalar(wden[:, :, :], wden[:, :, :], 1e-20, None, ALU.add))
                c.sync()
                c(dve.reciprocal(wrec[:, :, :], wden[:, :, :]))
                c.sync()
                c(dve.tensor_tensor(wn[:, :, :], w4[:, :, :], wrec[:, :, :].to_broadcast([P, 2, TOPK]), ALU.mult))
                c.sync()
                c(dve.tensor_scalar(wn[:, :, :], wn[:, :, :], tg[:, 2:3], ROUTE_SCALE, ALU.mult, ALU.mult))
                c.end()

            def route_b1(i, s):
                hold(dve, (pos2, i.at(1, 1)), (ra, i.at(RA, RA)), *free(ix2, i))
                c = Chain(rb, i, RB)
                pos = bank(1)[:, 0:2 * E].rearrange("p (t e) -> p t e", t=2)
                c(dve.tensor_tensor(wsel[:, :, :, :], oh[:, :, :, :],
                                    pos[:, :, None, :].to_broadcast([P, 2, TOPK, E]), ALU.mult))
                c(dve.tensor_tensor(mcum[:, :], mcum[:, :], mm[:, 0, :], ALU.add))
                c.sync()
                c(dve.tensor_tensor(mcum[:, :], mcum[:, :], mm[:, 1, :], ALU.add))
                c(dve.tensor_reduce(posk[:, :, :], wsel[:, :, :, :], AX.X, ALU.add))

            def route_b2(i, s):
                c = Chain(rb, i, RB, 4)
                c.sync()
                c(dve.tensor_scalar(vald[:, :, :], posk[:, :, :], float(CAP), None, ALU.is_lt))
                c(dve.tensor_scalar(dst[:, :, :], posk[:, :, :], float(CAP - 1), None, ALU.min))
                c.sync()
                c(dve.tensor_tensor(wk_all[:, tiles(i), :], wn[:, :, :], vald[:, :, :], ALU.mult))
                c(dve.scalar_tensor_tensor(dst_all[:, tiles(i), :], eif[:, :, :], float(CAP), dst[:, :, :],
                                           ALU.mult, ALU.add))
                c(dve.tensor_tensor(te[:, :, :], oh[:, :, :, :].rearrange("p t k e -> p t (k e)"),
                                    tokid[:, tiles(i), None].to_broadcast([P, 2, TOPK * E]), ALU.mult))
                for r in range(8):
                    c(dve.tensor_scalar(ck[:, r, :], iota_c[:, :], posk[:, r // TOPK, r % TOPK:r % TOPK + 1], None,
                                        ALU.is_equal))
                c.end()

            def add_slots(i, s):
                hold(dve, (ix2, i.at(1, 1)), *free(ia2, i))
                dve.tensor_tensor(idxf[:, :], bank(1)[:, 2 * E:3 * E], idxf[:, :], ALU.add).then_inc(ia2, 1)

            dve.wait_ge(c_w2, 16 * 11)
            dve.wait_ge(tg_ok, 1)
            run_steps(dve, NP, [(0, o_stats), (2, route_a1), (2, route_a2), (2, route_a3), (2, route_a4), (3, add_slots), (0, z),
                                (1, x1), (0, wy), (1, xn_), (2, route_b1), (2, route_b2), (2, shared)])
            dve.wait_ge(ia2, NP)
            dve.tensor_copy(idxi[:, :], idxf[:, :]).then_inc(idx_ok, 1)

            def relu_h(i, s):
                hold(dve, (u3, i.at(1, 1)), *slot_free(ht3, i))
                dve.tensor_scalar(hr[:, s, 0, :], bank(3)[:, 0:2 * P], 0.0, None, ALU.max).then_inc(hr3, 1)

            def copy_y(i, s):
                st = landed_before(yst[s], i, s)
                hold(dve, (yd3, i.at(1, 1)), *st)
                dve.tensor_copy(yr[:, s, :, :], bank(s, 2, D)).then_inc(yc3, 1)

            dve.wait_ge(wq_s, 1)
            dve.tensor_scalar(wmean[:, :], bank(6)[:, 0:3], 1.0 / (I * D), Q_EPS, ALU.mult, ALU.max).then_inc(wq_r, 1)
            dve.wait_ge(wq_r, 1)
            dve.reciprocal(winv[:, :], wmean[:, :]).then_inc(wq_r, 1)
            dve.tensor_scalar(wdown[:, :], wmean[:, 2:3], 1.0 / 127.0, tg[:, 3:4], ALU.mult, ALU.mult).then_inc(wq_r, 1)
            dve.wait_ge(wq_r, 3)

            def ternary(i, s):
                n = K * I // NG
                cols = bass.ds(i.at(n), n)
                v = wraw[:, :, cols]
                c = Chain(wqs, i, 3)
                c(dve.tensor_tensor(v, v, winv[:, :, None].to_broadcast([P, 3, n]), ALU.mult))
                c.sync()
                c(dve.tensor_scalar(v, v, ROUND, ROUND + 1.0, ALU.add, ALU.min))
                c.sync()
                c(dve.tensor_scalar(q_w[:, :, cols], v, ROUND - 1.0, ROUND, ALU.max, ALU.subtract))
                c.end()

            run_steps(dve, NG, [(1, relu_h), (0, ternary), (2, copy_y)])

            def combine(i, s):
                c = Chain(c4, i, 12)
                if not i.below(1):
                    hold(dve, *[(gin[s][t], i.at(8 * TOPK, 16 * TOPK - 8 * TOPK * s)) for t in range(2)])
                order = [(k, t) for k in range(TOPK) for t in range(2)]
                for k, t in sorted(order, key=lambda kt: kt[1]) if i.below(1) else order:
                        if i.below(1) and k == 0:
                            dve.wait_ge(gin[s][t], 16 * TOPK)
                        if k > 0:
                            c.sync(0 if i.below(1) else 1)
                        w = wk_all[:, bass.ds(i.at(2, t), 1), k:k + 1].rearrange("p a b -> p (a b)")
                        c(dve.scalar_tensor_tensor(xt(i, t), gath[:, s, t * TOPK + k, :], w, xt(i, t),
                                                   ALU.mult, ALU.add))
                c.sync()
                stats(c, xtile(i), s, bn, mv)
                c.end()

            def x2n(i, s):
                normalise(rs4, xtile(i), s, i, mv, rs, xn4, xn, (c4, i.at(12, 12)), *slot_free(t4, i))

            def smax(i, s):
                hold(dve, (sc4, i.at(1, 1)), *slot_free(x34, i, 6))
                dve.tensor_reduce(smx[:, s, :], bank(5)[:, 0:2 * P].rearrange("p (t m) -> p t m", t=2), AX.X, ALU.max)\
                   .then_inc(mx4, 1)
                hold(dve, (mx4, i.at(2, 1)))
                dve.tensor_scalar(nmx[:, s, :], smx[:, s, :], -SM_SCALE, None, ALU.mult).then_inc(mx4, 1)

            def x3(i, s):
                hold(dve, (rws, i.at(3, 3)), (ro4, i.at(1, 1)))
                c = Chain(x34, i, 6)
                for t in range(2):
                    c(dve.scalar_tensor_tensor(xt(i, t), bank(6, 2, D)[:, t, :], prt[:, s, t:t + 1], xt(i, t),
                                               ALU.mult, ALU.add))
                c.sync()
                stats(c, xtile(i), s, bnx, mvx)
                c.end()

            def x3_absmax(i, s):
                hold(dve, (rs5, i.at(2, 2)), (x34, i.at(6, 6)))
                c = Chain(qa5, i, 3)
                for t in range(2):
                    c(dve.tensor_scalar(x3n[:, s, t, :], xt(i, t), mvx[:, s, t, 0:1], rsx[:, s, t:t + 1],
                                        ALU.subtract, ALU.mult))
                c.sync()
                c(dve.tensor_reduce(amx[:, s, :], x3n[:, s, :, :], AX.X, ALU.max, apply_absolute_value=True))
                c.end()

            def x3_quant(i, s):
                hold(dve, (xsc, i.at(4, 4)), *slot_free(t5, i))
                for t in range(2):
                    dve.tensor_scalar(xq[:, s, t, :], x3n[:, s, t, :], qs[:, s, t:t + 1], ROUND, ALU.mult, ALU.add)\
                       .then_inc(q5, 1)

            def h_(t):
                def stage(i, s):
                    hold(dve, (gu, i.at(2, t + 1)), (sl, i.at(2, t + 1)), *free(ssd, i, 2, t - 1))
                    dve.scalar_tensor_tensor(hh[:, t, :].rearrange("p (b n) -> p b n", b=2), psum[:, 2:4, :],
                                             cus[:, s, t:t + 1], sg[:, t, :].rearrange("p (b n) -> p b n", b=2),
                                             ALU.mult, ALU.mult).then_inc(hd, 1)
                return stage

            def hw_(t):
                def stage(i, s):
                    hold(dve, (hd, i.at(2, t + 1)))
                    dve.tensor_tensor(hw[:, t, :], hh[:, t, :], lnw[:, :], ALU.mult).then_inc(hwd, 1)
                    hold(dve, (hwd, i.at(4, 2 * t + 1)))
                    dve.tensor_reduce(ham[:, t, :], hw[:, t, :], AX.X, ALU.max, apply_absolute_value=True)\
                       .then_inc(hwd, 1)
                return stage

            def hquant(t):
                def stage(i, s):
                    hold(dve, (hss[t], i.at(6, 6)), *free(ht, i, 4, 2 * t - 2))
                    dve.tensor_scalar(hq[:, t, :], hw[:, t, :], hs1[:, t, 2:3], ROUND, ALU.mult, ALU.add)\
                       .then_inc(hqd, 1)
                return stage

            def final(t):
                def stage(i, s):
                    hold(dve, (dwn, i.at(2, t + 1)))
                    dve.scalar_tensor_tensor(xt(i, t), bank(t)[:, 0:D], hs1[:, t, 3:4], xt(i, t),
                                             ALU.mult, ALU.add).then_inc(fo, 1)
                return stage

            dve.wait_ge(c_lnw, 16)
            run_steps(dve, NP, [
                (2, final(0)), (0, combine), (1, h_(0)), (0, x2n), (1, hw_(0)), (2, hquant(1)), (0, smax),
                (1, h_(1)), (1, hw_(1)), (2, final(1)), (0, x3), (1, hquant(0)), (0, x3_absmax), (0, x3_quant)])


def decay_masks():
    gam = (1.0 - 2.0 ** (-5.0 - np.arange(H, dtype=np.float32))).astype(np.float32)
    idx = np.arange(S, dtype=np.float32)
    expo = idx[None, :] - idx[:, None]
    d = np.where(expo[None] <= 0, gam[:, None, None] ** np.minimum(expo, 0)[None], np.float32(0)).astype(np.float32)
    d = d / np.sqrt(d.sum(axis=-1))[:, None, :]
    return np.ascontiguousarray((d / np.sqrt(np.float32(HD))).astype(np.float32).transpose(1, 0, 2))


def kernel(**inputs):
    import concourse.bacc as _bacc
    import ml_dtypes
    from concourse.bass_utils import run_bass_kernel_spmd as _run

    v = {k: np.asarray(w) for k, w in inputs.items()}

    def cont(w):
        return np.ascontiguousarray(w)

    def blocks(w, rows=P):
        return cont(w.reshape(-1, rows, w.shape[-1]).transpose(1, 0, 2))

    feeds = {
        "x": cont(v["x"].reshape(T, D)),
        "ctx": cont(v["ctx_2048"].reshape(T, D)),
        "ctxT": cont(v["ctx_2048"].reshape(T, D).T),
        "mask": cont(v["mask_BxS2_bk0"].reshape(NT, 2, S).transpose(1, 0, 2)).view(np.int32),
        "gates": cont(np.concatenate([v["g_xattn"], v["g_ffn"]])[None]),
        "wh": cont(v["L0_xattn_Wh"].transpose(1, 0, 2)),
        "whT": cont(v["L0_xattn_Wh"].transpose(2, 0, 1)),
        "wg": blocks(v["L0_xattn_wg_w"]),
        "wo": blocks(v["L0_xattn_wo_w"]),
        "gnp": cont(np.stack([v["L0_xattn_gn_gamma"].reshape(K, P), v["L0_xattn_gn_beta"].reshape(K, P)])
                    .transpose(2, 0, 1)),
        "gateT": blocks(cont(v["L0_ffn_gate_w"].T)),
        "bias": cont(v["L0_ffn_bias_corr"][None]),
        "upT": cont(v["L0_ffn_up_w"].reshape(E, P, K, P).transpose(3, 0, 2, 1)),
        "dnT": cont(v["L0_ffn_down_w"].transpose(2, 0, 1)),
        "shup": blocks(cont(v["L0_ffn_shared_up_w"].T)),
        "shdn": blocks(cont(v["L0_ffn_shared_down_w"].T)),
        "w_gate": blocks(cont(v["L1_ffn_w_gate"].T)).reshape(P, K * I),
        "w_up": blocks(cont(v["L1_ffn_w_up"].T)).reshape(P, K * I),
        "w_down": blocks(cont(v["L1_ffn_w_down"].T)).reshape(P, K * I),
        "lnw": cont(v["L1_ffn_ln_weight"][None]),
        "c_ident": np.eye(P, dtype=np.float32),
        "c_dn": decay_masks(),
        "c_tri": np.triu(np.ones((P, P), np.float32), 1).astype(ml_dtypes.bfloat16),
        "c_iota_c": np.tile(np.arange(P, dtype=np.float16), (P, 1)),
        "c_iota_e": np.tile(np.arange(E, dtype=np.float32), (P, 1)),
        "c_tokid": (np.arange(NT)[None, :] * P + np.arange(P)[:, None]).astype(np.float32),
    }
    nc = _bacc.Bacc("TRN2", target_bir_lowering=False, num_devices=1)
    arrays, aps = {}, {}
    for name, w in feeds.items():
        arrays[f"in_{name}_dram"] = w
        aps[name] = nc.dram_tensor(f"in_{name}_dram", w.shape, mybir.dt.from_np(w.dtype), kind="ExternalInput").ap()
    out = nc.dram_tensor("out_0_dram", (T, D), F32, kind="ExternalOutput").ap()
    build(nc, aps, out)
    r = _run(nc, [arrays], core_ids=[0])
    return r.results[0]["out_0_dram"].reshape(B, S, D)
```

```python
from contextlib import ExitStack

import concourse.bass as bass
import numpy as np
from concourse import mybir

F32 = mybir.dt.float32
F16 = mybir.dt.float16
BF16 = mybir.dt.bfloat16
U32 = mybir.dt.uint32
I32 = mybir.dt.int32
U8 = mybir.dt.uint8
ALU = mybir.AluOpType
ACT = mybir.ActivationFunctionType
AX = mybir.AxisListType

P = 128
B, S, D = 32, 64, 256
T = B * S
NT = T // P
NP = NT // 2
K = D // P
H, HD = 2, 128
E, G, TOPG, TOPK, CAP = 32, 8, 4, 4, 128
HS = 512
NHS = HS // P
I = 1024
NI = I // P
NG = E // 2
ROUTE_SCALE = 2.5
GN_EPS, LN_EPS, RMS_EPS, Q_EPS = 1e-3, 1e-5, 1e-6, 1e-5
ROUND = 1.5 * 2.0 ** 23
NEG = -1.6e31
SM_SCALE = 1.0 / 16.0
RA, RA_MASK = 25, 22
RA_STARTS = (0, 1, 2, 6, 7, 9, 11, 12, 13, 14, 15, 17, 19, 20, 21, 23, 24)
RB = 17
RB_STARTS = (0, 2, 4, 6)


class Item:

    def __init__(self, c, j=None):
        self.c, self.j, self.slot = c, j, c % 2

    def at(self, per=1, plus=0):
        if self.j is None:
            return self.c * per + plus
        assert self.c * per + plus >= 0
        return self.j * (2 * per) + (self.c * per + plus)

    def below(self, n):
        return self.j is None and self.c < n


def run_steps(eng, n, stages):
    top = max(lag for lag, _ in stages)
    first = top + 2
    turns = max(0, (n - first) // 2)

    def step(t):
        for lag, stage in stages:
            if 0 <= t - lag < n:
                stage(Item(t - lag), (t - lag) % 2)

    for t in range(first):
        step(t)
    if turns:
        with eng.Fori(0, turns) as j:
            for k in range(2):
                for lag, stage in stages:
                    stage(Item(first + k - lag, j), (first + k - lag) % 2)
    for t in range(first + 2 * turns, n + top):
        step(t)


def slot_free(done, i, per=1):
    return [] if i.below(2) else [(done, i.at(per, -per))]


def free(done, i, per=1, plus=0):
    return [] if i.below(1) else [(done, i.at(per, plus))]


def landed(i, s):
    return i.at(8, 16 - 8 * s)


def landed_before(done, i, s):
    return [] if i.below(2) else [(done, i.at(8, -8 * s))]


def build(nc, a, out):
    with ExitStack() as ctx:
        def sb(name, shape, dt=F32):
            return ctx.enter_context(nc.sbuf_tensor(name, shape, dt))

        def sem(name):
            return ctx.enter_context(nc.semaphore(name))

        psum = ctx.enter_context(nc.psum_tensor("psum", [P, 8, 512], F32))

        xn_dram = nc.dram_tensor("xn_dram", (T, D), F32, kind="Internal").ap()
        ye_dram = nc.dram_tensor("ye_dram", (E * CAP, D), F32, kind="Internal").ap()

        ident = sb("ident", [P, P])
        dn = sb("dn", [S, H, S])
        tri = sb("tri", [P, P], BF16)
        ones = sb("ones", [P, P], BF16)
        onesf = sb("onesf", [P, P])
        iota_c = sb("iota_c", [P, P], F16)
        iota_e = sb("iota_e", [P, E])
        tokid = sb("tokid", [P, NT])
        sel = sb("sel", [2, P], BF16)
        mhalf = sb("mhalf", [P, 4])
        mround = sb("mround", [P, 1])
        mone = sb("mone", [P, 2])
        wh = sb("wh", [P, H, HD])
        whT = sb("whT", [P, H, HD])
        gram = sb("gram", [P, H, HD])
        wg = sb("wg", [P, K, D])
        wo = sb("wo", [P, K, D])
        gnp = sb("gnp", [P, 2, K])
        gateT = sb("gateT", [P, K, E])
        biasc = sb("biasc", [P, E])
        shup = sb("shup", [P, K, HS])
        shdn = sb("shdn", [P, NHS, D])
        upT = sb("upT", [P, E, K, P])
        dnT = sb("dnT", [P, E, D])
        gates = sb("gates", [P, 4])
        tg = sb("tg", [P, 4])
        q_w = sb("q_w", [P, 3, K * I], BF16)
        wabs = sb("wabs", [P, 4])
        wmean = sb("wmean", [P, 3])
        winv = sb("winv", [P, 3])
        wdown = sb("wdown", [P, 1])
        table = sb("table", [P, 1])
        msk = sb("msk", [2, NT, S // 4], I32)
        msk8 = msk[:, :, :].bitcast(U8)

        x_all = sb("x_all", [P, NT, D])
        ctx_all = sb("ctx_all", [P, NT, D])
        ctxT_all = sb("ctxT_all", [P, K, T])
        big = sb("big", [P, 2, NT * D])
        v_all = big[:, 0, :].rearrange("p (n d) -> p n d", n=NT)
        xhT_all = big[:, 1, :].rearrange("p (k t) -> p k t", k=K)
        gath = big[:, 0, :].rearrange("p (s r d) -> p s r d", s=2, r=8)
        wraw = big[:, :, :].rearrange("p a n -> p (a n)")[:, 2 * NT * D - 3 * K * I:].rearrange("p (w n) -> p w n", w=3)

        bn = sb("bn", [P, 2, 2, 6])
        mv = sb("mv", [P, 2, 2, 2])
        ve = sb("ve", [P, 2, 2])
        rs = sb("rs", [P, 2, 2])
        sh = sb("sh", [P, 2, 2])
        bnx = sb("bnx", [P, 2, 2, 6])
        mvx = sb("mvx", [P, 2, 2, 2])
        vex = sb("vex", [P, 2, 2])
        rsx = sb("rsx", [P, 2, 2])
        shx = sb("shx", [P, 2, 2])
        xn = sb("xn", [P, 2, 2, D])
        xnT = sb("xnT", [P, 2, K, 2 * P])
        zr = sb("zr", [P, 2, 2, D])
        tr = sb("tr", [P, 2, K, 2 * P])
        wyT = tr
        rh = sb("rh", [P, 2, NHS * 2 * P])
        cring = rh[:, :, 0:K * 2 * P].rearrange("p s (k t) -> p s k t", k=K)
        ptr = wyT
        amat = tr[0:S, 0, :, 0:2 * S]
        bda = sb("bda", [P, H, P])
        lgt = sb("lgt", [P, 2 * E])
        sig = sb("sig", [P, 2, E])
        sc = sb("sc", [P, 2, E])
        psm = sb("psm", [P, 2 * G, 6])
        gs = sb("gs", [P, 2 * G])
        m8 = sb("m8", [P, 2, 8])
        i8 = sb("i8", [P, 2, 8], U32)
        gif = sb("gif", [P, 2, TOPG])
        eqg = sb("eqg", [P, 2, G, TOPG])
        gm = sb("gm", [P, 2 * G])
        msc = sb("msc", [P, 2, E])
        eif = sb("eif", [P, 2, TOPK])
        oh = wh[:, :, :].rearrange("p h (k e) -> p h k e", k=TOPK)
        mm = sb("mm", [P, 2, E], BF16)
        mcum = sb("mcum", [P, E], BF16)
        wsel = whT[:, :, :].rearrange("p h (k e) -> p h k e", k=TOPK)
        w4 = sb("w4", [P, 2, TOPK])
        wden = sb("wden", [P, 2, 1])
        wrec = sb("wrec", [P, 2, 1])
        wn = sb("wn", [P, 2, TOPK])
        posk = sb("posk", [P, 2, TOPK])
        vald = sb("vald", [P, 2, TOPK])
        dst = sb("dst", [P, 2, TOPK])
        ck = sb("ck", [P, 8, P], F16)
        te = gram[:, 0, :].bitcast(F16).rearrange("p (t n) -> p t n", t=2)
        idxf = sb("idxf", [P, E])
        tix = sb("tix", [P, 2, 2], I32)
        rix = sb("rix", [P, 2, 2 * TOPK], I32)
        wk_all = sb("wk_all", [P, NT, TOPK])
        dst_all = sb("dst_all", [P, NT, TOPK], I32)

        xe = xn
        xeT = xnT
        hr = zr
        h2T = tr
        yr = rh[:, :, 0:2 * D].rearrange("p s (t d) -> p s t d", t=2)

        smx = sb("smx", [P, 2, 2])
        nmx = sb("nmx", [P, 2, 2])
        pexp = rh[:, 0, 0:4 * P].rearrange("p (s t m) -> p s t m", s=2, t=2)
        psumr = sb("psumr", [P, 2, 2])
        prec = sb("prec", [P, 2, 2])
        prt = sb("prt", [P, 2, 2])
        pT = rh[:, 1, 0:4 * P].rearrange("p (s m) -> p s m", s=2)
        x3n = zr
        amx = sb("amx", [P, 2, 2])
        qc = sb("qc", [P, 2, 2])
        qs = sb("qs", [P, 2, 2])
        cgs = sb("cgs", [P, 2, 2])
        cus = sb("cus", [P, 2, 2])
        xq = tr
        xqT = rh[:, 0, 4 * P:8 * P].bitcast(BF16).rearrange("p (s k t) -> p s k t", s=2, k=K)
        upf = upT[:, :, :, :].rearrange("p e k h -> p (e k h)")
        sg = upf[:, 0:2048].rearrange("p (s i) -> p s i", s=2)
        hh = upf[:, 2048:4096].rearrange("p (s i) -> p s i", s=2)
        hw = upf[:, 4096:6144].rearrange("p (s i) -> p s i", s=2)
        sqj = upf[:, 6144:7168]
        lnw = upf[:, 7168:8192]
        dnf = dnT[:, :, :].rearrange("p e d -> p (e d)")
        hq = dnf[:, 2048:4096].rearrange("p (s i) -> p s i", s=2)
        hqT = dnf[:, 0:1024].bitcast(BF16).rearrange("p (s i) -> p s i", s=2)
        mnegb = shup[0:2, :, :].rearrange("p k n -> p (k n)").bitcast(BF16).rearrange("p (n a m) -> p n a m", n=NT, a=2)
        sst = sb("sst", [P, 2, 1])
        msq = sb("msq", [P, 2, 1])
        rq = sb("rq", [P, 2, 1])
        ham = sb("ham", [P, 2, 1])
        hs1 = sb("hs1", [P, 2, 4])

        c_in = sem("consts_in")
        c_x = [sem(f"x_in{i}") for i in range(2)]
        c_cr = [sem(f"ctxT_ring_in{i}") for i in range(2)]
        c_ctx = sem("ctx_in")
        c_w2 = sem("phase2_weights_in")
        c_w3 = sem("expert_weights_in")
        c_w4 = sem("ffn_weights_in")
        c_lnw = sem("ln_weight_in")
        tixs = [sem(f"token_index{e}") for e in range(2)]
        wns, rixs, wqs = sem("route_weight_steps"), sem("row_index"), sem("ternary_steps")
        hss = [sem(f"h_scale_steps{t}") for t in range(2)]
        rws, xsc, tbl = sem("read_weight"), sem("x_scale_steps"), sem("table_loads")
        half_ok = sem("half_ok")
        gates_in, tg_ok = sem("gates_in"), sem("tanh_of_gates")
        gram_ps, gram_sb = sem("gram_ps"), sem("gram_sb")
        st1, rs1, xh1 = sem("stats1"), sem("rstd1"), sem("normed1")
        t1, xhT1 = sem("transposed1"), sem("xhT_copied")
        pt1, ptc1 = sem("proj1"), sem("proj_copied")
        v1, vc1 = sem("values"), sem("values_copied")
        s1 = sem("scores1")
        am, at, bd = sem("a_matrix"), sem("a_transposed"), sem("a_blocks")
        o2, sto, rso, z2 = sem("o_ready"), sem("o_stats"), sem("o_rstd"), sem("z_ready")
        w2, zt2, aff, wy2 = sem("w_ready"), sem("z_transposed"), sem("z_scaled"), sem("wy_ready")
        y2, x2, rs2, xn2 = sem("y_ready"), sem("x1_stats"), sem("x1_rstd"), sem("xn_ready")
        xnst = [sem(f"xn_stored{i}") for i in range(2)]
        t2, xnT2 = sem("xn_transposed"), sem("xnT_copied")
        lg2, su2, lt2, rl2, sq2 = sem("logits"), sem("shared_up"), sem("tanh_logits"), sem("shared_relu"), sem("shared_sq")
        sd2, sa2 = sem("shared_down"), sem("shared_added")
        ra, pos2, rb, ix2, ia2 = sem("route_a"), sem("positions"), sem("route_b"), sem("slots_ready"), sem("slots_added")
        xg = [sem(f"tokens_gathered{i}") for i in range(4)]
        t3 = [sem(f"xe_transposed{e}") for e in range(2)]
        xeT3, u3, hr3 = sem("xeT_copied"), sem("h_ready"), sem("h_relu")
        ht3, h23, yd3, yc3 = sem("h_transposed"), sem("h_squared"), sem("ye_ready"), sem("ye_copied")
        yst = [sem(f"ye_stored{i}") for i in range(2)]
        gin = [[sem(f"rows_gathered{i}_{r}") for r in range(2)] for i in range(2)]
        c4, rs4, xn4 = sem("combined"), sem("x2_rstd"), sem("x2_normed")
        t4, xT4, sc4, mx4, ex4 = sem("x2_transposed"), sem("x2T_copied"), sem("scores4"), sem("scores_max"), sem("exp_done")
        pt4, pc4, ro4, x34 = sem("p_transposed"), sem("pT_copied"), sem("read_out"), sem("x3_stats")
        rs5, qa5, q5, t5, qT5 = sem("x3_rstd"), sem("x3_absmax"), sem("x3_quant"), sem("xq_transposed"), sem("xqT_copied")
        ga, gu, sl, hd, ssd = sem("gate_ready"), sem("up_ready"), sem("silu_done"), sem("h_done"), sem("h_sumsq")
        hwd, hqd = sem("hw_done"), sem("h_quant")
        ht, hc, dwn, fo = sem("hq_transposed"), sem("hqT_copied"), sem("down_ready"), sem("x4_ready")
        wq_a, wq_s, wq_r, wq_g = sem("w_abs"), sem("w_total"), sem("w_scale"), sem("w_quant")
        mask_in, mk = sem("mask_in"), sem("mask_ready")
        ost = [sem(f"out_stored{i}") for i in range(2)]

        wait_values = {e.engine: [e.alloc_register(f"wait_value{n}") for n in range(4)]
                       for e in (nc.scalar, nc.vector, nc.gpsimd)}

        def hold(eng, *waits):
            waits = [(s, v) for s, v in waits if not isinstance(v, int) or v > 0]
            if eng.engine in wait_values and any(not isinstance(v, int) for _, v in waits):
                regs = iter(wait_values[eng.engine])
                values = []
                for _, v in waits:
                    if not isinstance(v, int):
                        reg = next(regs)
                        eng.reg_mov(reg, v)
                        v = reg
                    values.append(v)
                eng.wait_ge(half_ok, 1)
                waits = [(s, v) for (s, _), v in zip(waits, values)]
            for s, v in waits:
                eng.wait_ge(s, v)

        def tiles(i, n=2):
            return bass.ds(i.at(2), n)

        def tok(i):
            return bass.ds(i.at(2 * P), 2 * P)

        def xt(i, t):
            return x_all[:, bass.ds(i.at(2, t), 1), :].rearrange("p a d -> p (a d)")

        def bank(b, *shape):
            v = psum[:, b, :]
            if len(shape) == 2:
                return v.rearrange("p (a b) -> p a b", a=shape[0])
            return v

        block = ctx.enter_context(nc.Block())

        @block.sync
        def _(sp):
            for name, t in (("whT", whT), ("wh", wh)):
                sp.dma_start(t[:, :, :], a[name]).then_inc(c_in, 16)
            sp.dma_start(ident[:, :], a["c_ident"]).then_inc(c_in, 16)
            sp.dma_start(dn[:, :, :], a["c_dn"]).then_inc(c_in, 16)
            xv = a["x"].rearrange("(n p) d -> p n d", p=P)
            cv = a["ctx"].rearrange("(n p) d -> p n d", p=P)
            ctv = a["ctxT"].rearrange("(k p) t -> p k t", p=P)

            for i in range(2):
                sp.dma_start(x_all[:, tiles(Item(i)), :], xv[:, tiles(Item(i)), :]).then_inc(c_x[i], 16)
            with sp.Fori(0, (NP - 2) // 2) as j:
                for k in range(2):
                    i = Item(2 + k, j)
                    hold(sp, (c_x[k], i.at(8, -8 * k)))
                    sp.dma_start(x_all[:, tiles(i), :], xv[:, tiles(i), :]).then_inc(c_x[k], 16)
            sp.wait_ge(v1, NP // 2)
            for name, t in (("wg", wg), ("wo", wo), ("gateT", gateT), ("shup", shup), ("shdn", shdn), ("gnp", gnp)):
                sp.dma_start(t[:, :, :], a[name]).then_inc(c_w2, 16)
            for name, t in (("c_tri", tri), ("c_iota_c", iota_c), ("c_iota_e", iota_e), ("c_tokid", tokid)):
                sp.dma_start(t[:, :], a[name]).then_inc(c_w2, 16)
            sp.dma_start(biasc[:, :], a["bias"].to_broadcast([P, E])).then_inc(c_w2, 16)
            sp.wait_ge(v1, NP)
            sp.dma_start(upT[:, :, :, :], a["upT"]).then_inc(c_w3, 16)
            sp.dma_start(dnT[:, :, :], a["dnT"]).then_inc(c_w3, 16)
            sp.dma_start(ctx_all[:, :, :], cv).then_inc(c_ctx, 16)
            sp.dma_start(ctxT_all[:, :, :], ctv).then_inc(c_ctx, 16)

            xnv = xn_dram.rearrange("(n p) d -> p n d", p=P)

            def store_xn(i, s):
                hold(sp, (xn2, i.at(2, 2)))
                sp.dma_start(xnv[:, tiles(i), :], xn[:, s, :, :]).then_inc(xnst[s], 16)

            run_steps(sp, NP - 1, [(0, store_xn)])
            sp.wait_ge(o2, NP)
            sp.wait_ge(w2, NP)
            for n, name in enumerate(("w_gate", "w_up", "w_down")):
                sp.dma_start(wraw[:, n, :], a[name]).then_inc(c_w4, 16)
            store_xn(Item(NP - 1), (NP - 1) % 2)

            yev = ye_dram.rearrange("(e c) d -> c e d", c=CAP)

            def store_ye(i, s):
                hold(sp, (yc3, i.at(1, 1)))
                sp.dma_start(yev[:, tiles(i), :], yr[:, s, :, :]).then_inc(yst[s], 16)

            run_steps(sp, NG, [(0, store_ye)])

            sp.wait_ge(yc3, NG)
            sp.dma_start(lnw, a["lnw"].to_broadcast([P, I])).then_inc(c_lnw, 16)
            ov = out.rearrange("(n p) d -> p n d", p=P)

            def store_out(i, s):
                hold(sp, (fo, i.at(2, 2)))
                sp.dma_start(ov[:, tiles(i), :], x_all[:, tiles(i), :]).then_inc(ost[s], 16)

            run_steps(sp, NP, [(0, store_out)])
            for s in range(2):
                sp.wait_ge(ost[s], 16 * NP // 2)

        @block.gpsimd
        def _(pl):
            pl.memset(mhalf[:, :], -0.5).then_inc(half_ok, 1)
            pl.dma_start(gates[:, :], a["gates"].to_broadcast([P, 4])).then_inc(gates_in, 16)
            pl.dma_start(msk[:, :, :], a["mask"]).then_inc(mask_in, 16)
            pl.memset(ones[:, :], 1.0)
            pl.memset(onesf[:, :], 1.0)
            pl.memset(mround[:, :], -ROUND)
            pl.memset(mone[:, :], -1.0)
            pl.memset(mcum[:, :], 0.0)
            pl.memset(idxf[:, :], 0.0)
            pl.memset(bda[:, :, :], 0.0)
            pl.memset(sel[:, :], 1.0).then_inc(half_ok, 1)
            pl.wait_ge(half_ok, 2)
            pl.affine_select(out=sel[:, :], in_=sel[:, :], compare_op=ALU.is_ge, fill=0.0, base=0,
                             pattern=[[1, P]], channel_multiplier=-S).then_inc(half_ok, 1)
            pl.wait_ge(half_ok, 3)
            pl.affine_select(out=sel[:, :], in_=sel[:, :], compare_op=ALU.is_ge, fill=0.0, base=S - 1,
                             pattern=[[-1, P]], channel_multiplier=S).then_inc(half_ok, 1)

            def rstd_shift(stats, val, mvb, veb, rsb, sh, eps, done):
                def stage(i, s):
                    hold(pl, (stats, val(i)))
                    pl.tensor_scalar(veb[:, s, :], mvb[:, s, :, 1], eps, None, ALU.add).then_inc(done, 1)
                    pl.tensor_scalar(sh[:, s, :], mvb[:, s, :, 0], -1.0, None, ALU.mult).then_inc(done, 1)
                    hold(pl, (done, i.at(4, 1)))
                    pl.tensor_tensor(rsb[:, s, :], veb[:, s, :], mhalf[:, 0:2], ALU.pow).then_inc(done, 1)
                    hold(pl, (done, i.at(4, 3)))
                    pl.tensor_tensor(sh[:, s, :], sh[:, s, :], rsb[:, s, :], ALU.mult).then_inc(done, 1)
                return stage

            def rstd(stats, val, mvb, veb, rsb, eps, done):
                def stage(i, s):
                    hold(pl, (stats, val(i)))
                    pl.tensor_scalar(veb[:, s, :], mvb[:, s, :, 1], eps, None, ALU.add).then_inc(done, 1)
                    hold(pl, (done, i.at(2, 1)))
                    pl.tensor_tensor(rsb[:, s, :], veb[:, s, :], mhalf[:, 0:2], ALU.pow).then_inc(done, 1)
                return stage

            run_steps(pl, NP, [(0, rstd(st1, lambda i: i.at(4, 4), mv, ve, rs, LN_EPS, rs1))])

            def route_weights(i, s):
                hold(pl, (ra, i.at(RA, RA)), *free(rb, i, RB))
                pl.tensor_scalar(wden[:, :, :], wden[:, :, :], 1e-20, None, ALU.add).then_inc(wns, 1)
                hold(pl, (wns, i.at(4, 1)))
                pl.tensor_tensor(wrec[:, :, 0], wden[:, :, 0], mone[:, :], ALU.pow).then_inc(wns, 1)
                hold(pl, (wns, i.at(4, 2)))
                pl.tensor_tensor(wn[:, :, :], w4[:, :, :], wrec[:, :, :].to_broadcast([P, 2, TOPK]), ALU.mult)\
                  .then_inc(wns, 1)
                hold(pl, (wns, i.at(4, 3)))
                pl.tensor_scalar(wn[:, :, :], wn[:, :, :], tg[:, 2:3], ROUTE_SCALE, ALU.mult, ALU.mult).then_inc(wns, 1)

            pl.wait_ge(tg_ok, 1)

            def square_shared(i, s):
                hold(pl, (rl2, i.at(1, 1)))
                pl.tensor_tensor(rh[:, s, :], rh[:, s, :], rh[:, s, :], ALU.mult).then_inc(sq2, 1)

            run_steps(pl, NP, [
                (3, route_weights), (0, rstd_shift(sto, lambda i: i.at(4, 4), mv, ve, rs, sh, GN_EPS, rso)),
                (2, square_shared), (1, rstd_shift(x2, lambda i: i.at(5, 5), mvx, vex, rsx, shx, LN_EPS, rs2))])

            pl.wait_ge(su2, NP)
            pl.wait_ge(mask_in, 16)
            for b in range(2):
                ins = pl.tensor_scalar(mnegb[:, :, b, :], msk8[:, :, :], -1.0, -NEG, ALU.add, ALU.mult)
            ins.then_inc(mk, 1)
            pl.wait_ge(mk, 1)
            pl.affine_select(out=mnegb, in_=mnegb, compare_op=ALU.is_equal, fill=NEG, base=0,
                             pattern=[[0, NT], [-1, 2], [0, S]], channel_multiplier=1).then_inc(mk, 1)

            for s in range(2):
                pl.wait_ge(xnst[s], 16 * NP // 2)

            def gather_tokens(e):
                def stage(i, s):
                    hold(pl, (tixs[e], i.at(1, 1)), *slot_free(t3[e], i))
                    pl.indirect_dma_start(out=xe[:, s, e, :], out_offset=None, in_=xn_dram[:, :],
                                          in_offset=bass.IndirectOffsetOnAxis(ap=tix[:, s, e:e + 1], axis=0),
                                          bounds_check=T - 1, oob_is_err=False).then_inc(xg[2 * s + e], 16)
                return stage

            run_steps(pl, NG, [(1, gather_tokens(1)), (0, gather_tokens(0))])

            pl.wait_ge(wqs, 3 * NG)
            for s in range(2):
                pl.wait_ge(yst[s], 16 * NG // 2)

            def rows(part):
                def stage(i, s):
                    if part == 0:
                        hold(pl, *slot_free(c4, i, 12))
                        pl.tensor_copy(rix[:, s, :], dst_all[:, tiles(i), :].rearrange("p t k -> p (t k)"))\
                          .then_inc(rixs, 1)
                        hold(pl, (rixs, i.at(1, 1)))
                    for r in range(2 * part, 2 * part + 2):
                        pl.indirect_dma_start(
                            out=gath[:, s, r, :], out_offset=None, in_=ye_dram[:, :],
                            in_offset=bass.IndirectOffsetOnAxis(ap=rix[:, s, r:r + 1], axis=0),
                            bounds_check=E * CAP - 1, oob_is_err=False).then_inc(gin[s][r // TOPK], 16)
                return stage

            def read_weight(i, s):
                hold(pl, (ex4, i.at(1, 1)))
                pl.tensor_scalar(prt[:, s, :], smx[:, s, :], NEG / 2, tg[:, 1:2], ALU.is_gt, ALU.mult).then_inc(rws, 1)
                pl.tensor_tensor(prec[:, s, :], psumr[:, s, :], mone[:, :], ALU.pow).then_inc(rws, 1)
                hold(pl, (rws, i.at(3, 2)))
                pl.tensor_tensor(prt[:, s, :], prt[:, s, :], prec[:, s, :], ALU.mult).then_inc(rws, 1)

            def x_scale(i, s):
                hold(pl, (qa5, i.at(3, 3)), *slot_free(hd, i, 2))
                pl.tensor_scalar(qc[:, s, :], amx[:, s, :], Q_EPS, 1.0 / 127.0, ALU.max, ALU.mult).then_inc(xsc, 1)
                hold(pl, (xsc, i.at(4, 1)))
                pl.tensor_tensor(qs[:, s, :], qc[:, s, :], mone[:, :], ALU.pow).then_inc(xsc, 1)
                pl.tensor_scalar(cgs[:, s, :], qc[:, s, :], wmean[:, 0:1], None, ALU.mult).then_inc(xsc, 1)
                pl.tensor_scalar(cus[:, s, :], qc[:, s, :], wmean[:, 1:2], None, ALU.mult).then_inc(xsc, 1)

            def h_scale(t):
                def stage(i, s):
                    def step(n):
                        hold(pl, (hss[t], i.at(6, n)))

                    hold(pl, (ssd, i.at(2, t + 1)), (hwd, i.at(4, 2 * t + 2)), *free(fo, i, 2, t - 1))
                    pl.tensor_scalar(msq[:, t, :], sst[:, t, :], 1.0 / I, RMS_EPS, ALU.mult, ALU.add)\
                      .then_inc(hss[t], 1)
                    step(1)
                    pl.tensor_tensor(rq[:, t, :], msq[:, t, :], mhalf[:, 0:1], ALU.pow).then_inc(hss[t], 1)
                    step(2)
                    pl.tensor_scalar(hs1[:, t, 0:1], ham[:, t, :], rq[:, t, :], Q_EPS, ALU.mult, ALU.max)\
                      .then_inc(hss[t], 1)
                    step(3)
                    pl.tensor_tensor(hs1[:, t, 1:2], hs1[:, t, 0:1], mone[:, 0:1], ALU.pow).then_inc(hss[t], 1)
                    step(4)
                    pl.tensor_scalar(hs1[:, t, 2:3], hs1[:, t, 1:2], rq[:, t, :], 127.0, ALU.mult, ALU.mult).then_inc(hss[t], 1)
                    pl.tensor_tensor(hs1[:, t, 3:4], hs1[:, t, 0:1], wdown[:, :], ALU.mult).then_inc(hss[t], 1)
                return stage

            pl.wait_ge(wq_r, 3)
            pl.wait_ge(tg_ok, 1)
            run_steps(pl, NP, [
                (0, rows(0)), (1, rstd_shift(c4, lambda i: i.at(12, 12), mv, ve, rs, sh, LN_EPS, rs4)),
                (0, rows(1)), (0, rows(3)), (0, rows(2)), (1, read_weight), (3, h_scale(1)), (2, h_scale(0)),
                (1, rstd(x34, lambda i: i.at(6, 6), mvx, vex, rsx, LN_EPS, rs5)), (1, x_scale)])

        @block.scalar
        def _(act):
            def copy_to(dst_ap, src, done, func=ACT.Copy, **kw):
                return act.activation(dst_ap, src, func, **kw).then_inc(done, 1)

            ring = a["ctxT"].rearrange("(k p) t -> p k t", p=P)

            def load_ring(i, s):
                hold(act, *slot_free(s1, i))
                act.dma_start(cring[:, s, :, :], ring[:, :, tok(i)]).then_inc(c_cr[s], 16)

            load_ring(Item(0), 0)
            act.wait_ge(gates_in, 16)
            act.activation(tg[:, :], gates[:, :], ACT.Tanh).then_inc(tg_ok, 1)
            act.wait_ge(gram_ps, 1)
            act.activation(gram[:, :, :], bank(0)[:, 0:H * HD].rearrange("p (h e) -> p h e", h=H), ACT.Copy)\
               .then_inc(gram_sb, 1)

            def p1_v(i, s):
                hold(act, (v1, i.at(1, 1)))
                copy_to(v_all[:, tiles(i), :], bank(1, 2, D), vc1)

            def p1_t(i, s):
                hold(act, (t1, i.at(1, 1)))
                copy_to(xhT_all[:, :, tok(i)], bank(2, K, 2 * P), xhT1)

            def load_ring_next(i, s):
                if not i.below(2):
                    load_ring(i, s)

            load_ring(Item(1), 1)
            run_steps(act, NP, [(2, p1_v), (0, load_ring_next), (0, p1_t)])

            def normalise(rsem, src, s, rsb, sh, done, dest, i, *waits):
                hold(act, (rsem, i.at(4, 4)), *waits)
                for t in range(2):
                    act.activation(dest[:, s, t, :], src(t), ACT.Identity, scale=rsb[:, s, t:t + 1],
                                   bias=sh[:, s, t:t + 1]).then_inc(done, 1)

            def z(i, s):
                normalise(rso, lambda t: bank(0, 2, D)[:, t, :], s, rs, sh, z2, zr, i, *slot_free(zt2, i))

            def xn_(i, s):
                normalise(rs2, lambda t: xt(i, t), s, rsx, shx, xn2, xn, i, *slot_free(t2, i),
                          *landed_before(xnst[s], i, s))

            def affine(i, s):
                hold(act, (zt2, i.at(1, 1)), *slot_free(wy2, i))
                for k in range(K):
                    ins = act.activation(tr[:, s, k, :], bank(2, K, 2 * P)[:, k, :], ACT.Identity,
                                         scale=gnp[:, 0, k:k + 1], bias=gnp[:, 1, k:k + 1])
                ins.then_inc(aff, 1)

            def copy_xnT(i, s):
                hold(act, (t2, i.at(1, 1)), *slot_free(su2, i))
                copy_to(xnT[:, s, :, :], bank(2, K, 2 * P), xnT2)

            def tanh_logits(i, s):
                hold(act, (lg2, i.at(1, 1)), *free(ra, i, RA))
                copy_to(lgt[:, :], bank(5)[:, 0:2 * E], lt2, ACT.Tanh, scale=0.5)

            def relu_shared(i, s):
                hold(act, (su2, i.at(1, 1)), *slot_free(sd2, i))
                copy_to(rh[:, s, :].rearrange("p (b n) -> p b n", b=2), psum[:, 6:8, :], rl2, ACT.Relu)

            act.wait_ge(c_w2, 16 * 11)
            run_steps(act, NP, [(0, z), (2, relu_shared), (0, affine), (1, xn_), (1, copy_xnT), (1, tanh_logits)])

            def token_index(e):
                def stage(i, s):
                    hold(act, *slot_free(t3[e], i))
                    act.activation(tix[:, s, e:e + 1], idxf[:, bass.ds(i.at(2, e), 1)], ACT.Copy).then_inc(tixs[e], 1)
                return stage

            def copy_xeT(i, s):
                hold(act, (t3[0], i.at(1, 1)), (t3[1], i.at(1, 1)), *slot_free(u3, i))
                copy_to(xeT[:, s, :, :], bank(2, K, 2 * P), xeT3)

            def square_h(i, s):
                hold(act, (ht3, i.at(1, 1)), *slot_free(yd3, i))
                copy_to(h2T[:, s, 0, :], bank(4)[:, 0:2 * P], h23, ACT.Square)

            act.wait_ge(c_w4, 48)
            for n in range(3):
                act.activation(q_w[:, n, :], wraw[:, n, :], ACT.Abs, accum_out=wabs[:, n:n + 1]).then_inc(wq_a, 1)

            act.wait_ge(ia2, NP)
            run_steps(act, NG, [(0, token_index(0)), (4, square_h), (2, copy_xeT), (0, token_index(1))])

            def x2n(i, s):
                normalise(rs4, lambda t: xt(i, t), s, rs, sh, xn4, xn, i, *slot_free(t4, i))

            def copy_x2T(i, s):
                hold(act, (t4, i.at(1, 1)), *slot_free(sc4, i))
                copy_to(xnT[:, s, :, :], bank(4, K, 2 * P), xT4)

            def exps(i, s):
                hold(act, (mx4, i.at(2, 2)), *slot_free(pt4, i))
                for t in range(2):
                    ins = act.activation(pexp[:, s, t, :], bank(5)[:, t * P:(t + 1) * P], ACT.Exp, scale=SM_SCALE,
                                         bias=nmx[:, s, t:t + 1], accum_out=psumr[:, s, t:t + 1])
                ins.then_inc(ex4, 1)

            def copy_pT(i, s):
                hold(act, (pt4, i.at(1, 1)), *slot_free(ro4, i))
                copy_to(pT[:, s, :], bank(4)[:, 0:2 * P], pc4)

            def copy_xqT(i, s):
                hold(act, (t5, i.at(1, 1)), *slot_free(gu, i, 2))
                copy_to(xqT[:, s, :, :], bank(4, K, 2 * P), qT5, ACT.Identity, bias=mround[:, :])

            def silu(t):
                def stage(i, s):
                    hold(act, (ga, i.at(2, t + 1)), *free(hd, i, 2, t - 1))
                    act.activation(sg[:, t, :].rearrange("p (b n) -> p b n", b=2), psum[:, 0:2, :], ACT.Silu,
                                   scale=cgs[:, s, t:t + 1]).then_inc(sl, 1)
                return stage

            def sumsq(t):
                def stage(i, s):
                    hold(act, (hd, i.at(2, t + 1)), *([] if i.below(1) and t == 0 else [(ssd, i.at(2, t))]),
                         *free(hss[t], i, 6, -5))
                    act.activation(sqj, hh[:, t, :], ACT.Square, accum_out=sst[:, t, :]).then_inc(ssd, 1)
                return stage

            def copy_hqT(t, b):
                def stage(i, s):
                    hold(act, (ht, i.at(4, 2 * t + b + 1)), *free(dwn, i, 2, t - 1))
                    copy_to(hqT[:, t, b * 512:(b + 1) * 512], bank(7), hc, ACT.Identity, bias=mround[:, :])
                return stage

            def load_table(func, n):
                def stage(i, s):
                    if not (i.below(1) and n == 0):
                        hold(act, (tbl, i.at(2, n)))
                    act.activation(table[:, :], mround[:, :], func).then_inc(tbl, 1)
                return stage

            run_steps(act, NP, [
                (3, copy_hqT(1, 0)), (3, copy_hqT(1, 1)), (1, copy_xqT), (0, x2n), (2, copy_hqT(0, 0)),
                (0, copy_x2T), (1, silu(0)), (1, load_table(ACT.Exp, 0)), (0, exps), (2, sumsq(1)),
                (2, copy_hqT(0, 1)), (0, copy_pT), (1, sumsq(0)), (1, load_table(ACT.Silu, 1)), (1, silu(1))])

        @block.tensor
        def _(pe):
            def mm_(o, l, r, first=True, last=True):
                return pe.matmul(o, l, r, start=first, stop=last, skip_group_check=True)

            pe.wait_ge(half_ok, 4)
            pe.wait_ge(c_in, 16 * 4)
            for h in range(H):
                ins = mm_(bank(0)[:, h * HD:(h + 1) * HD], whT[:, h, :], whT[:, h, :])
            ins.then_inc(gram_ps, 1)
            for h in range(H):
                mm_(bank(3)[0:S, h * S:(h + 1) * S], bda[:, h, 0:S], bda[:, h, 0:S], h == 0, False)

            def p1_v(i, s):
                n16 = landed(i, s)
                hold(pe, (c_cr[s], n16), *free(vc1, i))
                for t in range(2):
                    for h in range(H):
                        ins = mm_(bank(1, 2, D)[:, t, h * HD:(h + 1) * HD],
                                  cring[:, s, h, t * P:(t + 1) * P], wh[:, h, :])
                ins.then_inc(v1, 1)

            def p1_t(i, s):
                hold(pe, (xh1, i.at(2, 2)), *free(xhT1, i))
                for t in range(2):
                    for k in range(K):
                        ins = pe.transpose(bank(2, K, 2 * P)[:, k, t * P:(t + 1) * P],
                                           xn[:, s, t, k * P:(k + 1) * P], ident[:, :])
                ins.then_inc(t1, 1)

            def p1_p(i, s):
                hold(pe, (xhT1, i.at(1, 1)), *free(ptc1, i))
                for h in range(H):
                    ins = mm_(bank(0, H, 2 * P)[:, h, :], gram[:, h, :], xhT_all[:, h, tok(i)])
                ins.then_inc(pt1, 1)

            def p1_s(i, s):
                hold(pe, (ptc1, i.at(1, 1)))
                for b in range(4):
                    for h in range(H):
                        ins = mm_(bank(3)[0:S, h * S:(h + 1) * S], ptr[:, s, h, b * S:(b + 1) * S],
                                  cring[:, s, h, b * S:(b + 1) * S], False, False)
                ins.then_inc(s1, 1)

            pe.wait_ge(gram_sb, 1)
            run_steps(pe, NP, [(0, p1_t), (1, p1_v), (1, p1_s), (0, p1_p)])
            pe.wait_ge(am, 4)
            for h in range(H):
                ins = pe.transpose(bank(4)[:, h * S:(h + 1) * S], amat[:, h, :], ident[0:S, 0:S])
            ins.then_inc(at, 1)

            def p2_o(i, s):
                hold(pe, *free(z2, i, 2))
                for h in range(H):
                    ins = mm_(bank(0, 2, D)[:, :, h * HD:(h + 1) * HD], bda[:, h, :],
                              v_all[:, tiles(i), h * HD:(h + 1) * HD])
                ins.then_inc(o2, 1)

            def p2_w(i, s):
                hold(pe, *free(wy2, i))
                for j in range(K):
                    for k in range(K):
                        ins = mm_(bank(3, K, 2 * P)[:, j, :], wg[:, k, j * P:(j + 1) * P], xhT_all[:, k, tok(i)],
                                  k == 0, k == K - 1)
                ins.then_inc(w2, 1)

            def p2_zt(i, s):
                hold(pe, (z2, i.at(2, 2)), *slot_free(xnT2, i))
                for t in range(2):
                    for k in range(K):
                        ins = pe.transpose(bank(2, K, 2 * P)[:, k, t * P:(t + 1) * P],
                                           zr[:, s, t, k * P:(k + 1) * P], ident[:, :])
                ins.then_inc(zt2, 1)

            def p2_y(i, s):
                hold(pe, (wy2, i.at(1, 1)), *slot_free(sa2, i))
                for t in range(2):
                    for k in range(K):
                        ins = mm_(bank(4, 2, D)[:, t, :], wyT[:, s, k, t * P:(t + 1) * P], wo[:, k, :],
                                  k == 0, k == K - 1)
                ins.then_inc(y2, 1)

            def p2_xt(i, s):
                last = i.j is None and i.c == NP - 1
                hold(pe, (xn2, i.at(2, 2)), (aff, i.at(1, 1 if last else 2)))
                for t in range(2):
                    for k in range(K):
                        ins = pe.transpose(bank(2, K, 2 * P)[:, k, t * P:(t + 1) * P],
                                           xn[:, s, t, k * P:(k + 1) * P], ident[:, :])
                ins.then_inc(t2, 1)

            def p2_lg(i, s):
                hold(pe, (xnT2, i.at(1, 1)), *free(lt2, i))
                for t in range(2):
                    for k in range(K):
                        ins = mm_(bank(5)[:, t * E:(t + 1) * E], xnT[:, s, k, t * P:(t + 1) * P], gateT[:, k, :],
                                  k == 0, k == K - 1)
                ins.then_inc(lg2, 1)

            def p2_su(i, s):
                hold(pe, *free(rl2, i))
                for n in range(NHS):
                    for k in range(K):
                        ins = mm_(psum[:, 6 + n // 2, (n % 2) * 256:(n % 2) * 256 + 256],
                                  shup[:, k, n * P:(n + 1) * P], xnT[:, s, k, :], k == 0, k == K - 1)
                ins.then_inc(su2, 1)

            def p2_sd(i, s):
                last = i.j is None and i.c == NP - 1
                hold(pe, (sq2, i.at(1, 1)), (x2, i.at(5, 1 if last else 6)))
                for t in range(2):
                    for n in range(NHS):
                        ins = mm_(bank(4, 2, D)[:, t, :],
                                  rh[:, s, n * 256 + t * P:n * 256 + (t + 1) * P],
                                  shdn[:, n, :], n == 0, n == NHS - 1)
                ins.then_inc(sd2, 1)

            def p2_pos(i, s):
                hold(pe, (ra, i.at(RA, RA_MASK)), *free(rb, i, RB), *free(ia2, i))
                pos = bank(1)[:, 0:2 * E]
                mm_(pos[:, 0:E], tri[:, :], mm[:, 0, :], True, False)
                mm_(pos[:, 0:E], ones[:, :], mcum[:, :], False, True)
                mm_(pos[:, E:2 * E], tri[:, :], mm[:, 1, :], True, False)
                mm_(pos[:, E:2 * E], ones[:, :], mm[:, 0, :], False, False)
                mm_(pos[:, E:2 * E], ones[:, :], mcum[:, :], False, True).then_inc(pos2, 1)

            def p2_ix(i, s):
                hold(pe, (rb, i.at(RB, RB)), *free(ia2, i))
                for r in range(8):
                    ins = mm_(bank(1)[:, 2 * E:3 * E], ck[:, r, :], te[:, r // TOPK, (r % TOPK) * E:(r % TOPK + 1) * E],
                              r == 0, r == 7)
                ins.then_inc(ix2, 1)

            pe.wait_ge(c_w2, 16 * 11)
            pe.wait_ge(bd, 2 * H)
            pe.wait_ge(vc1, NP)
            run_steps(pe, NP, [
                (1, p2_w), (3, p2_sd), (2, p2_xt), (0, p2_o), (2, p2_lg), (3, p2_pos), (2, p2_su), (1, p2_y),
                (3, p2_ix), (0, p2_zt)])

            def p3_t(e):
                def stage(i, s):
                    hold(pe, (xg[2 * s + e], landed(i, s)), *free(xeT3, i))
                    for k in range(K):
                        ins = pe.transpose(bank(2, K, 2 * P)[:, k, e * P:(e + 1) * P],
                                           xe[:, s, e, k * P:(k + 1) * P], ident[:, :])
                    ins.then_inc(t3[e], 1)
                return stage

            def p3_u(i, s):
                hold(pe, (xeT3, i.at(1, 1)), *free(hr3, i))
                for e in range(2):
                    for k in range(K):
                        w = upT[:, bass.ds(i.at(2, e), 1), k, :]
                        ins = mm_(bank(3)[:, e * P:(e + 1) * P], xeT[:, s, k, e * P:(e + 1) * P],
                                  w.rearrange("p a h -> p (a h)"), k == 0, k == K - 1)
                ins.then_inc(u3, 1)

            def p3_ht(i, s):
                hold(pe, (hr3, i.at(1, 1)), *free(h23, i))
                for e in range(2):
                    ins = pe.transpose(bank(4)[:, e * P:(e + 1) * P], hr[:, s, 0, e * P:(e + 1) * P], ident[:, :])
                ins.then_inc(ht3, 1)

            def p3_d(i, s):
                hold(pe, (h23, i.at(1, 1)), *slot_free(yc3, i))
                for e in range(2):
                    w = dnT[:, bass.ds(i.at(2, e), 1), :]
                    ins = mm_(bank(s, 2, D)[:, e, :], h2T[:, s, 0, e * P:(e + 1) * P],
                              w.rearrange("p a d -> p (a d)"))
                ins.then_inc(yd3, 1)

            pe.wait_ge(wq_a, 3)
            mm_(bank(6)[:, 0:3], onesf[:, :], wabs[:, 0:3]).then_inc(wq_s, 1)
            pe.wait_ge(c_w3, 32)
            run_steps(pe, NG, [(0, p3_t(0)), (2, p3_ht), (0, p3_t(1)), (1, p3_u), (2, p3_d)])

            def x2t(i, s):
                hold(pe, (xn4, i.at(2, 2)), *free(qT5, i))
                for t in range(2):
                    for k in range(K):
                        ins = pe.transpose(bank(4, K, 2 * P)[:, k, t * P:(t + 1) * P],
                                           xn[:, s, t, k * P:(k + 1) * P], ident[:, :])
                ins.then_inc(t4, 1)

            def score(i, s):
                hold(pe, (xT4, i.at(1, 1)), *free(ex4, i))
                for t in range(2):
                    o = bank(5)[:, t * P:(t + 1) * P]
                    mm_(o, sel[:, :], mnegb[:, bass.ds(i.at(2, t), 1), :, :].rearrange("p n a m -> p (n a m)"),
                        True, False)
                    for k in range(K):
                        ins = mm_(o, xnT[:, s, k, t * P:(t + 1) * P],
                                  ctxT_all[:, k, bass.ds(i.at(2 * P, t * P), P)], False, k == K - 1)
                ins.then_inc(sc4, 1)

            def pt(i, s):
                hold(pe, (ex4, i.at(1, 1)), (xT4, i.at(1, 1)))
                for t in range(2):
                    ins = pe.transpose(bank(4)[:, t * P:(t + 1) * P], pexp[:, s, t, :], ident[:, :])
                ins.then_inc(pt4, 1)

            def read(i, s):
                hold(pe, (pc4, i.at(1, 1)), *free(x34, i, 6, -4))
                for t in range(2):
                    ins = mm_(bank(6, 2, D)[:, t, :], pT[:, s, t * P:(t + 1) * P],
                              ctx_all[:, bass.ds(i.at(2, t), 1), :].rearrange("p a d -> p (a d)"))
                ins.then_inc(ro4, 1)

            def xqt(i, s):
                hold(pe, (q5, i.at(2, 2)), (pc4, i.at(1, 1)))
                for t in range(2):
                    for k in range(K):
                        ins = pe.transpose(bank(4, K, 2 * P)[:, k, t * P:(t + 1) * P],
                                           xq[:, s, t, k * P:(k + 1) * P], ident[:, :])
                ins.then_inc(t5, 1)

            def project(w, t):
                def stage(i, s):
                    if w == 0:
                        hold(pe, (qT5, i.at(1, 1)), *([] if i.below(1) and t == 0 else [(sl, i.at(2, t))]),
                             *(free(fo, i, 2, -1) if t else slot_free(fo, i, 2)))
                    else:
                        hold(pe, (qT5, i.at(1, 1)), *([] if i.below(1) and t == 0 else [(hd, i.at(2, t))]))
                    for b in range(2):
                        for k in range(K):
                            ins = mm_(psum[:, 2 * w + b, :], xqT[:, s, k, t * P:(t + 1) * P],
                                      q_w[:, w, k * I + b * 512:k * I + (b + 1) * 512], k == 0, k == K - 1)
                    ins.then_inc(gu if w else ga, 1)
                return stage

            def hqt(t, b):
                def stage(i, s):
                    first = i.below(1) and t == 0 and b == 0
                    hold(pe, (hqd, i.at(2, t + 1)), *([] if first else [(hc, i.at(4, 2 * t + b))]))
                    for c in range(4):
                        ins = pe.transpose(bank(7)[:, c * P:(c + 1) * P],
                                           hq[:, t, (4 * b + c) * P:(4 * b + c + 1) * P], ident[:, :])
                    ins.then_inc(ht, 1)
                return stage

            def down(t):
                def stage(i, s):
                    last = i.j is None and i.c == NP - 1
                    hold(pe, (hc, i.at(4, 2 * t + 2)), (sl, i.at(2, 2 if last else 3 + t)),
                         *free(fo, i, 2, t - 1))
                    for c in range(NI):
                        ins = mm_(bank(t)[:, 0:D], hqT[:, t, c * P:(c + 1) * P],
                                  q_w[:, 2, c * D:(c + 1) * D], c == 0, c == NI - 1)
                    ins.then_inc(dwn, 1)
                return stage

            pe.wait_ge(c_ctx, 32)
            pe.wait_ge(mk, 2)
            pe.wait_ge(wqs, 3 * NG)
            run_steps(pe, NP, [
                (3, hqt(1, 1)), (3, down(1)), (1, xqt), (2, hqt(0, 0)), (1, project(0, 0)), (0, x2t),
                (0, score), (1, project(1, 0)), (2, hqt(0, 1)), (1, project(1, 1)), (0, pt), (2, down(0)),
                (0, read), (1, project(0, 1)), (2, hqt(1, 0))])

        @block.vector
        def _(dve):
            class Chain:

                def __init__(self, s_, i, per, n=0):
                    self.s, self.i, self.per, self.n = s_, i, per, n

                def __call__(self, ins):
                    self.n += 1
                    return ins.then_inc(self.s, 1)

                def sync(self, but=0):
                    hold(dve, (self.s, self.i.at(self.per, self.n - but)))

                def end(self):
                    assert self.n == self.per, (self.n, self.per)

            def stats(c, src, s, bnb, mvb):
                for t in range(2):
                    c(dve.bn_stats(bnb[:, s, t, :], src(t)))
                for t in range(2):
                    c.sync(1 - t)
                    c(dve.bn_aggr(mvb[:, s, t, :], bnb[:, s, t, :]))

            dve.wait_ge(half_ok, 1)

            def p1_stats(i, s):
                n16 = landed(i, s)
                hold(dve, (c_x[s], n16))
                c = Chain(st1, i, 4)
                stats(c, lambda t: xt(i, t), s, bn, mv)
                c.end()

            def normalise(rsem, src, s, i, mvb, rsb, done, dest, *waits):
                hold(dve, (rsem, i.at(2, 2)), *waits)
                for t in range(2):
                    dve.tensor_scalar(dest[:, s, t, :], src(t), mvb[:, s, t, 0:1], rsb[:, s, t:t + 1],
                                      ALU.subtract, ALU.mult).then_inc(done, 1)

            def xtile(i):
                return lambda t: xt(i, t)

            def p1_norm(i, s):
                normalise(rs1, xtile(i), s, i, mv, rs, xh1, xn, (st1, i.at(4, 4)), *slot_free(t1, i))

            def p1_pt(i, s):
                hold(dve, (pt1, i.at(1, 1)), *slot_free(s1, i))
                dve.tensor_copy(ptr[:, s, :, :], bank(0, H, 2 * P)).then_inc(ptc1, 1)

            run_steps(dve, NP, [(0, p1_stats), (0, p1_norm), (1, p1_pt)])

            dve.wait_ge(s1, NP)
            dve.tensor_tensor(amat[:, :, 0:S], bank(3)[0:S, 0:H * S].rearrange("p (h t) -> p h t", h=H),
                              dn[:, :, :], ALU.mult).then_inc(am, 1)
            dve.wait_ge(am, 1)
            dve.scalar_tensor_tensor(amat[:, :, S:2 * S], amat[:, :, 0:S], -1.0, amat[:, :, 0:S],
                                     ALU.mult, ALU.max).then_inc(am, 1)
            dve.wait_ge(am, 2)
            dve.tensor_scalar(amat[:, :, 0:S], amat[:, :, S:2 * S], 1.0, None, ALU.max).then_inc(am, 1)
            dve.wait_ge(am, 3)
            dve.tensor_copy(amat[:, :, S:2 * S], amat[:, :, 0:S]).then_inc(am, 1)
            dve.wait_ge(at, 1)
            dve.wait_ge(half_ok, 2)
            for h in range(H):
                for b in range(2):
                    dve.tensor_copy(bda[b * S:(b + 1) * S, h, b * S:(b + 1) * S],
                                    bank(4)[b * S:(b + 1) * S, h * S:(h + 1) * S]).then_inc(bd, 1)

            def o_stats(i, s):
                hold(dve, (o2, i.at(1, 1)))
                c = Chain(sto, i, 4)
                stats(c, lambda t: bank(0, 2, D)[:, t, :], s, bn, mv)
                c.end()

            def wy(i, s):
                hold(dve, (aff, i.at(1, 1)), (w2, i.at(1, 1)), *slot_free(y2, i))
                dve.scalar_tensor_tensor(wyT[:, s, :, :], bank(3, K, 2 * P), 0.0, tr[:, s, :, :],
                                         ALU.max, ALU.mult).then_inc(wy2, 1)

            def x1(i, s):
                hold(dve, (y2, i.at(1, 1)))
                c = Chain(x2, i, 5)
                c(dve.scalar_tensor_tensor(x_all[:, tiles(i), :], bank(4, 2, D), tg[:, 0:1], x_all[:, tiles(i), :],
                                           ALU.mult, ALU.add))
                c.sync()
                stats(c, xtile(i), s, bnx, mvx)
                c.end()

            def shared(i, s):
                hold(dve, (sd2, i.at(1, 1)))
                dve.scalar_tensor_tensor(x_all[:, tiles(i), :], bank(4, 2, D), tg[:, 2:3], x_all[:, tiles(i), :],
                                         ALU.mult, ALU.add).then_inc(sa2, 1)

            def route_a(part):
                def stage(i, s):
                    c = Chain(ra, i, RA, RA_STARTS[part])
                    v = sc[:, :, :].rearrange("p t (g m) -> p (t g) m", g=G)
                    if part == 0:
                        hold(dve, (lt2, i.at(1, 1)))
                        c(dve.tensor_scalar(sig[:, :, :], lgt[:, :].rearrange("p (t e) -> p t e", t=2), 0.5, 0.5,
                                            ALU.mult, ALU.add))
                        return
                    c.sync()
                    if part == 1:
                        c(dve.tensor_tensor(sc[:, :, :], sig[:, :, :], biasc[:, None, :].to_broadcast([P, 2, E]),
                                            ALU.add))
                    elif part == 2:
                        c(dve.tensor_tensor(psm[:, :, 0:2], v[:, :, 0:4:2], v[:, :, 1:4:2], ALU.add))
                        c(dve.tensor_tensor(psm[:, :, 2:4], v[:, :, 0:2], v[:, :, 2:4], ALU.add))
                        c(dve.tensor_tensor(psm[:, :, 4:5], v[:, :, 0:1], v[:, :, 3:4], ALU.add))
                        c(dve.tensor_tensor(psm[:, :, 5:6], v[:, :, 1:2], v[:, :, 2:3], ALU.add))
                    elif part == 3:
                        c(dve.tensor_reduce(gs[:, :], psm[:, :, :], AX.X, ALU.max))
                    elif part == 4:
                        for t in range(2):
                            c(dve.max(m8[:, t, :], gs[:, t * G:(t + 1) * G]))
                    elif part == 5:
                        for t in range(2):
                            c(dve.max_index(i8[:, t, :], m8[:, t, :], gs[:, t * G:(t + 1) * G]))
                    elif part == 6:
                        c(dve.tensor_copy(gif[:, :, :], i8[:, :, 0:TOPG]))
                    elif part == 7:
                        c(dve.tensor_tensor(eqg[:, :, :, :], iota_e[:, None, 0:G, None].to_broadcast([P, 2, G, TOPG]),
                                            gif[:, :, None, :].to_broadcast([P, 2, G, TOPG]), ALU.is_equal))
                    elif part == 8:
                        c(dve.tensor_reduce(gm[:, :], eqg[:, :, :, :].rearrange("p t g k -> p (t g) k"), AX.X, ALU.add))
                    elif part == 9:
                        c(dve.tensor_tensor(msc[:, :, :].rearrange("p t (g m) -> p (t g) m", g=G), v,
                                            gm[:, :, None].to_broadcast([P, 2 * G, E // G]), ALU.mult))
                    elif part == 10:
                        for t in range(2):
                            c(dve.max(m8[:, t, :], msc[:, t, :]))
                    elif part == 11:
                        for t in range(2):
                            c(dve.max_index(i8[:, t, :], m8[:, t, :], msc[:, t, :]))
                    elif part == 12:
                        c(dve.tensor_copy(eif[:, :, :], i8[:, :, 0:TOPK]))
                    elif part == 13:
                        c(dve.tensor_tensor(oh[:, :, :, :], iota_e[:, None, None, :].to_broadcast([P, 2, TOPK, E]),
                                            eif[:, :, :, None].to_broadcast([P, 2, TOPK, E]), ALU.is_equal))
                    elif part == 14:
                        with nc.allow_low_precision(reason="sums of at most one 1"):
                            c(dve.tensor_reduce(mm[:, :, :], oh[:, :, :, :].rearrange("p t k e -> p t e k"), AX.X,
                                                ALU.add))
                        c(dve.tensor_tensor(wsel[:, :, :, :], oh[:, :, :, :],
                                            sig[:, :, None, :].to_broadcast([P, 2, TOPK, E]), ALU.mult))
                    elif part == 15:
                        c(dve.tensor_reduce(w4[:, :, :], wsel[:, :, :, :], AX.X, ALU.add))
                    elif part == 16:
                        c(dve.tensor_reduce(wden[:, :, 0], w4[:, :, :], AX.X, ALU.add))
                    assert c.n == (*RA_STARTS, RA)[part + 1]
                return stage

            def route_b(part):
                def stage(i, s):
                    c = Chain(rb, i, RB, RB_STARTS[part])
                    if part == 0:
                        hold(dve, (pos2, i.at(1, 1)), (ra, i.at(RA, RA)), *free(ix2, i))
                        pos = bank(1)[:, 0:2 * E].rearrange("p (t e) -> p t e", t=2)
                        c(dve.tensor_tensor(wsel[:, :, :, :], oh[:, :, :, :],
                                            pos[:, :, None, :].to_broadcast([P, 2, TOPK, E]), ALU.mult))
                        c(dve.tensor_tensor(mcum[:, :], mcum[:, :], mm[:, 0, :], ALU.add))
                        return
                    c.sync()
                    if part == 1:
                        c(dve.tensor_tensor(mcum[:, :], mcum[:, :], mm[:, 1, :], ALU.add))
                        c(dve.tensor_reduce(posk[:, :, :], wsel[:, :, :, :], AX.X, ALU.add))
                    elif part == 2:
                        c(dve.tensor_scalar(vald[:, :, :], posk[:, :, :], float(CAP), None, ALU.is_lt))
                        c(dve.tensor_scalar(dst[:, :, :], posk[:, :, :], float(CAP - 1), None, ALU.min))
                    elif part == 3:
                        hold(dve, (wns, i.at(4, 4)))
                        c(dve.tensor_tensor(wk_all[:, tiles(i), :], wn[:, :, :], vald[:, :, :], ALU.mult))
                        c(dve.scalar_tensor_tensor(dst_all[:, tiles(i), :], eif[:, :, :], float(CAP), dst[:, :, :],
                                                   ALU.mult, ALU.add))
                        c(dve.tensor_tensor(te[:, :, :], oh[:, :, :, :].rearrange("p t k e -> p t (k e)"),
                                            tokid[:, tiles(i), None].to_broadcast([P, 2, TOPK * E]), ALU.mult))
                        for r in range(8):
                            c(dve.tensor_scalar(ck[:, r, :], iota_c[:, :], posk[:, r // TOPK, r % TOPK:r % TOPK + 1],
                                                None, ALU.is_equal))
                    assert c.n == (*RB_STARTS, RB)[part + 1]
                return stage

            def add_slots(i, s):
                hold(dve, (ix2, i.at(1, 1)), *free(ia2, i))
                dve.tensor_tensor(idxf[:, :], bank(1)[:, 2 * E:3 * E], idxf[:, :], ALU.add).then_inc(ia2, 1)

            dve.wait_ge(c_w2, 16 * 11)
            dve.wait_ge(tg_ok, 1)
            run_steps(dve, NP, [
                (3, route_b(0)), (0, o_stats), (2, route_a(0)), (3, route_b(1)), (3, shared), (3, route_b(2)),
                (2, route_a(1)), (3, route_b(3)), (2, route_a(2)), (2, route_a(3)), (2, route_a(4)),
                (2, route_a(5)), (2, route_a(6)), (2, route_a(7)), (1, x1), (2, route_a(8)), (2, route_a(9)),
                (2, route_a(10)), (3, add_slots), (2, route_a(11)), (2, route_a(12)), (2, route_a(13)),
                (2, route_a(14)), (2, route_a(15)), (0, wy), (2, route_a(16))])

            def relu_h(i, s):
                hold(dve, (u3, i.at(1, 1)), *slot_free(ht3, i))
                dve.tensor_scalar(hr[:, s, 0, :], bank(3)[:, 0:2 * P], 0.0, None, ALU.max).then_inc(hr3, 1)

            def copy_y(i, s):
                st = landed_before(yst[s], i, s)
                hold(dve, (yd3, i.at(1, 1)), *st)
                dve.tensor_copy(yr[:, s, :, :], bank(s, 2, D)).then_inc(yc3, 1)

            dve.wait_ge(wq_s, 1)
            dve.tensor_scalar(wmean[:, :], bank(6)[:, 0:3], 1.0 / (I * D), Q_EPS, ALU.mult, ALU.max).then_inc(wq_r, 1)
            dve.wait_ge(wq_r, 1)
            dve.reciprocal(winv[:, :], wmean[:, :]).then_inc(wq_r, 1)
            dve.tensor_scalar(wdown[:, :], wmean[:, 2:3], 1.0 / 127.0, tg[:, 3:4], ALU.mult, ALU.mult).then_inc(wq_r, 1)
            dve.wait_ge(wq_r, 3)

            def ternary(i, s):
                n = K * I // NG
                cols = bass.ds(i.at(n), n)
                v = wraw[:, :, cols]
                c = Chain(wqs, i, 3)
                c(dve.tensor_tensor(v, v, winv[:, :, None].to_broadcast([P, 3, n]), ALU.mult))
                c.sync()
                c(dve.tensor_scalar(v, v, ROUND, ROUND + 1.0, ALU.add, ALU.min))
                c.sync()
                c(dve.tensor_scalar(q_w[:, :, cols], v, ROUND - 1.0, ROUND, ALU.max, ALU.subtract))
                c.end()

            run_steps(dve, NG, [(1, ternary), (3, copy_y), (1, relu_h)])

            def combine(i, s):
                c = Chain(c4, i, 12)
                if not i.below(1):
                    hold(dve, *[(gin[s][t], i.at(8 * TOPK, 16 * TOPK - 8 * TOPK * s)) for t in range(2)])
                order = [(k, t) for k in range(TOPK) for t in range(2)]
                for k, t in sorted(order, key=lambda kt: kt[1]) if i.below(1) else order:
                    if i.below(1) and k == 0:
                        dve.wait_ge(gin[s][t], 16 * TOPK)
                    if k > 0:
                        c.sync(0 if i.below(1) else 1)
                    w = wk_all[:, bass.ds(i.at(2, t), 1), k:k + 1].rearrange("p a b -> p (a b)")
                    c(dve.scalar_tensor_tensor(xt(i, t), gath[:, s, t * TOPK + k, :], w, xt(i, t),
                                               ALU.mult, ALU.add))
                c.sync()
                stats(c, xtile(i), s, bn, mv)
                c.end()

            def smax(i, s):
                hold(dve, (sc4, i.at(1, 1)), *slot_free(x34, i, 6))
                dve.tensor_reduce(smx[:, s, :], bank(5)[:, 0:2 * P].rearrange("p (t m) -> p t m", t=2), AX.X, ALU.max)\
                   .then_inc(mx4, 1)
                hold(dve, (mx4, i.at(2, 1)))
                dve.tensor_scalar(nmx[:, s, :], smx[:, s, :], -SM_SCALE, None, ALU.mult).then_inc(mx4, 1)

            def x3(i, s):
                hold(dve, (rws, i.at(3, 3)), (ro4, i.at(1, 1)))
                c = Chain(x34, i, 6)
                for t in range(2):
                    c(dve.scalar_tensor_tensor(xt(i, t), bank(6, 2, D)[:, t, :], prt[:, s, t:t + 1], xt(i, t),
                                               ALU.mult, ALU.add))
                c.sync()
                stats(c, xtile(i), s, bnx, mvx)
                c.end()

            def x3_absmax(i, s):
                hold(dve, (rs5, i.at(2, 2)), (x34, i.at(6, 6)))
                c = Chain(qa5, i, 3)
                for t in range(2):
                    c(dve.tensor_scalar(x3n[:, s, t, :], xt(i, t), mvx[:, s, t, 0:1], rsx[:, s, t:t + 1],
                                        ALU.subtract, ALU.mult))
                c.sync()
                c(dve.tensor_reduce(amx[:, s, :], x3n[:, s, :, :], AX.X, ALU.max, apply_absolute_value=True))
                c.end()

            def x3_quant(i, s):
                hold(dve, (xsc, i.at(4, 4)), *slot_free(t5, i))
                for t in range(2):
                    dve.tensor_scalar(xq[:, s, t, :], x3n[:, s, t, :], qs[:, s, t:t + 1], ROUND, ALU.mult, ALU.add)\
                       .then_inc(q5, 1)

            def h_(t):
                def stage(i, s):
                    hold(dve, (gu, i.at(2, t + 1)), (sl, i.at(2, t + 1)), *free(ssd, i, 2, t - 1))
                    dve.scalar_tensor_tensor(hh[:, t, :].rearrange("p (b n) -> p b n", b=2), psum[:, 2:4, :],
                                             cus[:, s, t:t + 1], sg[:, t, :].rearrange("p (b n) -> p b n", b=2),
                                             ALU.mult, ALU.mult).then_inc(hd, 1)
                return stage

            def hw_(t):
                def stage(i, s):
                    hold(dve, (hd, i.at(2, t + 1)))
                    dve.tensor_tensor(hw[:, t, :], hh[:, t, :], lnw[:, :], ALU.mult).then_inc(hwd, 1)
                    hold(dve, (hwd, i.at(4, 2 * t + 1)))
                    dve.tensor_reduce(ham[:, t, :], hw[:, t, :], AX.X, ALU.max, apply_absolute_value=True)\
                       .then_inc(hwd, 1)
                return stage

            def hquant(t):
                def stage(i, s):
                    hold(dve, (hss[t], i.at(6, 6)), *free(ht, i, 4, 2 * t - 2))
                    dve.tensor_scalar(hq[:, t, :], hw[:, t, :], hs1[:, t, 2:3], ROUND, ALU.mult, ALU.add)\
                       .then_inc(hqd, 1)
                return stage

            def final(t):
                def stage(i, s):
                    hold(dve, (dwn, i.at(2, t + 1)))
                    dve.scalar_tensor_tensor(xt(i, t), bank(t)[:, 0:D], hs1[:, t, 3:4], xt(i, t),
                                             ALU.mult, ALU.add).then_inc(fo, 1)
                return stage

            dve.wait_ge(c_lnw, 16)
            run_steps(dve, NP, [
                (1, x3), (2, hquant(0)), (1, x3_absmax), (3, final(1)), (0, combine), (1, x3_quant),
                (2, h_(1)), (2, hw_(1)), (0, smax), (1, h_(0)), (1, hw_(0)), (2, final(0)), (2, hquant(1))])


def decay_masks():
    gam = (1.0 - 2.0 ** (-5.0 - np.arange(H, dtype=np.float32))).astype(np.float32)
    idx = np.arange(S, dtype=np.float32)
    expo = idx[None, :] - idx[:, None]
    d = np.where(expo[None] <= 0, gam[:, None, None] ** np.minimum(expo, 0)[None], np.float32(0)).astype(np.float32)
    d = d / np.sqrt(d.sum(axis=-1))[:, None, :]
    return np.ascontiguousarray((d / np.sqrt(np.float32(HD))).astype(np.float32).transpose(1, 0, 2))


def kernel(**inputs):
    import concourse.bacc as _bacc
    import ml_dtypes
    from concourse.bass_utils import run_bass_kernel_spmd as _run

    v = {k: np.asarray(w) for k, w in inputs.items()}

    def cont(w):
        return np.ascontiguousarray(w)

    def blocks(w, rows=P):
        return cont(w.reshape(-1, rows, w.shape[-1]).transpose(1, 0, 2))

    feeds = {
        "x": cont(v["x"].reshape(T, D)),
        "ctx": cont(v["ctx_2048"].reshape(T, D)),
        "ctxT": cont(v["ctx_2048"].reshape(T, D).T),
        "mask": cont(v["mask_BxS2_bk0"].reshape(NT, 2, S).transpose(1, 0, 2)).view(np.int32),
        "gates": cont(np.concatenate([v["g_xattn"], v["g_ffn"]])[None]),
        "wh": cont(v["L0_xattn_Wh"].transpose(1, 0, 2)),
        "whT": cont(v["L0_xattn_Wh"].transpose(2, 0, 1)),
        "wg": blocks(v["L0_xattn_wg_w"]),
        "wo": blocks(v["L0_xattn_wo_w"]),
        "gnp": cont(np.stack([v["L0_xattn_gn_gamma"].reshape(K, P), v["L0_xattn_gn_beta"].reshape(K, P)])
                    .transpose(2, 0, 1)),
        "gateT": blocks(cont(v["L0_ffn_gate_w"].T)),
        "bias": cont(v["L0_ffn_bias_corr"][None]),
        "upT": cont(v["L0_ffn_up_w"].reshape(E, P, K, P).transpose(3, 0, 2, 1)),
        "dnT": cont(v["L0_ffn_down_w"].transpose(2, 0, 1)),
        "shup": blocks(cont(v["L0_ffn_shared_up_w"].T)),
        "shdn": blocks(cont(v["L0_ffn_shared_down_w"].T)),
        "w_gate": blocks(cont(v["L1_ffn_w_gate"].T)).reshape(P, K * I),
        "w_up": blocks(cont(v["L1_ffn_w_up"].T)).reshape(P, K * I),
        "w_down": blocks(cont(v["L1_ffn_w_down"].T)).reshape(P, K * I),
        "lnw": cont(v["L1_ffn_ln_weight"][None]),
        "c_ident": np.eye(P, dtype=np.float32),
        "c_dn": decay_masks(),
        "c_tri": np.triu(np.ones((P, P), np.float32), 1).astype(ml_dtypes.bfloat16),
        "c_iota_c": np.tile(np.arange(P, dtype=np.float16), (P, 1)),
        "c_iota_e": np.tile(np.arange(E, dtype=np.float32), (P, 1)),
        "c_tokid": (np.arange(NT)[None, :] * P + np.arange(P)[:, None]).astype(np.float32),
    }
    nc = _bacc.Bacc("TRN2", target_bir_lowering=False, num_devices=1)
    arrays, aps = {}, {}
    for name, w in feeds.items():
        arrays[f"in_{name}_dram"] = w
        aps[name] = nc.dram_tensor(f"in_{name}_dram", w.shape, mybir.dt.from_np(w.dtype), kind="ExternalInput").ap()
    out = nc.dram_tensor("out_0_dram", (T, D), F32, kind="ExternalOutput").ap()
    build(nc, aps, out)
    r = _run(nc, [arrays], core_ids=[0])
    return r.results[0]["out_0_dram"].reshape(B, S, D)
```
